# Optimizing a Trainium2 kernel written in Bass

```python
import numpy as np
import jax
import jax.numpy as jnp

def _softmax(x, axis=-1):
    return jax.nn.softmax(x, axis=axis)

def _gelu(x):
    return jax.nn.gelu(x, approximate=True)

def _silu(x):
    return jax.nn.silu(x)

def _sigmoid(x):
    return jax.nn.sigmoid(x)

def _layernorm(x, axis=-1, eps=1e-05):
    m = jnp.mean(x, axis=axis, keepdims=True)
    v = jnp.var(x, axis=axis, keepdims=True)
    return (x - m) / jnp.sqrt(v + eps)

def _scatter_add(tgt, idx, src, axis=0):
    return tgt.at[idx].add(src)

def _segment_sum(src, seg, n):
    return jax.ops.segment_sum(src, seg, n)
kernel_name = 'mk_perceiver_d1_seqx_r4_2daf17'

def setup_inputs(seed: int=0):
    np.random.seed(seed)
    _w = jnp.asarray

    def _rec_inputs():
        import jax
        import jax.numpy as jnp
        _rk = jax.random.key(seed)
        x = 7.22e-05 + 1 * jax.random.normal(jax.random.fold_in(_rk, 1), (64, 32, 256), jnp.float32)
        _lenS = 32 - jax.random.randint(jax.random.fold_in(_rk, 7), (64,), 0, max(1, 32 // 4) + 1, jnp.int32)
        _lenS2 = 257 - jax.random.randint(jax.random.fold_in(_rk, 8), (64,), 0, max(1, 257 // 4) + 1, jnp.int32)
        _ctx_1024P = jax.random.normal(jax.random.fold_in(_rk, 11), (64, 16, 256), jnp.float32)
        _ctx_1024c = jax.random.dirichlet(jax.random.fold_in(_rk, 511), 0.3 * jnp.ones((16,), jnp.float32), (64, 257))
        _ctx_1024t = jnp.einsum('bsk,bkd->bsd', _ctx_1024c, _ctx_1024P)
        _ctx_1024t = _ctx_1024t * jax.lax.rsqrt(jnp.mean(jnp.square(_ctx_1024t)) + 1e-12) * 0.953939
        ctx_1024 = 4.13588e-05 + 0.999923 * (_ctx_1024t + 0.3 * jax.random.normal(jax.random.fold_in(_rk, 611), (64, 257, 256), jnp.float32))
        return (x, ctx_1024)
    x, ctx_1024 = _rec_inputs()

    def _L0_xattn_setup():
        import jax, jax.numpy as jnp
        import numpy as np
        B, S, D = (4, 512, 256)
        key = jax.random.key(seed)
        ks = jax.random.split(key, 10)
        sc = 1.0 / np.sqrt(D)
        return {'x': jax.random.normal(ks[0], (B, S, D), dtype=jnp.float32), 'y': jax.random.normal(ks[1], (B, S, D), dtype=jnp.float32), 'Wq': jax.random.normal(ks[2], (D, D), dtype=jnp.float32) * sc, 'bq': jnp.zeros((D,), dtype=jnp.float32), 'Wk': jax.random.normal(ks[3], (D, D), dtype=jnp.float32) * sc, 'bk': jnp.zeros((D,), dtype=jnp.float32), 'Wv': jax.random.normal(ks[4], (D, D), dtype=jnp.float32) * sc, 'bv': jnp.zeros((D,), dtype=jnp.float32), 'Wr': jax.random.normal(ks[5], (D, D), dtype=jnp.float32) * sc, 'br': jnp.zeros((D,), dtype=jnp.float32)}
    _L0_xattn_all = _L0_xattn_setup()
    _L0_xattn_in = {k: v for k, v in _L0_xattn_all.items() if k in ('Wq', 'bq', 'Wk', 'bk', 'Wv', 'bv', 'Wr', 'br')}
    del _L0_xattn_all

    def _L0_attn_setup():
        import math
        import jax, jax.numpy as jnp
        import numpy as np
        K_TOP = 8
        D_HEAD = 32

        def causal_topk_adjacency(x, K):
            B, T, D = x.shape
            sim = jnp.einsum('btd,bsd->bts', x, x) / math.sqrt(D)
            causal = jnp.tril(jnp.ones((T, T), dtype=bool), k=-1)
            neg = jnp.finfo(sim.dtype).min
            sim_m = jnp.where(causal[None], sim, neg)
            vals, idx = jax.lax.top_k(sim_m, K)
            valid = (vals > neg).astype(x.dtype)
            b = jnp.arange(B)[:, None, None]
            t = jnp.arange(T)[None, :, None]
            A = jnp.zeros((B, T, T), x.dtype).at[b, t, idx].max(valid)
            return A
        key = jax.random.key(seed)
        ks = jax.random.split(key, 3)
        B, T, D = (2, 1024, 256)
        x = jax.random.normal(ks[0], (B, T, D), dtype=jnp.float32)
        W_q = jax.random.normal(ks[1], (D_HEAD, D), dtype=jnp.float32) * (1.0 / math.sqrt(D))
        W_k = jax.random.normal(ks[2], (D_HEAD, D), dtype=jnp.float32) * (1.0 / math.sqrt(D))
        gain = jnp.ones((D,), dtype=jnp.float32)
        bias = jnp.zeros((D,), dtype=jnp.float32)
        log_mix = jnp.zeros((), dtype=jnp.float32)
        log_scale = jnp.zeros((), dtype=jnp.float32)
        return {'x': x, 'W_q': W_q, 'W_k': W_k, 'gain': gain, 'bias': bias, 'log_mix': log_mix, 'log_scale': log_scale}
    _L0_attn_all = _L0_attn_setup()
    _L0_attn_in = {k: v for k, v in _L0_attn_all.items() if k in ('W_q', 'W_k', 'gain', 'bias', 'log_mix', 'log_scale')}
    del _L0_attn_all

    def _L0_ffn_setup():
        import jax, jax.numpy as jnp
        import numpy as np
        B, S, D, E, F = (2, 512, 256, 8, 1024)
        key = jax.random.key(seed)
        ks = jax.random.split(key, 4)
        return {'hidden_states': jax.random.normal(ks[0], (B, S, D), dtype=jnp.float32), 'Wr': jax.random.normal(ks[1], (D, E), dtype=jnp.float32) * (1.0 / np.sqrt(D)), 'W1': jax.random.normal(ks[2], (E, D, F), dtype=jnp.float32) * (1.0 / np.sqrt(D)), 'b1': jnp.zeros((E, F), dtype=jnp.float32), 'W2': jax.random.normal(ks[3], (E, F, D), dtype=jnp.float32) * (1.0 / np.sqrt(F)), 'b2': jnp.zeros((E, D), dtype=jnp.float32)}
    _L0_ffn_all = _L0_ffn_setup()
    _L0_ffn_in = {k: v for k, v in _L0_ffn_all.items() if k in ('Wr', 'W1', 'b1', 'W2', 'b2')}
    del _L0_ffn_all
    return {'x': x, 'ctx_1024': ctx_1024, 'L0_xattn_Wq': _L0_xattn_in['Wq'], 'L0_xattn_bq': _L0_xattn_in['bq'], 'L0_xattn_Wk': _L0_xattn_in['Wk'], 'L0_xattn_bk': _L0_xattn_in['bk'], 'L0_xattn_Wv': _L0_xattn_in['Wv'], 'L0_xattn_bv': _L0_xattn_in['bv'], 'L0_xattn_Wr': _L0_xattn_in['Wr'], 'L0_xattn_br': _L0_xattn_in['br'], 'L0_attn_W_q': _L0_attn_in['W_q'], 'L0_attn_W_k': _L0_attn_in['W_k'], 'L0_attn_gain': _L0_attn_in['gain'], 'L0_attn_bias': _L0_attn_in['bias'], 'L0_attn_log_mix': _L0_attn_in['log_mix'], 'L0_attn_log_scale': _L0_attn_in['log_scale'], 'L0_ffn_Wr': _L0_ffn_in['Wr'], 'L0_ffn_W1': _L0_ffn_in['W1'], 'L0_ffn_b1': _L0_ffn_in['b1'], 'L0_ffn_W2': _L0_ffn_in['W2'], 'L0_ffn_b2': _L0_ffn_in['b2']}

def reference(x, ctx_1024, L0_xattn_Wq, L0_xattn_bq, L0_xattn_Wk, L0_xattn_bk, L0_xattn_Wv, L0_xattn_bv, L0_xattn_Wr, L0_xattn_br, L0_attn_W_q, L0_attn_W_k, L0_attn_gain, L0_attn_bias, L0_attn_log_mix, L0_attn_log_scale, L0_ffn_Wr, L0_ffn_W1, L0_ffn_b1, L0_ffn_W2, L0_ffn_b2):
    import jax
    import jax.numpy as jnp

    def _L0_xattn_ref(x, y, Wq, bq, Wk, bk, Wv, bv, Wr, br):
        import jax, jax.numpy as jnp
        import numpy as np
        B, S, D = (4, 512, 256)
        Q = jnp.einsum('bsd,de->bse', x, Wq) + bq
        K = jnp.einsum('bsd,de->bse', y, Wk) + bk
        V = jnp.einsum('bsd,de->bse', y, Wv) + bv
        K_hat = jnp.cos(jnp.einsum('bsd,dr->bsr', K, Wr) + br)
        scores = jnp.einsum('bqr,bkr->bqk', Q, K_hat)
        probs = jax.nn.softmax(scores, axis=-1)
        return jnp.einsum('bqk,bkd->bqd', probs, V)

    def _L0_attn_ref(x, W_q, W_k, gain, bias, log_mix, log_scale):
        import math
        import jax, jax.numpy as jnp
        import numpy as np
        K_TOP = 8
        D_HEAD = 32

        def causal_topk_adjacency(x, K):
            B, T, D = x.shape
            sim = jnp.einsum('btd,bsd->bts', x, x) / math.sqrt(D)
            causal = jnp.tril(jnp.ones((T, T), dtype=bool), k=-1)
            neg = jnp.finfo(sim.dtype).min
            sim_m = jnp.where(causal[None], sim, neg)
            vals, idx = jax.lax.top_k(sim_m, K)
            valid = (vals > neg).astype(x.dtype)
            b = jnp.arange(B)[:, None, None]
            t = jnp.arange(T)[None, :, None]
            A = jnp.zeros((B, T, T), x.dtype).at[b, t, idx].max(valid)
            return A
        B, T, D = x.shape
        mix = jax.nn.sigmoid(log_mix)
        scale = jax.nn.softplus(log_scale) + 0.01
        A = causal_topk_adjacency(x, K_TOP)
        q = jnp.einsum('btd,hd->bth', x, W_q)
        k = jnp.einsum('bsd,hd->bsh', x, W_k)
        score = jnp.einsum('bth,bsh->bts', q, k) / math.sqrt(D_HEAD)
        score = jnp.where(A < 0.5, -1000000000.0, score)
        row_max = jax.lax.stop_gradient(jnp.max(score, axis=-1, keepdims=True))
        score = score - row_max
        attn = jax.nn.softmax(score, axis=-1)
        attn = jnp.nan_to_num(attn, nan=0.0)
        msg = jnp.einsum('bts,bsd->btd', attn, x)
        blended = mix * x + (1.0 - mix) * msg
        delta = jax.nn.gelu(blended * gain + bias, approximate=False) * scale
        return delta

    def _L0_ffn_ref(hidden_states, Wr, W1, b1, W2, b2):
        import jax, jax.numpy as jnp
        import numpy as np
        B, S, D, E, F = (2, 512, 256, 8, 1024)
        b, s, d = hidden_states.shape
        e = Wr.shape[1]
        x = hidden_states.reshape(b * s, d)
        router_logits = x @ Wr
        router_probs = jax.nn.softmax(router_logits, axis=-1)
        expert_idx = jnp.argmax(router_probs, axis=-1)
        p_max = jnp.max(router_probs, axis=-1, keepdims=True)

        def expert_mlp(w1, bb1, w2, bb2):
            h = jax.nn.gelu(x @ w1 + bb1, approximate=False)
            return h @ w2 + bb2
        outs = jax.vmap(expert_mlp)(W1, b1, W2, b2)
        onehot = jax.nn.one_hot(expert_idx, e, dtype=x.dtype)
        next_states = jnp.einsum('te,etd->td', onehot, outs)
        out = p_max * next_states
        return out.reshape(b, s, d)
    x = x + _L0_xattn_ref(_layernorm(x, axis=-1), ctx_1024, L0_xattn_Wq, L0_xattn_bq, L0_xattn_Wk, L0_xattn_bk, L0_xattn_Wv, L0_xattn_bv, L0_xattn_Wr, L0_xattn_br)
    x = x + _L0_attn_ref(_layernorm(x, axis=-1), L0_attn_W_q, L0_attn_W_k, L0_attn_gain, L0_attn_bias, L0_attn_log_mix, L0_attn_log_scale)
    x = x + _L0_ffn_ref(_layernorm(x, axis=-1), L0_ffn_Wr, L0_ffn_W1, L0_ffn_b1, L0_ffn_W2, L0_ffn_b2)
    return x

_drawn_inputs = setup_inputs


def setup_inputs(seed=0):
    import zlib

    import numpy as np

    out = dict(_drawn_inputs(seed))
    spreads = {'L0_xattn_bq': (0.0, 0.1),
     'L0_xattn_bk': (0.0, 0.1),
     'L0_xattn_bv': (0.0, 0.1),
     'L0_xattn_br': (0.0, 0.1),
     'L0_attn_gain': (1.0, 0.2),
     'L0_attn_bias': (0.0, 0.1),
     'L0_ffn_b1': (0.0, 0.5),
     'L0_ffn_b2': (0.0, 0.347)}
    factors = {}
    for name, (base, spread) in spreads.items():
        noise = np.random.default_rng([zlib.crc32(name.encode()), seed]).standard_normal(out[name].shape)
        drawn = base * np.exp(spread * noise) if base else spread * noise
        out[name] = jnp.asarray(drawn.astype(out[name].dtype))
    for name, factor in factors.items():
        out[name] = (out[name] * factor).astype(out[name].dtype)
    return out
```

```python
from contextlib import ExitStack

import numpy as np

import concourse.bass as bass
from concourse import mybir

F32 = mybir.dt.float32
BF16 = mybir.dt.bfloat16
I32 = mybir.dt.int32
ALU = mybir.AluOpType
ACT = mybir.ActivationFunctionType
AX = mybir.AxisListType

B, T, D, C = 64, 32, 256, 257
P = 128
DC = D // P
TOK = B * T
NG = TOK // P
BG = P // T
CF = C - 1
CC = CF // P
E, F = 8, 1024
FC = F // P
H = 32
NBLK = TOK // P + E - 1
SLOTS = NBLK * P
TOP = 8

EPS = 1e-5
INV_2PI = float(1.0 / (2.0 * np.pi))
TWO_PI = 6.283185
ROUND = float(3 << 22)
LOWEST = -3.4028234663852886e38
PICKED = 3.0e38
UNPICKED = -1.0e9
OUTSIDE = -3.0e38

STAGES = 5
PEELED = 6


def at_least(eng, sem, count):
    if not isinstance(count, int) or count > 0:
        eng.wait_ge(sem, count)


def settle(eng, sem):
    eng.wait_ge(sem, 1)


def in_register(eng, count):
    return count if isinstance(count, int) else eng.to_reg(count)


def upto(value, most):
    return min(value, most) if isinstance(value, int) else value


def groups(k, parity, behind):
    g = 2 * k + parity - behind
    if isinstance(g, int) and not 0 <= g < NG:
        return None
    return g, (parity - behind) % 2, k + (parity - behind) // 2


def run_steps(eng, step):
    for s in range(PEELED):
        step(s // 2, s % 2)
    with eng.Fori(PEELED // 2, NG // 2 - 1) as k:
        step(k, 0)
        step(k, 1)
    for s in range(NG - 2, NG + STAGES - 1):
        step(s // 2, s % 2)


def run_blocks(eng, step):
    for j in range(2):
        step(j, j, 0)
    with eng.Fori(1, (NBLK - 3) // 2) as k:
        step(2 * k, 0, k)
        step(2 * k + 1, 1, k)
    for j in range(NBLK - 3, NBLK):
        step(j, j % 2, j // 2)


def perceiver_layer(nc, a, out):
    ctx = ExitStack()
    with ctx:
        def sb(name, shape, dt=F32):
            return ctx.enter_context(nc.sbuf_tensor(name, shape, dt))

        def ps(name):
            return ctx.enter_context(nc.psum_tensor(name, [P, 512], F32))

        def sem(name):
            return ctx.enter_context(nc.semaphore(name))

        xs_dram = nc.dram_tensor("sorted_tokens", [SLOTS, D], F32, kind="Internal").ap()
        ys_dram = nc.dram_tensor("sorted_results", [SLOTS, D], F32, kind="Internal").ap()

        X = sb("X", [P, NG, D])
        XN = sb("XN", [P, NG * D])
        xn_all = XN[:, :].rearrange("p (g d) -> p g d", g=NG)
        spare = XN[:, (NG - 4) * D:]
        W1 = sb("W1", [P, E, DC, F])
        W2 = sb("W2", [P, E * FC * D])
        w2 = W2[:, :].rearrange("p (e c d) -> p e c d", e=E, c=FC)
        used = [0]

        def room(n):
            used[0] += n
            assert used[0] <= E * FC * D
            return W2[:, used[0] - n:used[0]]

        ctx_rows = [room(BG * CC * D).rearrange("p (j c d) -> p j c d", j=BG, c=CC) for _ in range(2)]
        ctx_T = room(DC * BG * CF).rearrange("p (c n) -> p c n", c=DC)
        khat = [room(DC * BG * C).rearrange("p (r j n) -> p r j n", r=DC, j=BG) for _ in range(2)]
        turns = [room(512) for _ in range(2)]
        frac = [room(512) for _ in range(2)]
        bias_rows = room(F + D)
        bias_part = room((F + D) // 2).bitcast(BF16)
        ctx_last = sb("ctx_last", [BG, 2, D])

        ident = sb("ident", [P, P])
        tri = sb("tri", [P, P], BF16)
        ones = sb("ones", [P, P], BF16)
        own_batch = sb("own_batch", [P, BG])
        causal = sb("causal", [P, P])
        pickable = sb("pickable", [P, P])
        unpicked = sb("unpicked", [P, P])
        zeros = sb("zeros", [P, D])
        minus_half = sb("minus_half", [P, 1])

        Wk, WkT, Wr = (room(DC * D).rearrange("p (c n) -> p c n", c=DC) for _ in range(3))
        Wkr = sb("Wkr", [P, DC, D])
        Wq = sb("Wq", [P, DC, D])
        Wv = sb("Wv", [P, DC, D])
        bq = sb("bq", [P, DC])
        bk = sb("bk", [P, DC])
        br = sb("br", [P, DC])
        bkr = sb("bkr", [P, DC])
        bv = sb("bv", [P, D])
        Wqk = sb("Wqk", [2 * H, D])
        WqkT = sb("WqkT", [P, DC, 2 * H])
        Wroute = sb("Wroute", [P, DC, E])
        gain = spare[:, 0:D]
        gbias = sb("gbias", [P, D])
        gain_msg = sb("gain_msg", [P, D])
        gain_self = sb("gain_self", [P, D])
        logs = sb("logs", [P, 2])
        sc = sb("sc", [P, 12])
        b_parts = sb("b_parts", [P, F + D], BF16)
        last_rows = spare[0:B, D:2 * D]
        last_T, last_turns, last_frac = (spare[:, 2 * D + i * P:2 * D + (i + 1) * P].rearrange("p (c n) -> p c n", c=DC)
                                         for i in range(3))
        khat_last = sb("khat_last", [P, DC, B])

        st1, st2, st3 = (sb(f"st{i}", [P, 6]) for i in (1, 2, 3))
        mv1, mv2, mv3 = (sb(f"mv{i}", [P, 2]) for i in (1, 2, 3))
        ve1, ve2, ve3 = (sb(f"ve{i}", [P, 1]) for i in (1, 2, 3))
        rs1, rs2, rs3 = (sb(f"rs{i}", [P, 1]) for i in (1, 2, 3))
        xn = sb("xn", [P, 2, D])
        xn3 = sb("xn3", [P, 2, D])
        xnT = sb("xnT", [P, DC, P])
        qT = sb("qT", [P, DC, P])
        nmaxA = sb("nmaxA", [P, 1])
        sumA = sb("sumA", [P, 1])
        rsumA = sb("rsumA", [P, 1])
        probs = sb("probs", [P, C])
        p_last = sb("p_last", [P, BG])
        probsT = sb("probsT", [P, CC, P])
        p_lastT = sb("p_lastT", [BG, P])
        o_norm = sb("o_norm", [P, D])
        o_T = sb("o_T", [P, DC, P])
        h = sb("h", [P, 2, D])
        hg = sb("hg", [P, 2, D])
        hT = sb("hT", [P, DC, P])
        qB = sb("qB", [H, P])
        kB = sb("kB", [H, P])
        simm = sb("simm", [P, P])
        top8 = sb("top8", [P, TOP])
        marked = sb("marked", [P, P])
        pick = sb("pick", [P, P], I32)
        scoreB = sb("scoreB", [P, 2, P])
        nmaxB = sb("nmaxB", [P, 2])
        expB = sb("expB", [P, P])
        sumB = sb("sumB", [P, 1])
        rsumB = sb("rsumB", [P, 1])
        att = sb("att", [P, P])
        attT = sb("attT", [P, P])
        y_msg = sb("y_msg", [P, D])
        y = sb("y", [P, D])
        gel = sb("gel", [P, D])
        xn3T = sb("xn3T", [P, DC, P])

        logits = sb("logits", [P, NG, E])
        rt = [t.rearrange("p (g e) -> p g e", g=NG) for t in (y_msg[:, 0:P], y_msg[:, P:2 * P], y[:, 0:P])]
        onehot = sb("onehot", [P, NG, E], BF16)
        per_token = sb("per_token", [P, 3, NG])
        p_max = sb("p_max", [P, NG])
        slot = sb("slot", [P, NG], I32)
        order_w = sb("order_w", [P, E])
        order_i = sb("order_i", [P, E], I32)
        cnt = sb("cnt", [P, E], BF16)
        blocks_i = sb("blocks_i", [P, 2, E], I32)
        blocks = sb("blocks", [P, E])
        ends = sb("ends", [P, E])
        starts = sb("starts", [P, E])
        one8 = sb("one8", [P, E])
        blk_i = sb("blk_i", [P, NBLK], I32)
        blk = sb("blk", [P, NBLK])
        past = gel[:, 0:NBLK * E].rearrange("p (n e) -> p n e", n=NBLK)
        expert = sb("expert", [P, NBLK])
        expert_i = sb("expert_i", [P, NBLK], I32)
        row_i = spare[:, 2 * D + 3 * P:2 * D + 4 * P].bitcast(I32)
        row_e = sb("row_e", [P, P])
        f_sel = simm[:].bitcast(BF16).rearrange("p (b n) -> p b n", b=2)
        f_h = XN[:, 0:F]
        f_hT = XN[:, F:2 * F]
        f_in, f_inT, f_out = (XN[:, 2 * F + 2 * i * D:2 * F + 2 * (i + 1) * D].rearrange("p (b n) -> p b n", b=2)
                              for i in range(3))

        pT = [ps("pT0"), ps("pT1")]
        pK = [ps("pK0"), ps("pK1")]
        b4, b5, b6, b7 = ps("b4"), ps("b5"), ps("b6"), ps("b7")
        p_score = b4[:, 0:C]
        p_pT = b4[:, 0:CF]
        p_plT = b4[0:BG, CF:CF + P]
        p_attT = b4[:, 0:P]
        p_oT = b4[:, 0:D]
        p_xnT = b5[:, 0:D]
        p_sim = b5[:, 0:P]
        p_scoreB = b5[:, 0:P]
        p_msg = b5[:, 0:D]
        p_hT = b6[:, 0:D]
        p_qk = b6[0:2 * H, 0:P]
        p_q = b6[:, 0:D]
        p_a = b6[:, 0:D]
        p_o = b7[:, 0:D]
        p_xn3T = b7[:, 0:D]
        p_route = b7[:, 0:E]
        p_in = (b6[:, 0:D], b7[:, 0:D])
        p_out = (b4[:, 0:D], b5[:, 0:D])

        names = """consts wk_ld w_ld x_ld xrest_ld last_ld bias_ld logs_ld xs_zero w1_ld w2_ld
            wkT_tr wkT_cp wkr_mm wkr_cp wqkT_tr wqkT_cp bkr_mm bkr_sum bkr_cp lastT_tr lastT_cp lastK_mm
            last_turn last_whole last_fr khat_last_r scal_act scal_dve gains bsplit bparts
            ctxT_tr ctxT0_cp ctxT1_cp kproj turns_r whole_r frac_r khat_r klast_r
            st1_r mv1_r ve1_r rs1_r xn_r xb_r xnT_tr xnT_cp qproj q_r
            scoresA nmaxA_r probsA rsumA_r plast_r pT_tr pT_cp pv o_r oT_tr oT_cp aproj x1_r
            st2_r mv2_r ve2_r rs2_r h_r hg_m hg_r hT_tr hT_cp sim_mm qk_mm qk_cp
            simm_r top_r marked_r pick_r base_r scoreB_mm selected nmaxB_r
            probsB rsumB_r att_r attT_tr attT_cp msg_mm ymsg_r y_r gelu_r x2_r
            st3_r mv3_r ve3_r rs3_r xn3_r xn3_kept xn3T_tr xn3T_cp route_mm logits_r
            route route_exp rank_mm slot_r expert_r scattered
            f_sel_r f_inT_tr f_inT_cp f_h_mm f_gelu f_hT_tr f_hT0_cp f_hT1_cp f_y_mm f_y_cp
            out_add stored""".split()
        S = {n: sem(n) for n in names}
        ctx_ld = [sem("ctx_ld0"), sem("ctx_ld1")]
        f_in_ld = [sem("f_in_ld0"), sem("f_in_ld1")]
        f_y_st = [sem("f_y_st0"), sem("f_y_st1")]
        gathered = [sem(f"gathered{i}") for i in range(NG // 2)]

        block = ctx.enter_context(nc.Block())
        CTX_LOADS = CC + 1
        W_LOADS = 9
        made_at = {}

        x_v = a["x"].rearrange("(g j) t d -> (j t) g d", j=BG)
        out_v = out.rearrange("(g j) t d -> (j t) g d", j=BG)
        c_in = a["ctx_1024"]

        def col(v):
            return v.rearrange("(c p) -> p c", p=P)

        def rows(w):
            return w.rearrange("(c p) n -> p c n", p=P)

        def group_of(t, g):
            return t[:, bass.ds(g, 1), :].rearrange("p o d -> p (o d)")

        @block.gpsimd
        def _(pool):
            n = [0]

            def made(ins):
                n[0] += 1
                ins.then_inc(S["consts"], 1)
                pool.wait_ge(S["consts"], n[0])

            def keep(t, pattern, base, mult, cmp, fill):
                made(pool.affine_select(t, t, pattern, cmp, fill, base=base, channel_multiplier=mult))

            def rstd(g, mv, ve, rs, mv_r, ve_r, rs_r):
                count = in_register(pool, g + 1)
                settle(pool, S["consts"])
                pool.wait_ge(S[mv_r], count)
                pool.tensor_scalar(ve[:], mv[:, 1:2], EPS, None, ALU.add).then_inc(S[ve_r], 1)
                pool.wait_ge(S[ve_r], g + 1)
                pool.tensor_tensor(rs[:], ve[:], minus_half[:], ALU.pow).then_inc(S[rs_r], 1)

            def norm_x(g):
                rstd(g, mv1, ve1, rs1, "mv1_r", "ve1_r", "rs1_r")
                pool.wait_ge(S["xn_r"], g + 1)
                pool.tensor_tensor(group_of(X, g), group_of(X, g), bv[:], ALU.add).then_inc(S["xb_r"], 1)

            made(pool.memset(ident[:], 0.0))
            keep(ident[:], [[-1, P]], 0, 1, ALU.not_equal, 1.0)
            made_at["ident"] = n[0]
            made(pool.memset(minus_half[:], -0.5))
            made(pool.memset(zeros[:], 0.0))
            made_at["zeros"] = n[0]
            pool.wait_ge(S["w_ld"], 16 * W_LOADS)
            norm_x(0)

            made(pool.memset(own_batch[:], 1.0))
            keep(own_batch[:], [[-T, BG]], 0, 1, ALU.is_ge, 0.0)
            keep(own_batch[:], [[T, BG]], T - 1, -1, ALU.is_ge, 0.0)
            made_at["own_batch"] = n[0]
            pool.wait_ge(S["scal_dve"], 3)
            pool.tensor_scalar(gain_msg[:], gain, sc[:, 3:4], None, ALU.mult).then_inc(S["gains"], 1)
            pool.tensor_scalar(gain_self[:], gain, sc[:, 2:3], None, ALU.mult).then_inc(S["gains"], 1)
            for t, start, fill in ((causal, 0.0, LOWEST), (pickable, PICKED, 1.0), (unpicked, UNPICKED, OUTSIDE)):
                v = t[:].rearrange("p (j n) -> p j n", j=BG)
                made(pool.memset(t[:], start))
                keep(v, [[-T, BG], [0, T]], 0, 1, ALU.is_ge, fill)
                keep(v, [[T, BG], [0, T]], T - 1, -1, ALU.is_ge, fill)
                if t is not unpicked:
                    keep(v, [[-T, BG], [-1, T]], 0, 1, ALU.is_gt, fill)
            made_at["masks"] = n[0]
            pool.wait_ge(S["gains"], 2)

            def step(k, parity):
                if w := groups(k, parity, 0):
                    g, b, _ = w
                    if isinstance(g, int) and g == 0:
                        pool.wait_ge(S["khat_last_r"], 1)
                    settle(pool, S["consts"])
                    at_least(pool, S["scoresA"], g - 1)
                    pool.tensor_copy(khat[b][:, :, :, CF], khat_last[:, :, bass.ds(g * BG, BG)]
                                     ).then_inc(S["klast_r"], 1)
                if w := groups(k, parity, 2):
                    g, b, _ = w
                    count = in_register(pool, g - 1)
                    settle(pool, S["consts"])
                    at_least(pool, S["probsB"], count)
                    pool.tensor_copy(scoreB[:, b, :], unpicked[:]).then_inc(S["base_r"], 1)
                if w := groups(k, parity, 4):
                    g, b, _ = w
                    rstd(g, mv3, ve3, rs3, "mv3_r", "ve3_r", "rs3_r")
                    settle(pool, S["consts"])
                    pool.wait_ge(S["xn3_r"], g + 1)
                    pool.tensor_copy(group_of(xn_all, g), xn3[:, b, :]).then_inc(S["xn3_kept"], 1)
                if w := groups(k, parity, 1):
                    g, b, _ = w
                    rstd(g, mv2, ve2, rs2, "mv2_r", "ve2_r", "rs2_r")
                    pool.wait_ge(S["h_r"], g + 1)
                    at_least(pool, S["y_r"], g - 1)
                    pool.tensor_tensor(hg[:, b, :], h[:, b, :], gain_self[:], ALU.mult).then_inc(S["hg_m"], 1)
                    pool.wait_ge(S["hg_m"], g + 1)
                    pool.tensor_tensor(hg[:, b, :], hg[:, b, :], gbias[:], ALU.add).then_inc(S["hg_r"], 1)
                if w := groups(k, parity, -1):
                    norm_x(w[0])
                if isinstance(k, int) and 2 * k + parity == 0:
                    made(pool.memset(b_parts[:], 0.0))
                    made(pool.memset(bias_rows, 0.0))
                    for i in range(3):
                        at = slice(32 * i, 32 * i + E)
                        pool.dma_start(bias_rows[at, 0:F], a["L0_ffn_b1"]).then_inc(S["bias_ld"], 16)
                        pool.dma_start(bias_rows[at, F:F + D], a["L0_ffn_b2"]).then_inc(S["bias_ld"], 16)
                    pool.wait_ge(S["bias_ld"], 6 * 16)
                    for i in range(3):
                        at = slice(32 * i, 32 * i + E)
                        pool.tensor_copy(bias_part, bias_rows).then_inc(S["bsplit"], 1)
                        pool.wait_ge(S["bsplit"], 2 * i + 1)
                        pool.tensor_copy(b_parts[at, :], bias_part[at, :]).then_inc(S["bparts"], 1)
                        pool.wait_ge(S["bparts"], i + 1)
                        pool.tensor_tensor(bias_rows, bias_rows, bias_part, ALU.subtract).then_inc(S["bsplit"], 1)
                        pool.wait_ge(S["bsplit"], 2 * i + 2)
                if isinstance(k, int) and 2 * k + parity == 1:
                    made(pool.memset(ones[:], 1.0))
                    made(pool.memset(tri[:], 1.0))
                    keep(tri[:], [[1, P]], 0, -1, ALU.is_gt, 0.0)
                    made(pool.iota(order_i[:], [[-1, E]], base=E, channel_multiplier=0))
                    made(pool.tensor_copy(order_w[:], order_i[:]))
                    made(pool.iota(blk_i[:], [[1, NBLK]], base=0, channel_multiplier=0))
                    made(pool.tensor_copy(blk[:], blk_i[:]))
                    made(pool.memset(one8[:], 1.0))
                    for q in range(0, P, 32):
                        made(pool.iota(row_i[q:q + 32, :], [[0, P]], base=0, channel_multiplier=1))
                    made(pool.tensor_copy(row_e[:], row_i))
                    made_at["routing"] = n[0]

            run_steps(pool, step)

            pool.wait_ge(S["slot_r"], 1)
            pool.wait_ge(S["xs_zero"], 16)
            pool.wait_ge(S["xn3_kept"], NG)
            for g in range(NG):
                pool.indirect_dma_start(xs_dram, bass.IndirectOffsetOnAxis(ap=slot[:, g:g + 1], axis=0),
                                        xn_all[:, g, :], None).then_inc(S["scattered"], 16)

            pool.wait_ge(f_y_st[0], 16 * ((NBLK + 1) // 2))
            pool.wait_ge(f_y_st[1], 16 * (NBLK // 2))
            for g in range(NG):
                pool.indirect_dma_start(xn_all[:, g, :], None, ys_dram,
                                        bass.IndirectOffsetOnAxis(ap=slot[:, g:g + 1], axis=0)
                                        ).then_inc(gathered[g // 2], 16)

        @block.sync
        def _(sp):
            def load_ctx(g, b):
                for i in range(CC):
                    sp.dma_start(ctx_rows[b][:, :, i, :],
                                 c_in[bass.ds(g * BG, BG), i * P:(i + 1) * P, :].rearrange("j p d -> p j d")
                                 ).then_inc(ctx_ld[b], 16)
                sp.dma_start(ctx_last[:, b, :], c_in[bass.ds(g * BG, BG), CF, :]).then_inc(ctx_ld[b], 16)

            sp.dma_start(Wk, rows(a["L0_xattn_Wk"])).then_inc(S["wk_ld"], 16)
            sp.dma_start(Wr, rows(a["L0_xattn_Wr"])).then_inc(S["wk_ld"], 16)
            load_ctx(0, 0)
            sp.dma_start(last_rows, c_in[:, CF, :]).then_inc(S["last_ld"], 16)
            sp.dma_start(X[:, 2:NG, :], x_v[:, 2:NG, :]).then_inc(S["xrest_ld"], 16)
            load_ctx(1, 1)
            sp.wait_ge(S["consts"], made_at["zeros"])
            sp.dma_start(xs_dram.rearrange("(n p) d -> p n d", p=P),
                         zeros[:].rearrange("p (o d) -> p o d", o=1).to_broadcast([P, NBLK, D])
                         ).then_inc(S["xs_zero"], 16)

            def load_w1(e):
                sp.dma_start(W1[:, bass.ds(e, 1)].rearrange("p e c f -> p (e c) f"),
                             a["L0_ffn_W1"][bass.ds(e, 1)].rearrange("e (c p) f -> p (e c) f", p=P)
                             ).then_inc(S["w1_ld"], 16)

            load_w1(0)
            with sp.Fori(1, NG // 2) as k:
                for b in range(2):
                    sp.wait_ge(S["pv"], 2 * k + b - 1)
                    load_ctx(2 * k + b, b)
                load_w1(k)
            sp.wait_ge(S["pv"], NG)
            sp.wait_ge(S["bparts"], 3)
            for e in range(E):
                sp.dma_start(w2[:, e], rows(a["L0_ffn_W2"][e])).then_inc(S["w2_ld"], 16)

            def load_block(j, b):
                sp.dma_start(f_in[:, b, :], xs_dram[bass.ds(j * P, P), :]).then_inc(f_in_ld[b], 16)

            def next_block(j, b, k):
                if not isinstance(j, int) or j + 2 < NBLK:
                    sp.wait_ge(S["f_inT_tr"], j + 1)
                    load_block(j + 2, b)

            sp.wait_ge(S["scattered"], 16 * NG)
            load_block(0, 0)
            load_block(1, 1)
            run_blocks(sp, next_block)
            for g in range(0, NG, 4):
                sp.wait_ge(S["out_add"], g + 4)
                sp.dma_start(out_v[:, g:g + 4, :], X[:, g:g + 4, :]).then_inc(S["stored"], 16)
            sp.wait_ge(S["stored"], 16 * NG // 4)

        @block.vector
        def _(v):
            def stats(g, st, mv, st_r, mv_r):
                v.bn_stats(st[:], group_of(X, g)).then_inc(S[st_r], 1)
                count = in_register(v, g + 1)
                settle(v, S["consts"])
                v.wait_ge(S[st_r], count)
                v.bn_aggr(mv[:], st[:]).then_inc(S[mv_r], 1)

            def normal(g, dst, mv, rs, rs_r, done):
                v.wait_ge(S[rs_r], g + 1)
                v.tensor_scalar(dst, group_of(X, g), mv[:, 0:1], rs[:, 0:1], ALU.subtract, ALU.mult
                                ).then_inc(S[done], 1)

            def stats_x(g):
                if isinstance(g, int) and g in (0, 2):
                    v.wait_ge(S["x_ld" if g == 0 else "xrest_ld"], 16)
                stats(g, st1, mv1, "st1_r", "mv1_r")

            def normal_x(g, b):
                at_least(v, S["xnT_tr"], g - 1)
                normal(g, xn[:, b, :], mv1, rs1, "rs1_r", "xn_r")

            v.wait_ge(S["wkT_tr"], 1)
            v.tensor_copy(WkT.rearrange("p c n -> p (c n)"), pT[0][:]).then_inc(S["wkT_cp"], 1)
            stats_x(0)
            v.wait_ge(S["wkr_mm"], 1)
            v.tensor_scalar(Wkr[:].rearrange("p c n -> p (c n)"), pK[0][:], INV_2PI, None, ALU.mult
                            ).then_inc(S["wkr_cp"], 1)
            v.wait_ge(S["bkr_mm"], 1)
            v.tensor_tensor(bkr[:], b4[:, 0:DC], br[:], ALU.add).then_inc(S["bkr_sum"], 1)
            v.wait_ge(S["bkr_sum"], 1)
            v.tensor_scalar(bkr[:], bkr[:], INV_2PI, 0.25, ALU.mult, ALU.add).then_inc(S["bkr_cp"], 1)
            normal_x(0, 0)
            v.wait_ge(S["wqkT_tr"], 1)
            v.tensor_copy(WqkT[:].rearrange("p c n -> p (c n)"), b5[:, 0:DC * 2 * H]).then_inc(S["wqkT_cp"], 1)
            v.wait_ge(S["lastT_tr"], 1)
            v.tensor_copy(last_T.rearrange("p c n -> p (c n)"), b7[:, 0:DC * B]).then_inc(S["lastT_cp"], 1)
            v.wait_ge(S["lastK_mm"], 1)
            v.wait_ge(S["bkr_cp"], 1)
            for r in range(DC):
                v.tensor_scalar(last_turns[:, r, :], b6[:, r * B:(r + 1) * B], bkr[:, r:r + 1], None, ALU.add
                                ).then_inc(S["last_turn"], 1)
            v.wait_ge(S["last_turn"], 2)
            v.tensor_scalar(last_frac, last_turns, ROUND, ROUND, ALU.add, ALU.subtract
                            ).then_inc(S["last_whole"], 1)
            v.wait_ge(S["last_whole"], 1)
            v.tensor_tensor(last_frac, last_turns, last_frac, ALU.subtract).then_inc(S["last_fr"], 1)
            v.wait_ge(S["scal_act"], 1)
            v.tensor_scalar(sc[:, 1:2], sc[:, 0:1], 1.0, None, ALU.add).then_inc(S["scal_dve"], 1)
            v.wait_ge(S["scal_dve"], 1)
            v.reciprocal(sc[:, 2:3], sc[:, 1:2]).then_inc(S["scal_dve"], 1)
            v.wait_ge(S["scal_dve"], 2)
            v.tensor_scalar(sc[:, 3:4], sc[:, 2:3], -1.0, 1.0, ALU.mult, ALU.add).then_inc(S["scal_dve"], 1)
            v.tensor_scalar(sc[:, 8:9], logs[:, 1:2], 0.0, 0.01, ALU.max, ALU.add).then_inc(S["scal_dve"], 1)
            v.wait_ge(S["scal_act"], 4)
            v.wait_ge(S["scal_dve"], 4)
            v.tensor_tensor(sc[:, 9:10], sc[:, 7:8], sc[:, 8:9], ALU.add).then_inc(S["scal_dve"], 1)
            v.wait_ge(S["scal_dve"], 5)

            def fraction(g, u):
                b = u % 2
                v.wait_ge(S["turns_r"], 4 * g + u + 1)
                at_least(v, S["khat_r"], 4 * g + u - 1)
                v.tensor_scalar(frac[b], turns[b], ROUND, ROUND, ALU.add, ALU.subtract).then_inc(S["whole_r"], 1)
                v.wait_ge(S["whole_r"], 4 * g + u + 1)
                v.tensor_tensor(frac[b], turns[b], frac[b], ALU.subtract).then_inc(S["frac_r"], 1)

            def ctx_T_copy(g, half):
                v.wait_ge(S["ctxT_tr"], 4 * g + 2 * half + 1)
                at_least(v, S["kproj"], 4 * g + 2 * half - 2)
                v.tensor_copy(ctx_T[:, 0, half * 512:(half + 1) * 512], pT[0][:]).then_inc(S["ctxT0_cp"], 1)

            def step(k, parity):
                if w := groups(k, parity, 1):
                    g, b, _ = w
                    v.wait_ge(S["scoresA"], g + 1)
                    v.tensor_reduce(nmaxA[:], p_score, AX.X, ALU.max, negate=True).then_inc(S["nmaxA_r"], 1)
                if w := groups(k, parity, 0):
                    g, b, _ = w
                    ctx_T_copy(g, 0)
                    v.wait_ge(S["xnT_tr"], g + 1)
                    at_least(v, S["qproj"], g)
                    v.tensor_copy(xnT[:].rearrange("p c n -> p (c n)"), p_xnT).then_inc(S["xnT_cp"], 1)
                if w := groups(k, parity, 4):
                    g, b, _ = w
                    v.wait_ge(S["gelu_r"], g + 1)
                    v.scalar_tensor_tensor(group_of(X, g), gel[:], sc[:, 9:10], group_of(X, g), ALU.mult, ALU.add
                                           ).then_inc(S["x2_r"], 1)
                    settle(v, S["consts"])
                    v.wait_ge(S["x2_r"], g + 1)
                    at_least(v, S["rs3_r"], g)
                    stats(g, st3, mv3, "st3_r", "mv3_r")
                if w := groups(k, parity, 3):
                    g, b, _ = w
                    v.wait_ge(S["probsB"], g + 1)
                    v.reciprocal(rsumB[:], sumB[:]).then_inc(S["rsumB_r"], 1)
                    v.wait_ge(S["rsumB_r"], g + 1)
                    at_least(v, S["attT_tr"], g)
                    v.tensor_scalar(att[:], expB[:], rsumB[:, 0:1], 0.0, ALU.mult, ALU.max).then_inc(S["att_r"], 1)
                if w := groups(k, parity, 1):
                    g, b, _ = w
                    v.wait_ge(S["probsA"], g + 1)
                    v.reciprocal(rsumA[:], sumA[:]).then_inc(S["rsumA_r"], 1)
                    if isinstance(g, int) and g == 0:
                        v.wait_ge(S["consts"], made_at["own_batch"])
                    at_least(v, S["pT_tr"], g)
                    v.tensor_scalar(p_last[:], own_batch[:], probs[:, CF:C], None, ALU.mult
                                    ).then_inc(S["plast_r"], 1)
                if w := groups(k, parity, 0):
                    fraction(w[0], 0)
                    fraction(w[0], 1)
                if w := groups(k, parity, 1):
                    g, b, _ = w
                    v.wait_ge(S["pT_tr"], g + 1)
                    at_least(v, S["pv"], g)
                    v.tensor_copy(probsT[:].rearrange("p c n -> p (c n)"), p_pT).then_inc(S["pT_cp"], 1)
                    v.tensor_copy(p_lastT[:], p_plT).then_inc(S["pT_cp"], 1)
                if w := groups(k, parity, 4):
                    g, b, _ = w
                    at_least(v, S["xn3_kept"], g)
                    at_least(v, S["xn3T_tr"], g)
                    normal(g, xn3[:, b, :], mv3, rs3, "rs3_r", "xn3_r")
                if w := groups(k, parity, 0):
                    ctx_T_copy(w[0], 1)
                if w := groups(k, parity, 2):
                    g, b, _ = w
                    if isinstance(g, int) and g == 0:
                        v.wait_ge(S["consts"], made_at["masks"])
                    v.wait_ge(S["sim_mm"], g + 1)
                    v.tensor_tensor(simm[:], p_sim, causal[:], ALU.add).then_inc(S["simm_r"], 1)
                    settle(v, S["consts"])
                    v.wait_ge(S["simm_r"], g + 1)
                    v.max(top8[:], simm[:]).then_inc(S["top_r"], 1)
                    settle(v, S["consts"])
                    v.wait_ge(S["top_r"], g + 1)
                    v.match_replace(marked[:], top8[:], simm[:], PICKED).then_inc(S["marked_r"], 1)
                    v.wait_ge(S["marked_r"], g + 1)
                    v.tensor_tensor(pick[:], marked[:], pickable[:], ALU.is_equal).then_inc(S["pick_r"], 1)
                if w := groups(k, parity, 3):
                    g, b, _ = w
                    v.wait_ge(S["attT_tr"], g + 1)
                    at_least(v, S["msg_mm"], g)
                    v.tensor_copy(attT[:], p_attT).then_inc(S["attT_cp"], 1)
                if w := groups(k, parity, 1):
                    g, b, _ = w
                    v.wait_ge(S["pv"], g + 1)
                    v.wait_ge(S["rsumA_r"], g + 1)
                    at_least(v, S["oT_tr"], g)
                    v.tensor_scalar(o_norm[:], p_o, rsumA[:, 0:1], None, ALU.mult).then_inc(S["o_r"], 1)
                if w := groups(k, parity, 2):
                    g, b, _ = w
                    settle(v, S["consts"])
                    v.wait_ge(S["scoreB_mm"], g + 1)
                    v.wait_ge(S["base_r"], g + 1)
                    v.wait_ge(S["pick_r"], g + 1)
                    v.copy_predicated(scoreB[:, b, :], pick[:], p_scoreB).then_inc(S["selected"], 1)
                    v.wait_ge(S["selected"], g + 1)
                    v.tensor_reduce(nmaxB[:, b:b + 1], scoreB[:, b, :], AX.X, ALU.max, negate=True
                                    ).then_inc(S["nmaxB_r"], 1)
                if w := groups(k, parity, 1):
                    g, b, _ = w
                    v.wait_ge(S["oT_tr"], g + 1)
                    at_least(v, S["aproj"], g)
                    v.tensor_copy(o_T[:].rearrange("p c n -> p (c n)"), p_oT).then_inc(S["oT_cp"], 1)
                if w := groups(k, parity, 0):
                    fraction(w[0], 2)
                    fraction(w[0], 3)
                if w := groups(k, parity, 3):
                    g, b, _ = w
                    v.wait_ge(S["msg_mm"], g + 1)
                    v.tensor_tensor(y_msg[:], p_msg, gain_msg[:], ALU.mult).then_inc(S["ymsg_r"], 1)
                    v.wait_ge(S["ymsg_r"], g + 1)
                    v.wait_ge(S["hg_r"], g + 1)
                    at_least(v, S["gelu_r"], g)
                    v.tensor_tensor(y[:], y_msg[:], hg[:, b, :], ALU.add).then_inc(S["y_r"], 1)
                if w := groups(k, parity, 1):
                    g, b, _ = w
                    v.wait_ge(S["aproj"], g + 1)
                    v.wait_ge(S["xb_r"], g + 1)
                    v.tensor_tensor(group_of(X, g), p_a, group_of(X, g), ALU.add).then_inc(S["x1_r"], 1)
                    settle(v, S["consts"])
                    v.wait_ge(S["x1_r"], g + 1)
                    at_least(v, S["rs2_r"], g)
                    stats(g, st2, mv2, "st2_r", "mv2_r")
                if w := groups(k, parity, -1):
                    g, b, _ = w
                    settle(v, S["consts"])
                    at_least(v, S["rs1_r"], g)
                    stats_x(g)
                if w := groups(k, parity, 4):
                    g, b, _ = w
                    v.wait_ge(S["route_mm"], g + 1)
                    v.tensor_copy(group_of(logits, g), p_route).then_inc(S["logits_r"], 1)
                if w := groups(k, parity, 1):
                    g, b, _ = w
                    at_least(v, S["msg_mm"], g - 1)
                    at_least(v, S["hg_m"], g - 1)
                    normal(g, h[:, b, :], mv2, rs2, "rs2_r", "h_r")
                if w := groups(k, parity, -1):
                    normal_x(w[0], w[1])

            run_steps(v, step)

            n = [0]

            def then(ins):
                n[0] += 1
                ins.then_inc(S["route"], 1)
                v.wait_ge(S["route"], n[0])

            def per_group(t):
                return t.rearrange("p (g o) -> p g o", o=1).to_broadcast([P, NG, E])

            def per_expert(t):
                return t.rearrange("p (o e) -> p o e", o=1).to_broadcast([P, NG, E])

            v.wait_ge(S["consts"], made_at["routing"])
            v.wait_ge(S["logits_r"], NG)
            then(v.tensor_reduce(per_token[:, 0, :], logits[:], AX.X, ALU.max))
            then(v.tensor_tensor(rt[0], logits[:], per_group(per_token[:, 0, :]), ALU.subtract))
            made_at["route_sub"] = n[0]
            v.wait_ge(S["route_exp"], 1)
            then(v.tensor_reduce(per_token[:, 1, :], rt[1], AX.X, ALU.add))
            then(v.reciprocal(per_token[:, 0, :], per_token[:, 1, :]))
            then(v.tensor_reduce(per_token[:, 2, :], rt[1], AX.X, ALU.max))
            then(v.tensor_tensor(p_max[:], per_token[:, 0, :], per_token[:, 2, :], ALU.mult))
            then(v.tensor_tensor(rt[0], rt[1], per_group(per_token[:, 2, :]), ALU.is_equal))
            then(v.tensor_tensor(rt[2], rt[0], per_expert(order_w[:]), ALU.mult))
            then(v.tensor_reduce(per_token[:, 0, :], rt[2], AX.X, ALU.max))
            then(v.tensor_tensor(onehot[:], rt[2], per_group(per_token[:, 0, :]), ALU.is_equal))
            then(v.tensor_reduce(starts[:], onehot[:].rearrange("p g e -> p e g"), AX.X, ALU.add))
            then(v.tensor_copy(cnt[:], starts[:]))
            made_at["onehot"] = n[0]
            v.wait_ge(S["rank_mm"], 1)
            then(v.tensor_scalar(blocks_i[:, 0, :], b7[:, 0:E], float(P - 1), None, ALU.add))
            then(v.tensor_scalar(blocks_i[:, 1, :], blocks_i[:, 0, :], 7, None, ALU.logical_shift_right))
            then(v.tensor_copy(blocks[:], blocks_i[:, 1, :]))
            then(v.tensor_tensor_scan(ends[:], one8[:], blocks[:], 0.0, ALU.mult, ALU.add))
            then(v.tensor_tensor(starts[:], ends[:], blocks[:], ALU.subtract))
            then(v.tensor_scalar(starts[:], starts[:], float(P), None, ALU.mult))
            then(v.tensor_tensor(rt[0], b6[:, 0:NG * E].rearrange("p (g e) -> p g e", g=NG),
                                 per_expert(starts[:]), ALU.add))
            then(v.tensor_tensor(rt[2], rt[0], onehot[:], ALU.mult))
            then(v.tensor_reduce(per_token[:, 1, :], rt[2], AX.X, ALU.add))
            v.tensor_copy(slot[:], per_token[:, 1, :]).then_inc(S["slot_r"], 1)
            then(v.tensor_tensor(past, blk[:].rearrange("p (n o) -> p n o", o=1).to_broadcast([P, NBLK, E]),
                                 ends[:].rearrange("p (o e) -> p o e", o=1).to_broadcast([P, NBLK, E]),
                                 ALU.is_ge))
            then(v.tensor_reduce(expert[:], past, AX.X, ALU.add))
            then(v.tensor_scalar(expert[:], expert[:], float(E - 1), None, ALU.min))
            v.tensor_copy(expert_i[:], expert[:]).then_inc(S["expert_r"], 1)

            def select(j, b):
                v.tensor_scalar(f_sel[:, b, :], row_e[:], expert[:, bass.ds(j, 1)], None, ALU.is_equal
                                ).then_inc(S["f_sel_r"], 1)

            def in_T(j, b):
                v.wait_ge(S["f_inT_tr"], j + 1)
                at_least(v, S["f_h_mm"], 2 * (j - 1))
                v.tensor_copy(f_inT[:, b, :], p_in[b]
                              ).then_inc(S["f_inT_cp"], 1)

            def expert_block(j, b, k):
                v.wait_ge(S["f_hT_tr"], 2 * j + 1)
                at_least(v, S["f_y_mm"], j)
                v.tensor_copy(f_hT[:, 0:512], pT[0][:]).then_inc(S["f_hT0_cp"], 1)
                if not isinstance(j, int) or j + 2 < NBLK:
                    in_T(j + 2, b)
                v.wait_ge(S["f_y_mm"], j + 1)
                at_least(v, f_y_st[b], 16 * k)
                v.tensor_copy(f_out[:, b, :], p_out[b]).then_inc(S["f_y_cp"], 1)
                if not isinstance(j, int) or j + 2 < NBLK:
                    select(j + 2, b)

            v.wait_ge(S["expert_r"], 1)
            select(0, 0)
            select(1, 1)
            in_T(0, 0)
            in_T(1, 1)
            run_blocks(v, expert_block)
            for g in range(NG):
                v.wait_ge(gathered[g // 2], 32)
                v.scalar_tensor_tensor(X[:, g, :], xn_all[:, g, :], p_max[:, g:g + 1], X[:, g, :],
                                       ALU.mult, ALU.add).then_inc(S["out_add"], 1)

        @block.scalar
        def _(act):
            act.dma_start(X[:, 0:2, :], x_v[:, 0:2, :]).then_inc(S["x_ld"], 16)
            act.dma_start(bk[:], col(a["L0_xattn_bk"]), allow_slow_non_contiguous=True).then_inc(S["wk_ld"], 16)
            act.dma_start(br[:], col(a["L0_xattn_br"]), allow_slow_non_contiguous=True).then_inc(S["wk_ld"], 16)
            act.dma_start(bq[:], col(a["L0_xattn_bq"]), allow_slow_non_contiguous=True).then_inc(S["w_ld"], 16)
            act.dma_start(Wqk[0:H, :], a["L0_attn_W_q"]).then_inc(S["w_ld"], 16)
            act.dma_start(Wqk[H:2 * H, :], a["L0_attn_W_k"]).then_inc(S["w_ld"], 16)
            act.dma_start(Wq[:], rows(a["L0_xattn_Wq"])).then_inc(S["w_ld"], 16)
            act.dma_start(bv[:], a["L0_xattn_bv"].partition_broadcast(P)).then_inc(S["w_ld"], 16)
            act.dma_start(gain, a["L0_attn_gain"].partition_broadcast(P)).then_inc(S["w_ld"], 16)
            act.dma_start(gbias[:], a["L0_attn_bias"].partition_broadcast(P)).then_inc(S["w_ld"], 16)
            act.dma_start(Wv[:], rows(a["L0_xattn_Wv"])).then_inc(S["w_ld"], 16)
            act.dma_start(Wroute[:], rows(a["L0_ffn_Wr"])).then_inc(S["w_ld"], 16)
            act.dma_start(logs[:, 0:1], a["L0_attn_log_mix"].partition_broadcast(P)).then_inc(S["logs_ld"], 16)
            act.dma_start(logs[:, 1:2], a["L0_attn_log_scale"].partition_broadcast(P)).then_inc(S["logs_ld"], 16)

            act.wait_ge(S["logs_ld"], 2 * 16)
            act.activation(sc[:, 0:1], logs[:, 0:1], ACT.Exp, scale=-1.0).then_inc(S["scal_act"], 1)
            act.activation(sc[:, 5:6], logs[:, 1:2], ACT.Abs).then_inc(S["scal_act"], 1)
            act.wait_ge(S["scal_act"], 2)
            act.activation(sc[:, 6:7], sc[:, 5:6], ACT.Exp, scale=-1.0).then_inc(S["scal_act"], 1)
            act.wait_ge(S["scal_act"], 3)
            act.activation(sc[:, 7:8], sc[:, 6:7], ACT.Ln, bias=1.0).then_inc(S["scal_act"], 1)
            act.wait_ge(S["last_fr"], 1)
            act.activation(khat_last[:], last_frac, ACT.Sin, scale=TWO_PI).then_inc(S["khat_last_r"], 1)

            def ctx_T_copy(g, half):
                act.wait_ge(S["ctxT_tr"], 4 * g + 2 * half + 2)
                at_least(act, S["kproj"], 4 * g + 2 * half - 2)
                act.copy(ctx_T[:, 1, half * 512:(half + 1) * 512], pT[1][:]).then_inc(S["ctxT1_cp"], 1)

            def turn(g, u):
                r = u % 2
                act.wait_ge(S["kproj"], 4 * g + u + 1)
                at_least(act, S["frac_r"], 4 * g + u - 1)
                act.activation(turns[r], pK[r][:], ACT.Identity, bias=bkr[:, r:r + 1]).then_inc(S["turns_r"], 1)

            def sine(g, b, u):
                half, r = u // 2, u % 2
                act.wait_ge(S["frac_r"], 4 * g + u + 1)
                at_least(act, S["scoresA"], g - 1)
                act.activation(khat[b][:, r, 2 * half:2 * half + 2, 0:CF], frac[r].rearrange("p (j n) -> p j n", j=2),
                               ACT.Sin, scale=TWO_PI).then_inc(S["khat_r"], 1)

            act.wait_ge(S["w_ld"], 16 * W_LOADS)
            act.wait_ge(S["bkr_cp"], 1)

            def step(k, parity):
                if w := groups(k, parity, 1):
                    g, b, _ = w
                    act.wait_ge(S["nmaxA_r"], g + 1)
                    at_least(act, S["pT_tr"], g)
                    at_least(act, S["plast_r"], g)
                    at_least(act, S["rsumA_r"], g)
                    act.activation(probs[:], p_score, ACT.Exp, bias=nmaxA[:, 0:1], accum_out=sumA[:]
                                   ).then_inc(S["probsA"], 1)
                if w := groups(k, parity, 0):
                    ctx_T_copy(w[0], 0)
                if w := groups(k, parity, 2):
                    g, b, _ = w
                    act.wait_ge(S["hT_tr"], g + 1)
                    at_least(act, S["qk_mm"], g)
                    act.copy(hT[:].rearrange("p c n -> p (c n)"), p_hT).then_inc(S["hT_cp"], 1)
                if w := groups(k, parity, 3):
                    g, b, _ = w
                    act.wait_ge(S["nmaxB_r"], g + 1)
                    at_least(act, S["att_r"], g)
                    act.activation(expB[:], scoreB[:, b, :], ACT.Exp, bias=nmaxB[:, b:b + 1], accum_out=sumB[:]
                                   ).then_inc(S["probsB"], 1)
                if w := groups(k, parity, 4):
                    g, b, _ = w
                    act.wait_ge(S["y_r"], g + 1)
                    at_least(act, S["x2_r"], g)
                    act.activation(gel[:], y[:], ACT.Gelu).then_inc(S["gelu_r"], 1)
                if w := groups(k, parity, 0):
                    turn(w[0], 0)
                    turn(w[0], 1)
                if w := groups(k, parity, 2):
                    g, b, _ = w
                    act.wait_ge(S["qk_mm"], g + 1)
                    at_least(act, S["scoreB_mm"], g)
                    act.mul(qB[:], p_qk[0:H, :], float(H ** -0.5)).then_inc(S["qk_cp"], 1)
                    act.copy(kB[:], p_qk[H:2 * H, :]).then_inc(S["qk_cp"], 1)
                if w := groups(k, parity, 0):
                    g, b, _ = w
                    sine(g, b, 0)
                    sine(g, b, 1)
                    ctx_T_copy(g, 1)
                    act.wait_ge(S["qproj"], g + 1)
                    at_least(act, S["scoresA"], g)
                    for c in range(DC):
                        act.activation(qT[:, c, :], p_q[:, c * P:(c + 1) * P], ACT.Identity, bias=bq[:, c:c + 1]
                                       ).then_inc(S["q_r"], 1)
                    turn(g, 2)
                    turn(g, 3)
                    sine(g, b, 2)
                    sine(g, b, 3)
                if w := groups(k, parity, 4):
                    g, b, _ = w
                    act.wait_ge(S["xn3T_tr"], g + 1)
                    at_least(act, S["route_mm"], g)
                    act.copy(xn3T[:].rearrange("p c n -> p (c n)"), p_xn3T).then_inc(S["xn3T_cp"], 1)

            run_steps(act, step)

            act.wait_ge(S["route"], made_at["route_sub"])
            act.activation(rt[1], rt[0], ACT.Exp).then_inc(S["route_exp"], 1)

            def gelus(j):
                at_least(act, S["f_hT_tr"], 2 * j)
                for i in range(2):
                    act.wait_ge(S["f_h_mm"], 2 * j + i + 1)
                    act.activation(f_h[:, i * 512:(i + 1) * 512], pK[i][:], ACT.Gelu).then_inc(S["f_gelu"], 1)

            def store_result(j, b):
                act.wait_ge(S["f_y_cp"], j + 1)
                act.dma_start(ys_dram[bass.ds(j * P, P), :], f_out[:, b, :]).then_inc(f_y_st[b], 16)

            def expert_block(j, b, k):
                act.wait_ge(S["f_hT_tr"], 2 * j + 2)
                at_least(act, S["f_y_mm"], j)
                act.copy(f_hT[:, 512:1024], pT[1][:]).then_inc(S["f_hT1_cp"], 1)
                if not isinstance(j, int) or j > 0:
                    store_result(j - 1, 1 - b)
                if not isinstance(j, int) or j + 1 < NBLK:
                    gelus(j + 1)

            gelus(0)
            run_blocks(act, expert_block)
            store_result(NBLK - 1, (NBLK - 1) % 2)

        @block.tensor
        def _(pe):
            def transposed(dst, src, done=None):
                k = src.shape[0]
                ins = pe.transpose(dst, src, ident[0:k, 0:k])
                if done:
                    ins.then_inc(S[done], 1)

            pe.wait_ge(S["consts"], made_at["ident"])
            pe.wait_ge(S["wk_ld"], 64)
            for ec in range(DC):
                for dc in range(DC):
                    transposed(pT[0][:, (ec * DC + dc) * P:(ec * DC + dc + 1) * P], Wk[:, dc, ec * P:(ec + 1) * P],
                               "wkT_tr" if (ec, dc) == (DC - 1, DC - 1) else None)
            pe.wait_ge(S["wkT_cp"], 1)
            for dc in range(DC):
                for ec in range(DC):
                    mm = pe.matmul(pK[0][:, dc * D:(dc + 1) * D], WkT[:, ec, dc * P:(dc + 1) * P], Wr[:, ec, :],
                                   start=ec == 0, stop=ec == DC - 1)
            mm.then_inc(S["wkr_mm"], 1)
            for r in range(DC):
                for ec in range(DC):
                    mm = pe.matmul(b4[:, r:r + 1], Wr[:, ec, r * P:(r + 1) * P], bk[:, ec:ec + 1],
                                   start=ec == 0, stop=ec == DC - 1)
            mm.then_inc(S["bkr_mm"], 1)
            pe.wait_ge(S["w_ld"], 16 * W_LOADS)
            for c in range(DC):
                transposed(b5[:, c * 2 * H:(c + 1) * 2 * H], Wqk[:, c * P:(c + 1) * P],
                           "wqkT_tr" if c == DC - 1 else None)
            pe.wait_ge(S["last_ld"], 16)
            for c in range(DC):
                transposed(b7[:, c * B:(c + 1) * B], last_rows[:, c * P:(c + 1) * P],
                           "lastT_tr" if c == DC - 1 else None)
            pe.wait_ge(S["wkr_cp"], 1)
            pe.wait_ge(S["lastT_cp"], 1)
            for r in range(DC):
                for c in range(DC):
                    mm = pe.matmul(b6[:, r * B:(r + 1) * B], Wkr[:, c, r * P:(r + 1) * P], last_T[:, c, :],
                                   start=c == 0, stop=c == DC - 1)
            mm.then_inc(S["lastK_mm"], 1)
            pe.wait_ge(S["bkr_cp"], 1)
            pe.wait_ge(S["wqkT_cp"], 1)
            pe.wait_ge(S["last_turn"], 2)

            def ctx_transposes(g, b, q, half):
                pe.wait_ge(ctx_ld[b], 16 * CTX_LOADS * (q + 1))
                for c in range(DC):
                    at_least(pe, S["ctxT0_cp" if c == 0 else "ctxT1_cp"], 2 * g + half)
                    for i in range(4):
                        src = ctx_rows[b][:, 2 * half + i // 2, i % 2, c * P:(c + 1) * P]
                        transposed(pT[c][:, i * P:(i + 1) * P], src, "ctxT_tr" if i == 3 else None)

            def ctx_project(g, half):
                pe.wait_ge(S["ctxT0_cp"], 2 * g + half + 1)
                pe.wait_ge(S["ctxT1_cp"], 2 * g + half + 1)
                for r in range(DC):
                    at_least(pe, S["turns_r"], 4 * g + 2 * half + r - 1)
                    for c in range(DC):
                        mm = pe.matmul(pK[r][:], Wkr[:, c, r * P:(r + 1) * P],
                                       ctx_T[:, c, half * 512:(half + 1) * 512], start=c == 0, stop=c == DC - 1)
                    mm.then_inc(S["kproj"], 1)

            def step(k, parity):
                if w := groups(k, parity, 1):
                    g, b, _ = w
                    pe.wait_ge(S["khat_r"], 4 * g + 4)
                    pe.wait_ge(S["klast_r"], g + 1)
                    pe.wait_ge(S["q_r"], 2 * g + 2)
                    at_least(pe, S["oT_cp"], g)
                    at_least(pe, S["attT_cp"], g - 2)
                    for r in range(DC):
                        for j in range(BG):
                            mm = pe.matmul(p_score[j * T:(j + 1) * T, :], qT[:, r, j * T:(j + 1) * T],
                                           khat[b][:, r, j, :], start=r == 0, stop=r == DC - 1,
                                           skip_group_check=True)
                    mm.then_inc(S["scoresA"], 1)
                if w := groups(k, parity, 0):
                    g, b, q = w
                    ctx_transposes(g, b, q, 0)
                    pe.wait_ge(S["xn_r"], g + 1)
                    at_least(pe, S["selected"], g - 2)
                    at_least(pe, S["ymsg_r"], g - 3)
                    for c in range(DC):
                        transposed(p_xnT[:, c * P:(c + 1) * P], xn[:, b, c * P:(c + 1) * P],
                                   "xnT_tr" if c == DC - 1 else None)
                if w := groups(k, parity, 2):
                    g, b, _ = w
                    pe.wait_ge(S["h_r"], g + 1)
                    pe.wait_ge(S["x1_r"], g + 1)
                    for c in range(DC):
                        transposed(p_hT[:, c * P:(c + 1) * P], h[:, b, c * P:(c + 1) * P],
                                   "hT_tr" if c == DC - 1 else None)
                if w := groups(k, parity, 0):
                    ctx_project(w[0], 0)
                if w := groups(k, parity, 1):
                    g, b, _ = w
                    pe.wait_ge(S["probsA"], g + 1)
                    pe.wait_ge(S["plast_r"], g + 1)
                    for c in range(CC):
                        transposed(p_pT[:, c * P:(c + 1) * P], probs[:, c * P:(c + 1) * P])
                    transposed(p_plT, p_last[:], "pT_tr")
                if w := groups(k, parity, 2):
                    g, b, _ = w
                    pe.wait_ge(S["hT_cp"], g + 1)
                    at_least(pe, S["xnT_cp"], upto(g + 3, NG))
                    at_least(pe, S["ymsg_r"], g - 1)
                    for c in range(DC):
                        mm = pe.matmul(p_sim, hT[:, c, :], hT[:, c, :], start=c == 0, stop=c == DC - 1)
                    mm.then_inc(S["sim_mm"], 1)
                    for c in range(DC):
                        mm = pe.matmul(p_qk, WqkT[:, c, :], hT[:, c, :], start=c == 0, stop=c == DC - 1)
                    mm.then_inc(S["qk_mm"], 1)
                if w := groups(k, parity, 0):
                    g, b, q = w
                    ctx_transposes(g, b, q, 1)
                if w := groups(k, parity, 1):
                    g, b, _ = w
                    pe.wait_ge(S["pT_cp"], 2 * g + 2)
                    at_least(pe, S["o_r"], g)
                    at_least(pe, S["logits_r"], g - 3)
                    for c in range(CC):
                        for j in range(BG):
                            pe.matmul(p_o[j * T:(j + 1) * T, :], probsT[:, c, j * T:(j + 1) * T],
                                      ctx_rows[b][:, j, c, :], start=c == 0, stop=False, skip_group_check=True)
                    pe.matmul(p_o, p_lastT[:], ctx_last[:, b, :], start=False, stop=True, skip_group_check=True
                              ).then_inc(S["pv"], 1)
                if w := groups(k, parity, 3):
                    g, b, _ = w
                    pe.wait_ge(S["att_r"], g + 1)
                    at_least(pe, S["pT_cp"], upto(2 * g + 6, 2 * NG))
                    at_least(pe, S["oT_cp"], upto(g + 2, NG))
                    transposed(p_attT, att[:], "attT_tr")
                if w := groups(k, parity, 2):
                    g, b, _ = w
                    pe.wait_ge(S["qk_cp"], 2 * g + 2)
                    pe.wait_ge(S["simm_r"], g + 1)
                    pe.matmul(p_scoreB, qB[:], kB[:], start=True, stop=True).then_inc(S["scoreB_mm"], 1)
                if w := groups(k, parity, 0):
                    g, b, _ = w
                    pe.wait_ge(S["xnT_cp"], g + 1)
                    at_least(pe, S["qk_cp"], 2 * g - 2)
                    at_least(pe, S["x1_r"], g - 1)
                    for r in range(DC):
                        for c in range(DC):
                            mm = pe.matmul(p_q[:, r * P:(r + 1) * P], Wq[:, c, r * P:(r + 1) * P], xnT[:, c, :],
                                           start=c == 0, stop=c == DC - 1)
                    mm.then_inc(S["qproj"], 1)
                    ctx_project(g, 1)
                if w := groups(k, parity, 1):
                    g, b, _ = w
                    pe.wait_ge(S["o_r"], g + 1)
                    at_least(pe, S["attT_cp"], g - 1)
                    for c in range(DC):
                        transposed(p_oT[:, c * P:(c + 1) * P], o_norm[:, c * P:(c + 1) * P],
                                   "oT_tr" if c == DC - 1 else None)
                if w := groups(k, parity, 3):
                    g, b, _ = w
                    pe.wait_ge(S["attT_cp"], g + 1)
                    at_least(pe, S["selected"], upto(g + 2, NG))
                    pe.matmul(p_msg, attT[:], h[:, b, :], start=True, stop=True).then_inc(S["msg_mm"], 1)
                if w := groups(k, parity, 1):
                    g, b, _ = w
                    pe.wait_ge(S["oT_cp"], g + 1)
                    at_least(pe, S["q_r"], upto(2 * g + 4, 2 * NG))
                    at_least(pe, S["qk_cp"], 2 * g)
                    for c in range(DC):
                        mm = pe.matmul(p_a, o_T[:, c, :], Wv[:, c, :], start=c == 0, stop=c == DC - 1)
                    mm.then_inc(S["aproj"], 1)
                if w := groups(k, parity, 4):
                    g, b, _ = w
                    pe.wait_ge(S["xn3_r"], g + 1)
                    at_least(pe, S["o_r"], upto(g + 4, NG))
                    at_least(pe, S["logits_r"], g)
                    for c in range(DC):
                        transposed(p_xn3T[:, c * P:(c + 1) * P], xn3[:, b, c * P:(c + 1) * P],
                                   "xn3T_tr" if c == DC - 1 else None)
                    pe.wait_ge(S["xn3T_cp"], g + 1)
                    for c in range(DC):
                        mm = pe.matmul(p_route, xn3T[:, c, :], Wroute[:, c, :], start=c == 0, stop=c == DC - 1)
                    mm.then_inc(S["route_mm"], 1)

            run_steps(pe, step)

            pe.wait_ge(S["route"], made_at["onehot"])
            pe.matmul(b6[:, 0:NG * E], tri[:], onehot[:].rearrange("p g e -> p (g e)"), start=True, stop=False,
                      skip_group_check=True)
            for g in range(NG - 1):
                later = NG - 1 - g
                pe.matmul(b6[:, (g + 1) * E:NG * E], ones[:],
                          onehot[:, g:g + 1, :].to_broadcast([P, later, E]), start=False, stop=g == NG - 2,
                          skip_group_check=True)
            pe.matmul(b7[:, 0:E], ones[:], cnt[:], start=True, stop=True).then_inc(S["rank_mm"], 1)

            def in_T(j, b, k):
                pe.wait_ge(f_in_ld[b], 16 * (k + 1))
                if isinstance(j, int) and j == 0:
                    pe.wait_ge(S["expert_r"], 1)
                at_least(pe, S["f_inT_cp"], j - 1)
                for c in range(DC):
                    transposed(p_in[b][:, c * P:(c + 1) * P], f_in[:, b, c * P:(c + 1) * P],
                               "f_inT_tr" if c == DC - 1 else None)

            def expert_of(j):
                return pe.value_load(expert_i[0:1, bass.ds(j, 1)], min_val=0, max_val=E - 1)

            def up(j, b, e):
                pe.wait_ge(S["f_inT_cp"], j + 1)
                pe.wait_ge(S["f_sel_r"], j + 1)
                for i in range(2):
                    at_least(pe, S["f_gelu"], 2 * (j - 1) + i + 1)
                    pe.matmul(pK[i][:], f_sel[:, b, :], b_parts[:, i * 512:(i + 1) * 512], start=True, stop=False)
                    for c in range(DC):
                        mm = pe.matmul(pK[i][:], f_inT[:, b, c * P:(c + 1) * P],
                                       W1[:, bass.ds(e, 1), c, i * 512:(i + 1) * 512].rearrange("p o n -> p (o n)"),
                                       start=False, stop=c == DC - 1)
                    mm.then_inc(S["f_h_mm"], 1)

            def expert_block(j, b, k):
                more = not isinstance(j, int)
                e = expert_of(j)
                if more or j + 1 < NBLK:
                    e_next = expert_of(j + 1)
                for i in range(2):
                    pe.wait_ge(S["f_gelu"], 2 * j + i + 1)
                    at_least(pe, S[f"f_hT{i}_cp"], j)
                    for c in range(4):
                        n = 4 * i + c
                        transposed(pT[i][:, c * P:(c + 1) * P], f_h[:, n * P:(n + 1) * P],
                                   "f_hT_tr" if c == 3 else None)
                if more or j + 2 < NBLK:
                    in_T(j + 2, b, k + 1)
                if more or j + 1 < NBLK:
                    up(j + 1, 1 - b, e_next)
                pe.wait_ge(S["f_hT0_cp"], j + 1)
                pe.wait_ge(S["f_hT1_cp"], j + 1)
                if not more and j == 0:
                    pe.wait_ge(S["w2_ld"], 16 * E)
                at_least(pe, S["f_y_cp"], j)
                acc = p_out[b]
                pe.matmul(acc, f_sel[:, b, :], b_parts[:, F:F + D], start=True, stop=False)
                for c in range(FC):
                    mm = pe.matmul(acc, f_hT[:, c * P:(c + 1) * P],
                                   w2[:, bass.ds(e, 1), c, :].rearrange("p o n -> p (o n)"),
                                   start=False, stop=c == FC - 1)
                mm.then_inc(S["f_y_mm"], 1)

            in_T(0, 0, 0)
            in_T(1, 1, 0)
            pe.wait_ge(S["w1_ld"], 16 * E)
            pe.wait_ge(S["bparts"], 3)
            up(0, 0, expert_of(0))
            run_blocks(pe, expert_block)


_INS = ["x", "ctx_1024", "L0_xattn_Wq", "L0_xattn_bq", "L0_xattn_Wk", "L0_xattn_bk", "L0_xattn_Wv", "L0_xattn_bv",
        "L0_xattn_Wr", "L0_xattn_br", "L0_attn_W_q", "L0_attn_W_k", "L0_attn_gain", "L0_attn_bias",
        "L0_attn_log_mix", "L0_attn_log_scale", "L0_ffn_Wr", "L0_ffn_W1", "L0_ffn_b1", "L0_ffn_W2", "L0_ffn_b2"]


def kernel(**inputs):
    import numpy as _np
    import concourse.bacc as _bacc
    from concourse import mybir as _mybir
    from concourse.bass_utils import run_bass_kernel_spmd as _run

    nc = _bacc.Bacc("TRN2", target_bir_lowering=False, num_devices=1)
    arrays, args = {}, {}
    for name in _INS:
        v = _np.ascontiguousarray(inputs[name])
        if not v.shape:
            v = v.reshape(1)
        arrays[f"in_{name}_dram"] = v
        args[name] = nc.dram_tensor(f"in_{name}_dram", v.shape, _mybir.dt.from_np(v.dtype), kind="ExternalInput").ap()
    o = nc.dram_tensor("out_0_dram", (B, T, D), F32, kind="ExternalOutput").ap()
    perceiver_layer(nc, args, o)
    r = _run(nc, [arrays], core_ids=[0])
    return r.results[0]["out_0_dram"]
```

```python
from contextlib import ExitStack

import numpy as np

import concourse.bass as bass
from concourse import mybir

F32 = mybir.dt.float32
BF16 = mybir.dt.bfloat16
I32 = mybir.dt.int32
ALU = mybir.AluOpType
ACT = mybir.ActivationFunctionType
AX = mybir.AxisListType

B, T, D, C = 64, 32, 256, 257
P = 128
DC = D // P
TOK = B * T
NG = TOK // P
BG = P // T
CF = C - 1
CC = CF // P
E, F = 8, 1024
FC = F // P
H = 32
NBLK = TOK // P + E - 1
SLOTS = NBLK * P
TOP = 8

EPS = 1e-5
INV_2PI = float(1.0 / (2.0 * np.pi))
TWO_PI = 6.283185
ROUND = float(3 << 22)
LOWEST = -3.4028234663852886e38
PICKED = 3.0e38
UNPICKED = -1.0e9
OUTSIDE = -3.0e38

STAGES = 5
PEELED = 6


def at_least(eng, sem, count):
    if not isinstance(count, int) or count > 0:
        eng.wait_ge(sem, count)


def settle(eng, sem):
    eng.wait_ge(sem, 1)


def in_register(eng, count):
    return count if isinstance(count, int) else eng.to_reg(count)


def upto(value, most):
    return min(value, most) if isinstance(value, int) else value


def groups(k, parity, behind):
    g = 2 * k + parity - behind
    if isinstance(g, int) and not 0 <= g < NG:
        return None
    return g, (parity - behind) % 2, k + (parity - behind) // 2


def run_steps(eng, step):
    for s in range(PEELED):
        step(s // 2, s % 2)
    with eng.Fori(PEELED // 2, NG // 2 - 1) as k:
        step(k, 0)
        step(k, 1)
    for s in range(NG - 2, NG + STAGES - 1):
        step(s // 2, s % 2)


def run_blocks(eng, step):
    for j in range(2):
        step(j, j, 0)
    with eng.Fori(1, (NBLK - 3) // 2) as k:
        step(2 * k, 0, k)
        step(2 * k + 1, 1, k)
    for j in range(NBLK - 3, NBLK):
        step(j, j % 2, j // 2)


def perceiver_layer(nc, a, out):
    ctx = ExitStack()
    with ctx:
        def sb(name, shape, dt=F32):
            return ctx.enter_context(nc.sbuf_tensor(name, shape, dt))

        def ps(name):
            return ctx.enter_context(nc.psum_tensor(name, [P, 512], F32))

        def sem(name):
            return ctx.enter_context(nc.semaphore(name))

        xs_dram = nc.dram_tensor("sorted_tokens", [SLOTS, D], F32, kind="Internal").ap()
        ys_dram = nc.dram_tensor("sorted_results", [SLOTS, D], F32, kind="Internal").ap()

        X = sb("X", [P, NG, D])
        XN = sb("XN", [P, NG * D])
        xn_all = XN[:, :].rearrange("p (g d) -> p g d", g=NG)
        spare = XN[:, (NG - 4) * D:]
        W1 = sb("W1", [P, E, DC, F])
        W2 = sb("W2", [P, E * FC * D])
        w2 = W2[:, :].rearrange("p (e c d) -> p e c d", e=E, c=FC)
        used = [0]

        def room(n):
            used[0] += n
            assert used[0] <= E * FC * D
            return W2[:, used[0] - n:used[0]]

        ctx_rows = [room(BG * CC * D).rearrange("p (j c d) -> p j c d", j=BG, c=CC) for _ in range(2)]
        ctx_T = room(DC * BG * CF).rearrange("p (c n) -> p c n", c=DC)
        khat = [room(DC * BG * C).rearrange("p (r j n) -> p r j n", r=DC, j=BG) for _ in range(2)]
        turns = [room(512) for _ in range(2)]
        frac = [room(512) for _ in range(2)]
        bias_rows = room(F + D)
        ctx_last = sb("ctx_last", [BG, 2, D])

        ident = sb("ident", [P, P])
        tri = sb("tri", [P, P], BF16)
        ones = sb("ones", [P, P], BF16)
        own_batch = sb("own_batch", [P, BG])
        causal = sb("causal", [P, P])
        pickable = sb("pickable", [P, P])
        unpicked = sb("unpicked", [P, P])
        zeros = sb("zeros", [P, D])
        minus_half = sb("minus_half", [P, 1])

        Wk, WkT, Wr = (room(DC * D).rearrange("p (c n) -> p c n", c=DC) for _ in range(3))
        Wkr = sb("Wkr", [P, DC, D])
        Wq = sb("Wq", [P, DC, D])
        Wv = sb("Wv", [P, DC, D])
        bq = sb("bq", [P, DC])
        bk = sb("bk", [P, DC])
        br = sb("br", [P, DC])
        bkr = sb("bkr", [P, DC])
        bv = sb("bv", [P, D])
        Wqk = sb("Wqk", [2 * H, D])
        WqkT = sb("WqkT", [P, DC, 2 * H])
        Wroute = sb("Wroute", [P, DC, E])
        gain = spare[:, 0:D]
        gbias = sb("gbias", [P, D])
        gain_msg = sb("gain_msg", [P, D])
        gain_self = sb("gain_self", [P, D])
        logs = sb("logs", [P, 2])
        sc = sb("sc", [P, 12])
        b_parts = sb("b_parts", [P, F + D], BF16)
        last_rows = spare[0:B, D:2 * D]
        last_T, last_turns, last_frac = (spare[:, 2 * D + i * P:2 * D + (i + 1) * P].rearrange("p (c n) -> p c n", c=DC)
                                         for i in range(3))
        khat_last = sb("khat_last", [P, DC, B])

        st1, st2, st3 = (sb(f"st{i}", [P, 6]) for i in (1, 2, 3))
        mv1, mv2, mv3 = (sb(f"mv{i}", [P, 2]) for i in (1, 2, 3))
        ve1, ve2, ve3 = (sb(f"ve{i}", [P, 1]) for i in (1, 2, 3))
        rs1, rs2, rs3 = (sb(f"rs{i}", [P, 1]) for i in (1, 2, 3))
        xn = sb("xn", [P, 2, D])
        xn3 = sb("xn3", [P, 2, D])
        xnT = sb("xnT", [P, DC, P])
        qT = sb("qT", [P, DC, P])
        nmaxA = sb("nmaxA", [P, 1])
        sumA = sb("sumA", [P, 1])
        rsumA = sb("rsumA", [P, 1])
        probs = sb("probs", [P, C])
        p_last = sb("p_last", [P, BG])
        probsT = sb("probsT", [P, CC, P])
        p_lastT = sb("p_lastT", [BG, P])
        o_norm = sb("o_norm", [P, D])
        o_T = sb("o_T", [P, DC, P])
        h = sb("h", [P, 2, D])
        hg = sb("hg", [P, 2, D])
        hT = sb("hT", [P, DC, P])
        qB = sb("qB", [H, P])
        kB = sb("kB", [H, P])
        simm = sb("simm", [P, P])
        top8 = sb("top8", [P, TOP])
        marked = sb("marked", [P, P])
        pick = sb("pick", [P, P], I32)
        scoreB = sb("scoreB", [P, 2, P])
        nmaxB = sb("nmaxB", [P, 2])
        expB = sb("expB", [P, P])
        sumB = sb("sumB", [P, 1])
        rsumB = sb("rsumB", [P, 1])
        att = sb("att", [P, P])
        attT = sb("attT", [P, P])
        y_msg = sb("y_msg", [P, D])
        y = sb("y", [P, D])
        gel = sb("gel", [P, D])
        xn3T = sb("xn3T", [P, DC, P])

        logits = sb("logits", [P, NG, E])
        rt = [t.rearrange("p (g e) -> p g e", g=NG) for t in (y_msg[:, 0:P], y_msg[:, P:2 * P], y[:, 0:P])]
        onehot = sb("onehot", [P, NG, E], BF16)
        per_token = sb("per_token", [P, 3, NG])
        p_max = sb("p_max", [P, NG])
        slot = sb("slot", [P, NG], I32)
        order_w = sb("order_w", [P, E])
        order_i = sb("order_i", [P, E], I32)
        cnt = sb("cnt", [P, E], BF16)
        blocks_i = sb("blocks_i", [P, 2, E], I32)
        blocks = sb("blocks", [P, E])
        ends = sb("ends", [P, E])
        starts = sb("starts", [P, E])
        one8 = sb("one8", [P, E])
        blk_i = sb("blk_i", [P, NBLK], I32)
        blk = sb("blk", [P, NBLK])
        past = gel[:, 0:NBLK * E].rearrange("p (n e) -> p n e", n=NBLK)
        expert = sb("expert", [P, NBLK])
        expert_i = sb("expert_i", [P, NBLK], I32)
        row_i = spare[:, 2 * D + 3 * P:2 * D + 4 * P].bitcast(I32)
        row_e = sb("row_e", [P, P])
        f_sel = simm[:].bitcast(BF16).rearrange("p (b n) -> p b n", b=2)
        f_h = XN[:, 0:F]
        f_hT = XN[:, F:2 * F]
        f_in, f_inT, f_out = (XN[:, 2 * F + 2 * i * D:2 * F + 2 * (i + 1) * D].rearrange("p (b n) -> p b n", b=2)
                              for i in range(3))

        pT = [ps("pT0"), ps("pT1")]
        pK = [ps("pK0"), ps("pK1")]
        b4, b5, b6, b7 = ps("b4"), ps("b5"), ps("b6"), ps("b7")
        p_score = b4[:, 0:C]
        p_pT = b4[:, 0:CF]
        p_plT = b4[0:BG, CF:CF + P]
        p_attT = b4[:, 0:P]
        p_oT = b4[:, 0:D]
        p_xnT = b5[:, 0:D]
        p_sim = b5[:, 0:P]
        p_scoreB = b5[:, 0:P]
        p_msg = b5[:, 0:D]
        p_hT = b6[:, 0:D]
        p_qk = b6[0:2 * H, 0:P]
        p_q = b6[:, 0:D]
        p_a = b6[:, 0:D]
        p_o = b7[:, 0:D]
        p_xn3T = b7[:, 0:D]
        p_route = b7[:, 0:E]
        p_in = (b6[:, 0:D], b7[:, 0:D])
        p_out = (b4[:, 0:D], b5[:, 0:D])

        names = """consts wk_ld w_ld x_ld xrest_ld last_ld bias_ld logs_ld xs_zero w1_ld w2_ld
            wkT_tr wkT_cp wkr_mm wkr_cp wqkT_tr wqkT_cp bkr_mm bkr_sum bkr_cp lastT_tr lastT_cp lastK_mm
            last_turn last_whole last_fr khat_last_r scal_act scal_dve gains bias_split
            ctxT_tr ctxT0_cp ctxT1_cp kproj turns_r whole_r frac_r khat_r klast_r
            st1_r mv1_r ve1_r rs1_r xn_r xb_r xnT_tr xnT_cp qproj q_r
            scoresA nmaxA_r probsA rsumA_r plast_r pT_tr pT_cp pv o_r oT_tr oT_cp aproj x1_r
            st2_r mv2_r ve2_r rs2_r h_r hg_m hg_r hT_tr hT_cp sim_mm qk_mm qk_cp
            simm_r top_r marked_r pick_r base_r scoreB_mm selected nmaxB_r
            probsB rsumB_r att_r attT_tr attT_cp msg_mm ymsg_r y_r gelu_r x2_r
            st3_r mv3_r ve3_r rs3_r xn3_r xn3_kept xn3T_tr xn3T_cp route_mm logits_r
            route route_exp rank_mm slot_r expert_r scattered
            f_sel_r f_inT_tr f_inT_cp f_h_mm f_gelu f_hT_tr f_hT0_cp f_hT1_cp f_y_mm f_y_cp
            out_add stored""".split()
        S = {n: sem(n) for n in names}
        ctx_ld = [sem("ctx_ld0"), sem("ctx_ld1")]
        f_in_ld = [sem("f_in_ld0"), sem("f_in_ld1")]
        f_y_st = [sem("f_y_st0"), sem("f_y_st1")]
        gathered = [sem(f"gathered{i}") for i in range(NG // 2)]

        block = ctx.enter_context(nc.Block())
        CTX_LOADS = CC + 1
        W_LOADS = 9
        made_at = {}

        x_v = a["x"].rearrange("(g j) t d -> (j t) g d", j=BG)
        out_v = out.rearrange("(g j) t d -> (j t) g d", j=BG)
        c_in = a["ctx_1024"]

        def col(v):
            return v.rearrange("(c p) -> p c", p=P)

        def rows(w):
            return w.rearrange("(c p) n -> p c n", p=P)

        def group_of(t, g):
            return t[:, bass.ds(g, 1), :].rearrange("p o d -> p (o d)")

        @block.gpsimd
        def _(pool):
            n = [0]

            def made(ins):
                n[0] += 1
                ins.then_inc(S["consts"], 1)
                pool.wait_ge(S["consts"], n[0])

            def keep(t, pattern, base, mult, cmp, fill):
                made(pool.affine_select(t, t, pattern, cmp, fill, base=base, channel_multiplier=mult))

            def rstd(g, mv, ve, rs, mv_r, ve_r, rs_r):
                count = in_register(pool, g + 1)
                settle(pool, S["consts"])
                pool.wait_ge(S[mv_r], count)
                pool.tensor_scalar(ve[:], mv[:, 1:2], EPS, None, ALU.add).then_inc(S[ve_r], 1)
                pool.wait_ge(S[ve_r], g + 1)
                pool.tensor_tensor(rs[:], ve[:], minus_half[:], ALU.pow).then_inc(S[rs_r], 1)

            def add_bv(g):
                pool.wait_ge(S["xn_r"], g + 1)
                pool.tensor_tensor(group_of(X, g), group_of(X, g), bv[:], ALU.add).then_inc(S["xb_r"], 1)

            made(pool.memset(ident[:], 0.0))
            keep(ident[:], [[-1, P]], 0, 1, ALU.not_equal, 1.0)
            made_at["ident"] = n[0]
            made(pool.memset(minus_half[:], -0.5))
            made(pool.memset(zeros[:], 0.0))
            made_at["zeros"] = n[0]
            made(pool.memset(bias_rows, 0.0))
            made_at["bias_rows"] = n[0]
            pool.wait_ge(S["w_ld"], 16 * W_LOADS)
            rstd(0, mv1, ve1, rs1, "mv1_r", "ve1_r", "rs1_r")
            add_bv(0)

            made(pool.memset(own_batch[:], 1.0))
            keep(own_batch[:], [[-T, BG]], 0, 1, ALU.is_ge, 0.0)
            keep(own_batch[:], [[T, BG]], T - 1, -1, ALU.is_ge, 0.0)
            made_at["own_batch"] = n[0]
            pool.wait_ge(S["scal_dve"], 3)
            pool.tensor_scalar(gain_msg[:], gain, sc[:, 3:4], None, ALU.mult).then_inc(S["gains"], 1)
            pool.tensor_scalar(gain_self[:], gain, sc[:, 2:3], None, ALU.mult).then_inc(S["gains"], 1)
            for t, start, fill in ((causal, 0.0, LOWEST), (pickable, PICKED, 1.0), (unpicked, UNPICKED, OUTSIDE)):
                v = t[:].rearrange("p (j n) -> p j n", j=BG)
                made(pool.memset(t[:], start))
                keep(v, [[-T, BG], [0, T]], 0, 1, ALU.is_ge, fill)
                keep(v, [[T, BG], [0, T]], T - 1, -1, ALU.is_ge, fill)
                if t is not unpicked:
                    keep(v, [[-T, BG], [-1, T]], 0, 1, ALU.is_gt, fill)
            made_at["masks"] = n[0]
            pool.wait_ge(S["gains"], 2)

            def step(k, parity):
                now, one, two, three, four, coming = (groups(k, parity, n) for n in (0, 1, 2, 3, 4, -1))
                if now:
                    g, b, _ = now
                    if isinstance(g, int) and g == 0:
                        pool.wait_ge(S["khat_last_r"], 1)
                    settle(pool, S["consts"])
                    at_least(pool, S["scoresA"], g - 1)
                    pool.tensor_copy(khat[b][:, :, :, CF], khat_last[:, :, bass.ds(g * BG, BG)]
                                     ).then_inc(S["klast_r"], 1)
                if two:
                    g, b, _ = two
                    count = in_register(pool, g - 1)
                    settle(pool, S["consts"])
                    at_least(pool, S["probsB"], count)
                    pool.tensor_copy(scoreB[:, b, :], unpicked[:]).then_inc(S["base_r"], 1)
                if coming:
                    rstd(coming[0], mv1, ve1, rs1, "mv1_r", "ve1_r", "rs1_r")
                if four:
                    rstd(four[0], mv3, ve3, rs3, "mv3_r", "ve3_r", "rs3_r")
                if coming:
                    add_bv(coming[0])
                if four:
                    g, b, _ = four
                    settle(pool, S["consts"])
                    pool.wait_ge(S["xn3_r"], g + 1)
                    pool.tensor_copy(group_of(xn_all, g), xn3[:, b, :]).then_inc(S["xn3_kept"], 1)
                if one:
                    g, b, _ = one
                    rstd(g, mv2, ve2, rs2, "mv2_r", "ve2_r", "rs2_r")
                    pool.wait_ge(S["h_r"], g + 1)
                    at_least(pool, S["y_r"], g - 1)
                    pool.tensor_tensor(hg[:, b, :], h[:, b, :], gain_self[:], ALU.mult).then_inc(S["hg_m"], 1)
                    pool.wait_ge(S["hg_m"], g + 1)
                    pool.tensor_tensor(hg[:, b, :], hg[:, b, :], gbias[:], ALU.add).then_inc(S["hg_r"], 1)
                if isinstance(k, int) and 2 * k + parity == 1:
                    made(pool.memset(ones[:], 1.0))
                    made(pool.memset(tri[:], 1.0))
                    keep(tri[:], [[1, P]], 0, -1, ALU.is_gt, 0.0)
                    made(pool.iota(order_i[:], [[-1, E]], base=E, channel_multiplier=0))
                    made(pool.tensor_copy(order_w[:], order_i[:]))
                    made(pool.iota(blk_i[:], [[1, NBLK]], base=0, channel_multiplier=0))
                    made(pool.tensor_copy(blk[:], blk_i[:]))
                    made(pool.memset(one8[:], 1.0))
                    for q in range(0, P, 32):
                        made(pool.iota(row_i[q:q + 32, :], [[0, P]], base=0, channel_multiplier=1))
                    made(pool.tensor_copy(row_e[:], row_i))
                    made_at["routing"] = n[0]

            run_steps(pool, step)

            pool.wait_ge(S["slot_r"], 1)
            pool.wait_ge(S["xs_zero"], 16)
            pool.wait_ge(S["xn3_kept"], NG)
            for g in range(NG):
                pool.indirect_dma_start(xs_dram, bass.IndirectOffsetOnAxis(ap=slot[:, g:g + 1], axis=0),
                                        xn_all[:, g, :], None).then_inc(S["scattered"], 16)

            pool.wait_ge(f_y_st[0], 16 * ((NBLK + 1) // 2))
            pool.wait_ge(f_y_st[1], 16 * (NBLK // 2))
            for g in range(NG):
                pool.indirect_dma_start(xn_all[:, g, :], None, ys_dram,
                                        bass.IndirectOffsetOnAxis(ap=slot[:, g:g + 1], axis=0)
                                        ).then_inc(gathered[g // 2], 16)

        @block.sync
        def _(sp):
            def load_ctx(g, b):
                for i in range(CC):
                    sp.dma_start(ctx_rows[b][:, :, i, :],
                                 c_in[bass.ds(g * BG, BG), i * P:(i + 1) * P, :].rearrange("j p d -> p j d")
                                 ).then_inc(ctx_ld[b], 16)
                sp.dma_start(ctx_last[:, b, :], c_in[bass.ds(g * BG, BG), CF, :]).then_inc(ctx_ld[b], 16)

            sp.dma_start(Wk, rows(a["L0_xattn_Wk"])).then_inc(S["wk_ld"], 16)
            sp.dma_start(Wr, rows(a["L0_xattn_Wr"])).then_inc(S["wk_ld"], 16)
            load_ctx(0, 0)
            sp.dma_start(last_rows, c_in[:, CF, :]).then_inc(S["last_ld"], 16)
            load_ctx(1, 1)
            sp.dma_start(X[:, 2:NG, :], x_v[:, 2:NG, :]).then_inc(S["xrest_ld"], 16)
            sp.wait_ge(S["consts"], made_at["bias_rows"])
            for i in range(3):
                at = slice(32 * i, 32 * i + E)
                sp.dma_start(bias_rows[at, 0:F], a["L0_ffn_b1"]).then_inc(S["bias_ld"], 16)
                sp.dma_start(bias_rows[at, F:F + D], a["L0_ffn_b2"]).then_inc(S["bias_ld"], 16)

            def load_w1(e):
                sp.dma_start(W1[:, bass.ds(e, 1)].rearrange("p e c f -> p (e c) f"),
                             a["L0_ffn_W1"][bass.ds(e, 1)].rearrange("e (c p) f -> p (e c) f", p=P)
                             ).then_inc(S["w1_ld"], 16)

            load_w1(0)
            with sp.Fori(1, NG // 2) as k:
                for b in range(2):
                    sp.wait_ge(S["pv"], 2 * k + b - 1)
                    load_ctx(2 * k + b, b)
                load_w1(k)
            sp.wait_ge(S["consts"], made_at["zeros"])
            sp.dma_start(xs_dram.rearrange("(n p) d -> p n d", p=P),
                         zeros[:].rearrange("p (o d) -> p o d", o=1).to_broadcast([P, NBLK, D])
                         ).then_inc(S["xs_zero"], 16)
            sp.wait_ge(S["pv"], NG)
            sp.wait_ge(S["bias_split"], 6)
            for e in range(E):
                sp.dma_start(w2[:, e], rows(a["L0_ffn_W2"][e])).then_inc(S["w2_ld"], 16)

            def load_block(j, b):
                sp.dma_start(f_in[:, b, :], xs_dram[bass.ds(j * P, P), :]).then_inc(f_in_ld[b], 16)

            def next_block(j, b, k):
                if not isinstance(j, int) or j + 2 < NBLK:
                    sp.wait_ge(S["f_inT_tr"], j + 1)
                    load_block(j + 2, b)

            sp.wait_ge(S["scattered"], 16 * NG)
            load_block(0, 0)
            load_block(1, 1)
            run_blocks(sp, next_block)
            for g in range(0, NG, 4):
                sp.wait_ge(S["out_add"], g + 4)
                sp.dma_start(out_v[:, g:g + 4, :], X[:, g:g + 4, :]).then_inc(S["stored"], 16)
            sp.wait_ge(S["stored"], 16 * NG // 4)

        @block.vector
        def _(v):
            def stats(g, st, st_r):
                v.bn_stats(st[:], group_of(X, g)).then_inc(S[st_r], 1)

            def moments(g, st, mv, st_r, mv_r):
                count = in_register(v, g + 1)
                settle(v, S["consts"])
                v.wait_ge(S[st_r], count)
                v.bn_aggr(mv[:], st[:]).then_inc(S[mv_r], 1)

            def normal(g, dst, mv, rs, rs_r, done):
                v.wait_ge(S[rs_r], g + 1)
                v.tensor_scalar(dst, group_of(X, g), mv[:, 0:1], rs[:, 0:1], ALU.subtract, ALU.mult
                                ).then_inc(S[done], 1)

            def stats_x(g):
                if isinstance(g, int) and g in (0, 2):
                    v.wait_ge(S["x_ld" if g == 0 else "xrest_ld"], 16)
                settle(v, S["consts"])
                at_least(v, S["rs1_r"], g)
                stats(g, st1, "st1_r")

            def normal_x(g, b):
                at_least(v, S["xnT_tr"], g - 1)
                normal(g, xn[:, b, :], mv1, rs1, "rs1_r", "xn_r")

            v.wait_ge(S["wkT_tr"], 1)
            v.tensor_copy(WkT.rearrange("p c n -> p (c n)"), pT[0][:]).then_inc(S["wkT_cp"], 1)
            stats_x(0)
            moments(0, st1, mv1, "st1_r", "mv1_r")
            v.wait_ge(S["wkr_mm"], 1)
            v.tensor_scalar(Wkr[:].rearrange("p c n -> p (c n)"), pK[0][:], INV_2PI, None, ALU.mult
                            ).then_inc(S["wkr_cp"], 1)
            v.wait_ge(S["bkr_mm"], 1)
            v.tensor_tensor(bkr[:], b4[:, 0:DC], br[:], ALU.add).then_inc(S["bkr_sum"], 1)
            v.wait_ge(S["bkr_sum"], 1)
            v.tensor_scalar(bkr[:], bkr[:], INV_2PI, 0.25, ALU.mult, ALU.add).then_inc(S["bkr_cp"], 1)
            normal_x(0, 0)
            v.wait_ge(S["wqkT_tr"], 1)
            v.tensor_copy(WqkT[:].rearrange("p c n -> p (c n)"), b5[:, 0:DC * 2 * H]).then_inc(S["wqkT_cp"], 1)
            v.wait_ge(S["lastT_tr"], 1)
            v.tensor_copy(last_T.rearrange("p c n -> p (c n)"), b7[:, 0:DC * B]).then_inc(S["lastT_cp"], 1)
            v.wait_ge(S["lastK_mm"], 1)
            v.wait_ge(S["bkr_cp"], 1)
            for r in range(DC):
                v.tensor_scalar(last_turns[:, r, :], b6[:, r * B:(r + 1) * B], bkr[:, r:r + 1], None, ALU.add
                                ).then_inc(S["last_turn"], 1)
            v.wait_ge(S["last_turn"], 2)
            v.tensor_scalar(last_frac, last_turns, ROUND, ROUND, ALU.add, ALU.subtract
                            ).then_inc(S["last_whole"], 1)
            v.wait_ge(S["last_whole"], 1)
            v.tensor_tensor(last_frac, last_turns, last_frac, ALU.subtract).then_inc(S["last_fr"], 1)
            v.wait_ge(S["scal_act"], 1)
            v.tensor_scalar(sc[:, 1:2], sc[:, 0:1], 1.0, None, ALU.add).then_inc(S["scal_dve"], 1)
            v.wait_ge(S["scal_dve"], 1)
            v.reciprocal(sc[:, 2:3], sc[:, 1:2]).then_inc(S["scal_dve"], 1)
            v.wait_ge(S["scal_dve"], 2)
            v.tensor_scalar(sc[:, 3:4], sc[:, 2:3], -1.0, 1.0, ALU.mult, ALU.add).then_inc(S["scal_dve"], 1)
            v.tensor_scalar(sc[:, 8:9], logs[:, 1:2], 0.0, 0.01, ALU.max, ALU.add).then_inc(S["scal_dve"], 1)
            v.wait_ge(S["scal_act"], 4)
            v.wait_ge(S["scal_dve"], 4)
            v.tensor_tensor(sc[:, 9:10], sc[:, 7:8], sc[:, 8:9], ALU.add).then_inc(S["scal_dve"], 1)
            v.wait_ge(S["scal_dve"], 5)

            def whole(g, u):
                b = u % 2
                v.wait_ge(S["turns_r"], 4 * g + u + 1)
                at_least(v, S["khat_r"], 4 * g + u - 1)
                v.tensor_scalar(frac[b], turns[b], ROUND, ROUND, ALU.add, ALU.subtract).then_inc(S["whole_r"], 1)

            def fraction(g, u):
                b = u % 2
                v.wait_ge(S["whole_r"], 4 * g + u + 1)
                v.tensor_tensor(frac[b], turns[b], frac[b], ALU.subtract).then_inc(S["frac_r"], 1)

            def ctx_T_copy(g, half):
                v.wait_ge(S["ctxT_tr"], 4 * g + 2 * half + 1)
                at_least(v, S["kproj"], 4 * g + 2 * half - 2)
                v.tensor_copy(ctx_T[:, 0, half * 512:(half + 1) * 512], pT[0][:]).then_inc(S["ctxT0_cp"], 1)

            def split_biases(third):
                def part(rows, n):
                    v.tensor_copy(b_parts[rows, :], bias_rows[rows, :]).then_inc(S["bias_split"], 1)
                    v.wait_ge(S["bias_split"], n)

                def rest(rows, n):
                    v.tensor_tensor(bias_rows[rows, :], bias_rows[rows, :], b_parts[rows, :], ALU.subtract
                                    ).then_inc(S["bias_split"], 1)
                    v.wait_ge(S["bias_split"], n)

                if third == 0:
                    v.wait_ge(S["bias_ld"], 6 * 16)
                    part(slice(0, P), 1)
                    rest(slice(0, P), 2)
                elif third == 1:
                    part(slice(32, 64), 3)
                    part(slice(64, P), 4)
                else:
                    rest(slice(64, P), 5)
                    part(slice(64, P), 6)

            def step(k, parity):
                now, one, two, three, four, coming = (groups(k, parity, n) for n in (0, 1, 2, 3, 4, -1))
                if now:
                    ctx_T_copy(now[0], 0)
                    g, b, _ = now
                    v.wait_ge(S["xnT_tr"], g + 1)
                    at_least(v, S["qproj"], g)
                    v.tensor_copy(xnT[:].rearrange("p c n -> p (c n)"), p_xnT).then_inc(S["xnT_cp"], 1)
                if one:
                    g, b, _ = one
                    v.wait_ge(S["scoresA"], g + 1)
                    v.tensor_reduce(nmaxA[:], p_score, AX.X, ALU.max, negate=True).then_inc(S["nmaxA_r"], 1)
                if three:
                    g, b, _ = three
                    v.wait_ge(S["probsB"], g + 1)
                    v.reciprocal(rsumB[:], sumB[:]).then_inc(S["rsumB_r"], 1)
                if coming:
                    stats_x(coming[0])
                if three:
                    g, b, _ = three
                    v.wait_ge(S["rsumB_r"], g + 1)
                    at_least(v, S["attT_tr"], g)
                    v.tensor_scalar(att[:], expB[:], rsumB[:, 0:1], 0.0, ALU.mult, ALU.max).then_inc(S["att_r"], 1)
                if coming:
                    moments(coming[0], st1, mv1, "st1_r", "mv1_r")
                if one:
                    g, b, _ = one
                    v.wait_ge(S["probsA"], g + 1)
                    v.reciprocal(rsumA[:], sumA[:]).then_inc(S["rsumA_r"], 1)
                    if isinstance(g, int) and g == 0:
                        v.wait_ge(S["consts"], made_at["own_batch"])
                    at_least(v, S["pT_tr"], g)
                    v.tensor_scalar(p_last[:], own_batch[:], probs[:, CF:C], None, ALU.mult
                                    ).then_inc(S["plast_r"], 1)
                if coming:
                    normal_x(coming[0], coming[1])
                if four:
                    g, b, _ = four
                    v.wait_ge(S["gelu_r"], g + 1)
                    v.scalar_tensor_tensor(group_of(X, g), gel[:], sc[:, 9:10], group_of(X, g), ALU.mult, ALU.add
                                           ).then_inc(S["x2_r"], 1)
                    settle(v, S["consts"])
                    v.wait_ge(S["x2_r"], g + 1)
                    at_least(v, S["rs3_r"], g)
                    stats(g, st3, "st3_r")
                if one:
                    g, b, _ = one
                    v.wait_ge(S["pT_tr"], g + 1)
                    at_least(v, S["pv"], g)
                    v.tensor_copy(probsT[:].rearrange("p c n -> p (c n)"), p_pT).then_inc(S["pT_cp"], 1)
                    v.tensor_copy(p_lastT[:], p_plT).then_inc(S["pT_cp"], 1)
                if four:
                    moments(four[0], st3, mv3, "st3_r", "mv3_r")
                if two:
                    g, b, _ = two
                    if isinstance(g, int) and g == 0:
                        v.wait_ge(S["consts"], made_at["masks"])
                    v.wait_ge(S["sim_mm"], g + 1)
                    v.tensor_tensor(simm[:], p_sim, causal[:], ALU.add).then_inc(S["simm_r"], 1)
                if now:
                    whole(now[0], 0)
                if two:
                    g, b, _ = two
                    settle(v, S["consts"])
                    v.wait_ge(S["simm_r"], g + 1)
                    v.max(top8[:], simm[:]).then_inc(S["top_r"], 1)
                if now:
                    fraction(now[0], 0)
                if two:
                    g, b, _ = two
                    settle(v, S["consts"])
                    v.wait_ge(S["top_r"], g + 1)
                    v.match_replace(marked[:], top8[:], simm[:], PICKED).then_inc(S["marked_r"], 1)
                if now:
                    whole(now[0], 1)
                    ctx_T_copy(now[0], 1)
                if two:
                    g, b, _ = two
                    v.wait_ge(S["marked_r"], g + 1)
                    v.tensor_tensor(pick[:], marked[:], pickable[:], ALU.is_equal).then_inc(S["pick_r"], 1)
                if now:
                    fraction(now[0], 1)
                if three:
                    g, b, _ = three
                    v.wait_ge(S["attT_tr"], g + 1)
                    at_least(v, S["msg_mm"], g)
                    v.tensor_copy(attT[:], p_attT).then_inc(S["attT_cp"], 1)
                if one:
                    g, b, _ = one
                    v.wait_ge(S["pv"], g + 1)
                    v.wait_ge(S["rsumA_r"], g + 1)
                    at_least(v, S["oT_tr"], g)
                    v.tensor_scalar(o_norm[:], p_o, rsumA[:, 0:1], None, ALU.mult).then_inc(S["o_r"], 1)
                if two:
                    g, b, _ = two
                    settle(v, S["consts"])
                    v.wait_ge(S["scoreB_mm"], g + 1)
                    v.wait_ge(S["base_r"], g + 1)
                    v.wait_ge(S["pick_r"], g + 1)
                    v.copy_predicated(scoreB[:, b, :], pick[:], p_scoreB).then_inc(S["selected"], 1)
                if four:
                    g, b, _ = four
                    at_least(v, S["xn3_kept"], g)
                    at_least(v, S["xn3T_tr"], g)
                    normal(g, xn3[:, b, :], mv3, rs3, "rs3_r", "xn3_r")
                if two:
                    g, b, _ = two
                    v.wait_ge(S["selected"], g + 1)
                    v.tensor_reduce(nmaxB[:, b:b + 1], scoreB[:, b, :], AX.X, ALU.max, negate=True
                                    ).then_inc(S["nmaxB_r"], 1)
                if now:
                    whole(now[0], 2)
                    fraction(now[0], 2)
                if one:
                    g, b, _ = one
                    v.wait_ge(S["oT_tr"], g + 1)
                    at_least(v, S["aproj"], g)
                    v.tensor_copy(o_T[:].rearrange("p c n -> p (c n)"), p_oT).then_inc(S["oT_cp"], 1)
                if now:
                    whole(now[0], 3)
                    fraction(now[0], 3)
                if three:
                    g, b, _ = three
                    v.wait_ge(S["msg_mm"], g + 1)
                    v.tensor_tensor(y_msg[:], p_msg, gain_msg[:], ALU.mult).then_inc(S["ymsg_r"], 1)
                if one:
                    g, b, _ = one
                    v.wait_ge(S["aproj"], g + 1)
                    v.wait_ge(S["xb_r"], g + 1)
                    v.tensor_tensor(group_of(X, g), p_a, group_of(X, g), ALU.add).then_inc(S["x1_r"], 1)
                    settle(v, S["consts"])
                    v.wait_ge(S["x1_r"], g + 1)
                    at_least(v, S["rs2_r"], g)
                    stats(g, st2, "st2_r")
                if three:
                    g, b, _ = three
                    v.wait_ge(S["ymsg_r"], g + 1)
                    v.wait_ge(S["hg_r"], g + 1)
                    at_least(v, S["gelu_r"], g)
                    v.tensor_tensor(y[:], y_msg[:], hg[:, b, :], ALU.add).then_inc(S["y_r"], 1)
                if one:
                    moments(one[0], st2, mv2, "st2_r", "mv2_r")
                if four:
                    g, b, _ = four
                    v.wait_ge(S["route_mm"], g + 1)
                    v.tensor_copy(group_of(logits, g), p_route).then_inc(S["logits_r"], 1)
                if one:
                    g, b, _ = one
                    at_least(v, S["msg_mm"], g - 1)
                    at_least(v, S["hg_m"], g - 1)
                    normal(g, h[:, b, :], mv2, rs2, "rs2_r", "h_r")
                if isinstance(k, int) and 1 <= 2 * k + parity <= 3:
                    split_biases(2 * k + parity - 1)

            run_steps(v, step)

            n = [0]

            def then(ins):
                n[0] += 1
                ins.then_inc(S["route"], 1)
                v.wait_ge(S["route"], n[0])

            def per_group(t):
                return t.rearrange("p (g o) -> p g o", o=1).to_broadcast([P, NG, E])

            def per_expert(t):
                return t.rearrange("p (o e) -> p o e", o=1).to_broadcast([P, NG, E])

            v.wait_ge(S["consts"], made_at["routing"])
            v.wait_ge(S["logits_r"], NG)
            then(v.tensor_reduce(per_token[:, 0, :], logits[:], AX.X, ALU.max))
            then(v.tensor_tensor(rt[0], logits[:], per_group(per_token[:, 0, :]), ALU.subtract))
            made_at["route_sub"] = n[0]
            v.wait_ge(S["route_exp"], 1)
            then(v.tensor_reduce(per_token[:, 1, :], rt[1], AX.X, ALU.add))
            then(v.reciprocal(per_token[:, 0, :], per_token[:, 1, :]))
            then(v.tensor_reduce(per_token[:, 2, :], rt[1], AX.X, ALU.max))
            then(v.tensor_tensor(p_max[:], per_token[:, 0, :], per_token[:, 2, :], ALU.mult))
            then(v.tensor_tensor(rt[0], rt[1], per_group(per_token[:, 2, :]), ALU.is_equal))
            then(v.tensor_tensor(rt[2], rt[0], per_expert(order_w[:]), ALU.mult))
            then(v.tensor_reduce(per_token[:, 0, :], rt[2], AX.X, ALU.max))
            then(v.tensor_tensor(onehot[:], rt[2], per_group(per_token[:, 0, :]), ALU.is_equal))
            then(v.tensor_reduce(starts[:], onehot[:].rearrange("p g e -> p e g"), AX.X, ALU.add))
            then(v.tensor_copy(cnt[:], starts[:]))
            made_at["onehot"] = n[0]
            v.wait_ge(S["rank_mm"], 1)
            then(v.tensor_scalar(blocks_i[:, 0, :], b7[:, 0:E], float(P - 1), None, ALU.add))
            then(v.tensor_scalar(blocks_i[:, 1, :], blocks_i[:, 0, :], 7, None, ALU.logical_shift_right))
            then(v.tensor_copy(blocks[:], blocks_i[:, 1, :]))
            then(v.tensor_tensor_scan(ends[:], one8[:], blocks[:], 0.0, ALU.mult, ALU.add))
            then(v.tensor_tensor(starts[:], ends[:], blocks[:], ALU.subtract))
            then(v.tensor_scalar(starts[:], starts[:], float(P), None, ALU.mult))
            then(v.tensor_tensor(rt[0], b6[:, 0:NG * E].rearrange("p (g e) -> p g e", g=NG),
                                 per_expert(starts[:]), ALU.add))
            then(v.tensor_tensor(rt[2], rt[0], onehot[:], ALU.mult))
            then(v.tensor_reduce(per_token[:, 1, :], rt[2], AX.X, ALU.add))
            v.tensor_copy(slot[:], per_token[:, 1, :]).then_inc(S["slot_r"], 1)
            then(v.tensor_tensor(past, blk[:].rearrange("p (n o) -> p n o", o=1).to_broadcast([P, NBLK, E]),
                                 ends[:].rearrange("p (o e) -> p o e", o=1).to_broadcast([P, NBLK, E]),
                                 ALU.is_ge))
            then(v.tensor_reduce(expert[:], past, AX.X, ALU.add))
            then(v.tensor_scalar(expert[:], expert[:], float(E - 1), None, ALU.min))
            v.tensor_copy(expert_i[:], expert[:]).then_inc(S["expert_r"], 1)

            def select(j, b):
                v.tensor_scalar(f_sel[:, b, :], row_e[:], expert[:, bass.ds(j, 1)], None, ALU.is_equal
                                ).then_inc(S["f_sel_r"], 1)

            def in_T(j, b):
                v.wait_ge(S["f_inT_tr"], j + 1)
                at_least(v, S["f_h_mm"], 2 * (j - 1))
                v.tensor_copy(f_inT[:, b, :], p_in[b]
                              ).then_inc(S["f_inT_cp"], 1)

            def expert_block(j, b, k):
                v.wait_ge(S["f_hT_tr"], 2 * j + 1)
                at_least(v, S["f_y_mm"], j)
                v.tensor_copy(f_hT[:, 0:512], pT[0][:]).then_inc(S["f_hT0_cp"], 1)
                if not isinstance(j, int) or j + 2 < NBLK:
                    in_T(j + 2, b)
                v.wait_ge(S["f_y_mm"], j + 1)
                at_least(v, f_y_st[b], 16 * k)
                v.tensor_copy(f_out[:, b, :], p_out[b]).then_inc(S["f_y_cp"], 1)
                if not isinstance(j, int) or j + 2 < NBLK:
                    select(j + 2, b)

            v.wait_ge(S["expert_r"], 1)
            select(0, 0)
            select(1, 1)
            in_T(0, 0)
            in_T(1, 1)
            run_blocks(v, expert_block)
            for g in range(NG):
                v.wait_ge(gathered[g // 2], 32)
                v.scalar_tensor_tensor(X[:, g, :], xn_all[:, g, :], p_max[:, g:g + 1], X[:, g, :],
                                       ALU.mult, ALU.add).then_inc(S["out_add"], 1)

        @block.scalar
        def _(act):
            act.dma_start(bk[:], col(a["L0_xattn_bk"]), allow_slow_non_contiguous=True).then_inc(S["wk_ld"], 16)
            act.dma_start(br[:], col(a["L0_xattn_br"]), allow_slow_non_contiguous=True).then_inc(S["wk_ld"], 16)
            act.dma_start(X[:, 0:2, :], x_v[:, 0:2, :]).then_inc(S["x_ld"], 16)
            act.dma_start(logs[:, 0:1], a["L0_attn_log_mix"].partition_broadcast(P)).then_inc(S["logs_ld"], 16)
            act.dma_start(logs[:, 1:2], a["L0_attn_log_scale"].partition_broadcast(P)).then_inc(S["logs_ld"], 16)
            act.dma_start(bq[:], col(a["L0_xattn_bq"]), allow_slow_non_contiguous=True).then_inc(S["w_ld"], 16)
            act.dma_start(Wqk[0:H, :], a["L0_attn_W_q"]).then_inc(S["w_ld"], 16)
            act.dma_start(Wqk[H:2 * H, :], a["L0_attn_W_k"]).then_inc(S["w_ld"], 16)
            act.dma_start(Wq[:], rows(a["L0_xattn_Wq"])).then_inc(S["w_ld"], 16)
            act.dma_start(bv[:], a["L0_xattn_bv"].partition_broadcast(P)).then_inc(S["w_ld"], 16)
            act.dma_start(gain, a["L0_attn_gain"].partition_broadcast(P)).then_inc(S["w_ld"], 16)
            act.dma_start(gbias[:], a["L0_attn_bias"].partition_broadcast(P)).then_inc(S["w_ld"], 16)
            act.dma_start(Wv[:], rows(a["L0_xattn_Wv"])).then_inc(S["w_ld"], 16)
            act.dma_start(Wroute[:], rows(a["L0_ffn_Wr"])).then_inc(S["w_ld"], 16)

            act.wait_ge(S["logs_ld"], 2 * 16)
            act.activation(sc[:, 0:1], logs[:, 0:1], ACT.Exp, scale=-1.0).then_inc(S["scal_act"], 1)
            act.activation(sc[:, 5:6], logs[:, 1:2], ACT.Abs).then_inc(S["scal_act"], 1)
            act.wait_ge(S["scal_act"], 2)
            act.activation(sc[:, 6:7], sc[:, 5:6], ACT.Exp, scale=-1.0).then_inc(S["scal_act"], 1)
            act.wait_ge(S["scal_act"], 3)
            act.activation(sc[:, 7:8], sc[:, 6:7], ACT.Ln, bias=1.0).then_inc(S["scal_act"], 1)
            act.wait_ge(S["last_fr"], 1)
            act.activation(khat_last[:], last_frac, ACT.Sin, scale=TWO_PI).then_inc(S["khat_last_r"], 1)

            def ctx_T_copy(g, half):
                act.wait_ge(S["ctxT_tr"], 4 * g + 2 * half + 2)
                at_least(act, S["kproj"], 4 * g + 2 * half - 2)
                act.copy(ctx_T[:, 1, half * 512:(half + 1) * 512], pT[1][:]).then_inc(S["ctxT1_cp"], 1)

            def turn(g, u):
                r = u % 2
                act.wait_ge(S["kproj"], 4 * g + u + 1)
                at_least(act, S["frac_r"], 4 * g + u - 1)
                act.activation(turns[r], pK[r][:], ACT.Identity, bias=bkr[:, r:r + 1]).then_inc(S["turns_r"], 1)

            def sine(g, b, u):
                half, r = u // 2, u % 2
                act.wait_ge(S["frac_r"], 4 * g + u + 1)
                at_least(act, S["scoresA"], g - 1)
                act.activation(khat[b][:, r, 2 * half:2 * half + 2, 0:CF], frac[r].rearrange("p (j n) -> p j n", j=2),
                               ACT.Sin, scale=TWO_PI).then_inc(S["khat_r"], 1)

            act.wait_ge(S["w_ld"], 16 * W_LOADS)
            act.wait_ge(S["bkr_cp"], 1)

            def step(k, parity):
                now, one, two, three, four = (groups(k, parity, n) for n in (0, 1, 2, 3, 4))
                if three:
                    g, b, _ = three
                    act.wait_ge(S["nmaxB_r"], g + 1)
                    at_least(act, S["att_r"], g)
                    act.activation(expB[:], scoreB[:, b, :], ACT.Exp, bias=nmaxB[:, b:b + 1], accum_out=sumB[:]
                                   ).then_inc(S["probsB"], 1)
                if now:
                    ctx_T_copy(now[0], 0)
                if one:
                    g, b, _ = one
                    act.wait_ge(S["nmaxA_r"], g + 1)
                    at_least(act, S["pT_tr"], g)
                    at_least(act, S["plast_r"], g)
                    at_least(act, S["rsumA_r"], g)
                    act.activation(probs[:], p_score, ACT.Exp, bias=nmaxA[:, 0:1], accum_out=sumA[:]
                                   ).then_inc(S["probsA"], 1)
                if four:
                    g, b, _ = four
                    act.wait_ge(S["y_r"], g + 1)
                    at_least(act, S["x2_r"], g)
                    act.activation(gel[:], y[:], ACT.Gelu).then_inc(S["gelu_r"], 1)
                if two:
                    g, b, _ = two
                    act.wait_ge(S["hT_tr"], g + 1)
                    at_least(act, S["qk_mm"], g)
                    act.copy(hT[:].rearrange("p c n -> p (c n)"), p_hT).then_inc(S["hT_cp"], 1)
                if now:
                    turn(now[0], 0)
                    turn(now[0], 1)
                if two:
                    g, b, _ = two
                    act.wait_ge(S["qk_mm"], g + 1)
                    at_least(act, S["scoreB_mm"], g)
                    act.mul(qB[:], p_qk[0:H, :], float(H ** -0.5)).then_inc(S["qk_cp"], 1)
                    act.copy(kB[:], p_qk[H:2 * H, :]).then_inc(S["qk_cp"], 1)
                if now:
                    g, b, _ = now
                    sine(g, b, 0)
                    ctx_T_copy(g, 1)
                    sine(g, b, 1)
                    act.wait_ge(S["qproj"], g + 1)
                    at_least(act, S["scoresA"], g)
                    for c in range(DC):
                        act.activation(qT[:, c, :], p_q[:, c * P:(c + 1) * P], ACT.Identity, bias=bq[:, c:c + 1]
                                       ).then_inc(S["q_r"], 1)
                    turn(g, 2)
                    turn(g, 3)
                if four:
                    g, b, _ = four
                    act.wait_ge(S["xn3T_tr"], g + 1)
                    at_least(act, S["route_mm"], g)
                    act.copy(xn3T[:].rearrange("p c n -> p (c n)"), p_xn3T).then_inc(S["xn3T_cp"], 1)
                if now:
                    g, b, _ = now
                    sine(g, b, 2)
                    sine(g, b, 3)

            run_steps(act, step)

            act.wait_ge(S["route"], made_at["route_sub"])
            act.activation(rt[1], rt[0], ACT.Exp).then_inc(S["route_exp"], 1)

            def gelus(j):
                at_least(act, S["f_hT_tr"], 2 * j)
                for i in range(2):
                    act.wait_ge(S["f_h_mm"], 2 * j + i + 1)
                    act.activation(f_h[:, i * 512:(i + 1) * 512], pK[i][:], ACT.Gelu).then_inc(S["f_gelu"], 1)

            def store_result(j, b):
                act.wait_ge(S["f_y_cp"], j + 1)
                act.dma_start(ys_dram[bass.ds(j * P, P), :], f_out[:, b, :]).then_inc(f_y_st[b], 16)

            def expert_block(j, b, k):
                act.wait_ge(S["f_hT_tr"], 2 * j + 2)
                at_least(act, S["f_y_mm"], j)
                act.copy(f_hT[:, 512:1024], pT[1][:]).then_inc(S["f_hT1_cp"], 1)
                if not isinstance(j, int) or j > 0:
                    store_result(j - 1, 1 - b)
                if not isinstance(j, int) or j + 1 < NBLK:
                    gelus(j + 1)

            gelus(0)
            run_blocks(act, expert_block)
            store_result(NBLK - 1, (NBLK - 1) % 2)

        @block.tensor
        def _(pe):
            def transposed(dst, src, done=None):
                k = src.shape[0]
                ins = pe.transpose(dst, src, ident[0:k, 0:k])
                if done:
                    ins.then_inc(S[done], 1)

            pe.wait_ge(S["consts"], made_at["ident"])
            pe.wait_ge(S["wk_ld"], 64)
            for ec in range(DC):
                for dc in range(DC):
                    transposed(pT[0][:, (ec * DC + dc) * P:(ec * DC + dc + 1) * P], Wk[:, dc, ec * P:(ec + 1) * P],
                               "wkT_tr" if (ec, dc) == (DC - 1, DC - 1) else None)
            pe.wait_ge(S["wkT_cp"], 1)
            for dc in range(DC):
                for ec in range(DC):
                    mm = pe.matmul(pK[0][:, dc * D:(dc + 1) * D], WkT[:, ec, dc * P:(dc + 1) * P], Wr[:, ec, :],
                                   start=ec == 0, stop=ec == DC - 1)
            mm.then_inc(S["wkr_mm"], 1)
            for r in range(DC):
                for ec in range(DC):
                    mm = pe.matmul(b4[:, r:r + 1], Wr[:, ec, r * P:(r + 1) * P], bk[:, ec:ec + 1],
                                   start=ec == 0, stop=ec == DC - 1)
            mm.then_inc(S["bkr_mm"], 1)
            pe.wait_ge(S["w_ld"], 16 * W_LOADS)
            for c in range(DC):
                transposed(b5[:, c * 2 * H:(c + 1) * 2 * H], Wqk[:, c * P:(c + 1) * P],
                           "wqkT_tr" if c == DC - 1 else None)
            pe.wait_ge(S["last_ld"], 16)
            for c in range(DC):
                transposed(b7[:, c * B:(c + 1) * B], last_rows[:, c * P:(c + 1) * P],
                           "lastT_tr" if c == DC - 1 else None)
            pe.wait_ge(S["wkr_cp"], 1)
            pe.wait_ge(S["lastT_cp"], 1)
            for r in range(DC):
                for c in range(DC):
                    mm = pe.matmul(b6[:, r * B:(r + 1) * B], Wkr[:, c, r * P:(r + 1) * P], last_T[:, c, :],
                                   start=c == 0, stop=c == DC - 1)
            mm.then_inc(S["lastK_mm"], 1)
            pe.wait_ge(S["bkr_cp"], 1)
            pe.wait_ge(S["wqkT_cp"], 1)
            pe.wait_ge(S["last_turn"], 2)

            def ctx_transposes(g, b, q, half):
                pe.wait_ge(ctx_ld[b], 16 * CTX_LOADS * (q + 1))
                for c in range(DC):
                    at_least(pe, S["ctxT0_cp" if c == 0 else "ctxT1_cp"], 2 * g + half)
                    for i in range(4):
                        src = ctx_rows[b][:, 2 * half + i // 2, i % 2, c * P:(c + 1) * P]
                        transposed(pT[c][:, i * P:(i + 1) * P], src, "ctxT_tr" if i == 3 else None)

            def ctx_project(g, half, r):
                pe.wait_ge(S["ctxT0_cp"], 2 * g + half + 1)
                pe.wait_ge(S["ctxT1_cp"], 2 * g + half + 1)
                at_least(pe, S["turns_r"], 4 * g + 2 * half + r - 1)
                for c in range(DC):
                    mm = pe.matmul(pK[r][:], Wkr[:, c, r * P:(r + 1) * P],
                                   ctx_T[:, c, half * 512:(half + 1) * 512], start=c == 0, stop=c == DC - 1)
                mm.then_inc(S["kproj"], 1)

            def step(k, parity):
                now, one, two, three, four = (groups(k, parity, n) for n in (0, 1, 2, 3, 4))
                if now:
                    g, b, q = now
                    ctx_transposes(g, b, q, 0)
                    pe.wait_ge(S["xn_r"], g + 1)
                    at_least(pe, S["selected"], g - 2)
                    at_least(pe, S["ymsg_r"], g - 3)
                    for c in range(DC):
                        transposed(p_xnT[:, c * P:(c + 1) * P], xn[:, b, c * P:(c + 1) * P],
                                   "xnT_tr" if c == DC - 1 else None)
                if one:
                    g, b, _ = one
                    pe.wait_ge(S["khat_r"], 4 * g + 4)
                    pe.wait_ge(S["klast_r"], g + 1)
                    pe.wait_ge(S["q_r"], 2 * g + 2)
                    at_least(pe, S["oT_cp"], g)
                    at_least(pe, S["attT_cp"], g - 2)
                    for r in range(DC):
                        for j in range(BG):
                            mm = pe.matmul(p_score[j * T:(j + 1) * T, :], qT[:, r, j * T:(j + 1) * T],
                                           khat[b][:, r, j, :], start=r == 0, stop=r == DC - 1,
                                           skip_group_check=True)
                    mm.then_inc(S["scoresA"], 1)
                if now:
                    ctx_project(now[0], 0, 0)
                if two:
                    g, b, _ = two
                    pe.wait_ge(S["h_r"], g + 1)
                    pe.wait_ge(S["x1_r"], g + 1)
                    for c in range(DC):
                        transposed(p_hT[:, c * P:(c + 1) * P], h[:, b, c * P:(c + 1) * P],
                                   "hT_tr" if c == DC - 1 else None)
                if now:
                    ctx_project(now[0], 0, 1)
                if one:
                    g, b, _ = one
                    pe.wait_ge(S["probsA"], g + 1)
                    pe.wait_ge(S["plast_r"], g + 1)
                    for c in range(CC):
                        transposed(p_pT[:, c * P:(c + 1) * P], probs[:, c * P:(c + 1) * P])
                    transposed(p_plT, p_last[:], "pT_tr")
                if two:
                    g, b, _ = two
                    pe.wait_ge(S["hT_cp"], g + 1)
                    at_least(pe, S["xnT_cp"], upto(g + 3, NG))
                    at_least(pe, S["ymsg_r"], g - 1)
                    for c in range(DC):
                        mm = pe.matmul(p_sim, hT[:, c, :], hT[:, c, :], start=c == 0, stop=c == DC - 1)
                    mm.then_inc(S["sim_mm"], 1)
                    for c in range(DC):
                        mm = pe.matmul(p_qk, WqkT[:, c, :], hT[:, c, :], start=c == 0, stop=c == DC - 1)
                    mm.then_inc(S["qk_mm"], 1)
                if now:
                    g, b, q = now
                    ctx_transposes(g, b, q, 1)
                if one:
                    g, b, _ = one
                    pe.wait_ge(S["pT_cp"], 2 * g + 2)
                    at_least(pe, S["o_r"], g)
                    at_least(pe, S["logits_r"], g - 3)
                    for c in range(CC):
                        for j in range(BG):
                            pe.matmul(p_o[j * T:(j + 1) * T, :], probsT[:, c, j * T:(j + 1) * T],
                                      ctx_rows[b][:, j, c, :], start=c == 0, stop=False, skip_group_check=True)
                    pe.matmul(p_o, p_lastT[:], ctx_last[:, b, :], start=False, stop=True, skip_group_check=True
                              ).then_inc(S["pv"], 1)
                if three:
                    g, b, _ = three
                    pe.wait_ge(S["att_r"], g + 1)
                    at_least(pe, S["pT_cp"], upto(2 * g + 6, 2 * NG))
                    at_least(pe, S["oT_cp"], upto(g + 2, NG))
                    transposed(p_attT, att[:], "attT_tr")
                if two:
                    g, b, _ = two
                    pe.wait_ge(S["qk_cp"], 2 * g + 2)
                    pe.wait_ge(S["simm_r"], g + 1)
                    pe.matmul(p_scoreB, qB[:], kB[:], start=True, stop=True).then_inc(S["scoreB_mm"], 1)
                if now:
                    g, b, _ = now
                    pe.wait_ge(S["xnT_cp"], g + 1)
                    at_least(pe, S["qk_cp"], 2 * g - 2)
                    at_least(pe, S["x1_r"], g - 1)
                    for r in range(DC):
                        for c in range(DC):
                            mm = pe.matmul(p_q[:, r * P:(r + 1) * P], Wq[:, c, r * P:(r + 1) * P], xnT[:, c, :],
                                           start=c == 0, stop=c == DC - 1)
                    mm.then_inc(S["qproj"], 1)
                    ctx_project(g, 1, 0)
                    ctx_project(g, 1, 1)
                if one:
                    g, b, _ = one
                    pe.wait_ge(S["o_r"], g + 1)
                    at_least(pe, S["attT_cp"], g - 1)
                    for c in range(DC):
                        transposed(p_oT[:, c * P:(c + 1) * P], o_norm[:, c * P:(c + 1) * P],
                                   "oT_tr" if c == DC - 1 else None)
                if four:
                    g, b, _ = four
                    pe.wait_ge(S["xn3_r"], g + 1)
                    at_least(pe, S["o_r"], upto(g + 4, NG))
                    at_least(pe, S["logits_r"], g)
                    for c in range(DC):
                        transposed(p_xn3T[:, c * P:(c + 1) * P], xn3[:, b, c * P:(c + 1) * P],
                                   "xn3T_tr" if c == DC - 1 else None)
                if three:
                    g, b, _ = three
                    pe.wait_ge(S["attT_cp"], g + 1)
                    at_least(pe, S["selected"], upto(g + 2, NG))
                    pe.matmul(p_msg, attT[:], h[:, b, :], start=True, stop=True).then_inc(S["msg_mm"], 1)
                if one:
                    g, b, _ = one
                    pe.wait_ge(S["oT_cp"], g + 1)
                    at_least(pe, S["q_r"], upto(2 * g + 4, 2 * NG))
                    at_least(pe, S["qk_cp"], 2 * g)
                    for c in range(DC):
                        mm = pe.matmul(p_a, o_T[:, c, :], Wv[:, c, :], start=c == 0, stop=c == DC - 1)
                    mm.then_inc(S["aproj"], 1)
                if four:
                    g, b, _ = four
                    pe.wait_ge(S["xn3T_cp"], g + 1)
                    for c in range(DC):
                        mm = pe.matmul(p_route, xn3T[:, c, :], Wroute[:, c, :], start=c == 0, stop=c == DC - 1)
                    mm.then_inc(S["route_mm"], 1)

            run_steps(pe, step)

            pe.wait_ge(S["route"], made_at["onehot"])
            pe.matmul(b6[:, 0:NG * E], tri[:], onehot[:].rearrange("p g e -> p (g e)"), start=True, stop=False,
                      skip_group_check=True)
            for g in range(NG - 1):
                later = NG - 1 - g
                pe.matmul(b6[:, (g + 1) * E:NG * E], ones[:],
                          onehot[:, g:g + 1, :].to_broadcast([P, later, E]), start=False, stop=g == NG - 2,
                          skip_group_check=True)
            pe.matmul(b7[:, 0:E], ones[:], cnt[:], start=True, stop=True).then_inc(S["rank_mm"], 1)

            def in_T(j, b, k):
                pe.wait_ge(f_in_ld[b], 16 * (k + 1))
                if isinstance(j, int) and j == 0:
                    pe.wait_ge(S["expert_r"], 1)
                at_least(pe, S["f_inT_cp"], j - 1)
                for c in range(DC):
                    transposed(p_in[b][:, c * P:(c + 1) * P], f_in[:, b, c * P:(c + 1) * P],
                               "f_inT_tr" if c == DC - 1 else None)

            def expert_of(j):
                return pe.value_load(expert_i[0:1, bass.ds(j, 1)], min_val=0, max_val=E - 1)

            def up(j, b, e):
                pe.wait_ge(S["f_inT_cp"], j + 1)
                pe.wait_ge(S["f_sel_r"], j + 1)
                for i in range(2):
                    at_least(pe, S["f_gelu"], 2 * (j - 1) + i + 1)
                    pe.matmul(pK[i][:], f_sel[:, b, :], b_parts[:, i * 512:(i + 1) * 512], start=True, stop=False)
                    for c in range(DC):
                        mm = pe.matmul(pK[i][:], f_inT[:, b, c * P:(c + 1) * P],
                                       W1[:, bass.ds(e, 1), c, i * 512:(i + 1) * 512].rearrange("p o n -> p (o n)"),
                                       start=False, stop=c == DC - 1)
                    mm.then_inc(S["f_h_mm"], 1)

            def expert_block(j, b, k):
                more = not isinstance(j, int)
                e = expert_of(j)
                if more or j + 1 < NBLK:
                    e_next = expert_of(j + 1)
                for i in range(2):
                    pe.wait_ge(S["f_gelu"], 2 * j + i + 1)
                    at_least(pe, S[f"f_hT{i}_cp"], j)
                    for c in range(4):
                        n = 4 * i + c
                        transposed(pT[i][:, c * P:(c + 1) * P], f_h[:, n * P:(n + 1) * P],
                                   "f_hT_tr" if c == 3 else None)
                if more or j + 2 < NBLK:
                    in_T(j + 2, b, k + 1)
                if more or j + 1 < NBLK:
                    up(j + 1, 1 - b, e_next)
                pe.wait_ge(S["f_hT0_cp"], j + 1)
                pe.wait_ge(S["f_hT1_cp"], j + 1)
                if not more and j == 0:
                    pe.wait_ge(S["w2_ld"], 16 * E)
                at_least(pe, S["f_y_cp"], j)
                acc = p_out[b]
                pe.matmul(acc, f_sel[:, b, :], b_parts[:, F:F + D], start=True, stop=False)
                for c in range(FC):
                    mm = pe.matmul(acc, f_hT[:, c * P:(c + 1) * P],
                                   w2[:, bass.ds(e, 1), c, :].rearrange("p o n -> p (o n)"),
                                   start=False, stop=c == FC - 1)
                mm.then_inc(S["f_y_mm"], 1)

            in_T(0, 0, 0)
            in_T(1, 1, 0)
            pe.wait_ge(S["w1_ld"], 16 * E)
            pe.wait_ge(S["bias_split"], 6)
            up(0, 0, expert_of(0))
            run_blocks(pe, expert_block)


_INS = ["x", "ctx_1024", "L0_xattn_Wq", "L0_xattn_bq", "L0_xattn_Wk", "L0_xattn_bk", "L0_xattn_Wv", "L0_xattn_bv",
        "L0_xattn_Wr", "L0_xattn_br", "L0_attn_W_q", "L0_attn_W_k", "L0_attn_gain", "L0_attn_bias",
        "L0_attn_log_mix", "L0_attn_log_scale", "L0_ffn_Wr", "L0_ffn_W1", "L0_ffn_b1", "L0_ffn_W2", "L0_ffn_b2"]


def kernel(**inputs):
    import numpy as _np
    import concourse.bacc as _bacc
    from concourse import mybir as _mybir
    from concourse.bass_utils import run_bass_kernel_spmd as _run

    nc = _bacc.Bacc("TRN2", target_bir_lowering=False, num_devices=1)
    arrays, args = {}, {}
    for name in _INS:
        v = _np.ascontiguousarray(inputs[name])
        if not v.shape:
            v = v.reshape(1)
        arrays[f"in_{name}_dram"] = v
        args[name] = nc.dram_tensor(f"in_{name}_dram", v.shape, _mybir.dt.from_np(v.dtype), kind="ExternalInput").ap()
    o = nc.dram_tensor("out_0_dram", (B, T, D), F32, kind="ExternalOutput").ap()
    perceiver_layer(nc, args, o)
    r = _run(nc, [arrays], core_ids=[0])
    return r.results[0]["out_0_dram"]
```

```python
from contextlib import ExitStack

import numpy as np

import concourse.bass as bass
from concourse import mybir

F32 = mybir.dt.float32
BF16 = mybir.dt.bfloat16
I32 = mybir.dt.int32
ALU = mybir.AluOpType
ACT = mybir.ActivationFunctionType
AX = mybir.AxisListType

B, T, D, C = 64, 32, 256, 257
P = 128
DC = D // P
TOK = B * T
NG = TOK // P
BG = P // T
CF = C - 1
CC = CF // P
E, F = 8, 1024
FC = F // P
H = 32
NBLK = TOK // P + E - 1
VALUES = 6
TOP = 8

EPS = 1e-5
INV_2PI = float(1.0 / (2.0 * np.pi))
TWO_PI = 6.283185
ROUND = float(3 << 22)
LOWEST = -3.4028234663852886e38
PICKED = 3.0e38
UNPICKED = -1.0e9
OUTSIDE = -3.0e38

STAGES = 5
PEELED = 6


def at_least(eng, sem, count):
    if not isinstance(count, int) or count > 0:
        eng.wait_ge(sem, count)


def settle(eng, sem):
    eng.wait_ge(sem, 1)


def in_register(eng, count):
    return count if isinstance(count, int) else eng.to_reg(count)


def upto(value, most):
    return min(value, most) if isinstance(value, int) else value


def groups(k, parity, behind):
    g = 2 * k + parity - behind
    if isinstance(g, int) and not 0 <= g < NG:
        return None
    return g, (parity - behind) % 2, k + (parity - behind) // 2


def run_steps(eng, step):
    for s in range(PEELED):
        step(s // 2, s % 2)
    with eng.Fori(0, (NG - 2 - PEELED) // 4) as i:
        for k in (PEELED // 2 + 2 * i, PEELED // 2 + 2 * i + 1):
            step(k, 0)
            step(k, 1)
    for s in range(NG - 2, NG + STAGES - 1):
        step(s // 2, s % 2)


def run_blocks(eng, step):
    for j in range(2):
        step(j, j, 0)
    with eng.Fori(1, (NBLK - 3) // 2) as k:
        step(2 * k, 0, k)
        step(2 * k + 1, 1, k)
    for j in range(NBLK - 3, NBLK):
        step(j, j % 2, j // 2)


def perceiver_layer(nc, a, out):
    ctx = ExitStack()
    with ctx:
        def sb(name, shape, dt=F32):
            return ctx.enter_context(nc.sbuf_tensor(name, shape, dt))

        def ps(name):
            return ctx.enter_context(nc.psum_tensor(name, [P, 512], F32))

        def sem(name):
            return ctx.enter_context(nc.semaphore(name))

        xn3_dram = nc.dram_tensor("normal_tokens", [TOK, D], F32, kind="Internal").ap()
        x2_dram = nc.dram_tensor("residual_tokens", [TOK, D], F32, kind="Internal").ap()

        X = sb("X", [P, NG, D])
        XF = sb("XF", [P, 2 * F + 8 * D])
        spare = XF[:, 2 * F + 4 * D:]
        W1 = sb("W1", [P, E, DC, F])
        W2 = sb("W2", [P, E * FC * D])
        w2 = W2[:, :].rearrange("p (e c d) -> p e c d", e=E, c=FC)
        used = [0]

        def room(n):
            used[0] += n
            assert used[0] <= E * FC * D
            return W2[:, used[0] - n:used[0]]

        ctx_rows = [room(BG * CC * D).rearrange("p (j c d) -> p j c d", j=BG, c=CC) for _ in range(2)]
        ctx_T = room(DC * BG * CF).rearrange("p (c n) -> p c n", c=DC)
        khat = [room(DC * BG * C).rearrange("p (r j n) -> p r j n", r=DC, j=BG) for _ in range(2)]
        turns = [room(512) for _ in range(2)]
        frac = [room(512) for _ in range(2)]
        bias_rows = room(F + D)
        ctx_last = sb("ctx_last", [P, 2, D])

        ident = sb("ident", [P, P])
        tri = sb("tri", [P, P], BF16)
        ones = sb("ones", [P, P], BF16)
        causal = sb("causal", [P, P])
        pickable = sb("pickable", [P, P])
        unpicked = sb("unpicked", [P, P])
        minus_half = sb("minus_half", [P, 1])

        Wk, WkT, Wr = (room(DC * D).rearrange("p (c n) -> p c n", c=DC) for _ in range(3))
        Wkr = sb("Wkr", [P, DC, D])
        Wq = sb("Wq", [P, DC, D])
        Wv = sb("Wv", [P, DC, D])
        bq = sb("bq", [P, DC])
        bk = sb("bk", [P, DC])
        br = sb("br", [P, DC])
        bkr = sb("bkr", [P, DC])
        bv = sb("bv", [P, D])
        Wqk = sb("Wqk", [2 * H, D])
        WqkT = sb("WqkT", [P, DC, 2 * H])
        Wroute = sb("Wroute", [P, DC, E])
        gain = spare[:, 0:D]
        gbias = sb("gbias", [P, D])
        gain_msg = sb("gain_msg", [P, D])
        gain_self = sb("gain_self", [P, D])
        logs = sb("logs", [P, 2])
        sc = sb("sc", [P, 12])
        b_parts = sb("b_parts", [P, F + D], BF16)
        last_rows = spare[0:B, D:2 * D]
        last_T, last_turns, last_frac = (spare[:, 2 * D + i * P:2 * D + (i + 1) * P].rearrange("p (c n) -> p c n", c=DC)
                                         for i in range(3))
        khat_last = sb("khat_last", [P, DC, B])

        st1, st2, st3 = (sb(f"st{i}", [P, 6]) for i in (1, 2, 3))
        mv1, mv2, mv3 = (sb(f"mv{i}", [P, 2]) for i in (1, 2, 3))
        ve1, ve2, ve3 = (sb(f"ve{i}", [P, 1]) for i in (1, 2, 3))
        rs1, rs2, rs3 = (sb(f"rs{i}", [P, 1]) for i in (1, 2, 3))
        xn = sb("xn", [P, 2, D])
        xn3 = sb("xn3", [P, 2, D])
        xnT = sb("xnT", [P, DC, P])
        qT = sb("qT", [P, DC, P])
        nmaxA = sb("nmaxA", [P, 1])
        sumA = sb("sumA", [P, 1])
        rsumA = sb("rsumA", [P, 1])
        probs = sb("probs", [P, C])
        probsT = sb("probsT", [P, CC, P])
        o_norm = sb("o_norm", [P, D])
        o_T = sb("o_T", [P, DC, P])
        h = sb("h", [P, 2, D])
        hg = sb("hg", [P, 2, D])
        hT = sb("hT", [P, DC, P])
        qB = sb("qB", [H, P])
        kB = sb("kB", [H, P])
        simm = sb("simm", [P, P])
        top8 = sb("top8", [P, TOP])
        marked = sb("marked", [P, P])
        pick = sb("pick", [P, P], I32)
        scoreB = sb("scoreB", [P, 2, P])
        nmaxB = sb("nmaxB", [P, 2])
        expB = sb("expB", [P, P])
        sumB = sb("sumB", [P, 1])
        rsumB = sb("rsumB", [P, 1])
        att = sb("att", [P, P])
        attT = sb("attT", [P, P])
        y_msg = sb("y_msg", [P, D])
        y = sb("y", [P, D])
        gel = sb("gel", [P, D])
        xn3T = sb("xn3T", [P, DC, P])

        logits = sb("logits", [P, NG, E])
        rt = [t.rearrange("p (g e) -> p g e", g=NG) for t in (y_msg[:, 0:P], y_msg[:, P:2 * P], y[:, 0:P])]
        onehot = sb("onehot", [P, NG, E], BF16)
        per_token = sb("per_token", [P, 3, NG])
        p_max = sb("p_max", [P, NG])
        routed = hg[:].rearrange("p b n -> p (b n)")
        at = np.cumsum([0, 2 * NG, NG, NG, NG, VALUES * NBLK, 2 * NBLK]).tolist()
        slot_i = routed[:, at[0]:at[1]].bitcast(I32).rearrange("p (i n) -> p i n", i=2)
        slot_blk, slot_lane, p_rest = (routed[:, at[i]:at[i + 1]] for i in (1, 2, 3))
        by_slot = routed[:, at[4]:at[5]].rearrange("p (v n) -> p v n", v=VALUES)
        token = routed[:, at[5]:at[6]].rearrange("p (i n) -> p i n", i=2)
        values = sb("values", [P, NG, VALUES], BF16)
        lane = XF[:, 2 * F + 2 * D:2 * F + 2 * D + P]
        pad_row = sb("pad_row", [P, 1])
        token_i = sb("token_i", [P, 2, NBLK], I32)
        p_slot = sb("p_slot", [P, NBLK])
        in_at, x2_at, out_at = (sb(f"{n}_at", [P, 2], I32) for n in ("in", "x2", "out"))
        order_w = sb("order_w", [P, E])
        order_i = sb("order_i", [P, E], I32)
        cnt = sb("cnt", [P, E], BF16)
        blocks_i = sb("blocks_i", [P, 2, E], I32)
        blocks = sb("blocks", [P, E])
        ends = sb("ends", [P, E])
        starts = sb("starts", [P, E])
        one8 = sb("one8", [P, E])
        blk_i = sb("blk_i", [P, NBLK], I32)
        blk = sb("blk", [P, NBLK])
        past = gel[:, 0:NBLK * E].rearrange("p (n e) -> p n e", n=NBLK)
        expert = sb("expert", [P, NBLK])
        expert_i = sb("expert_i", [P, NBLK], I32)
        row_i = XF[:, 0:P].bitcast(I32)
        lane_i = XF[:, P:2 * P].bitcast(I32)
        few_i = XF[:, 2 * P:2 * P + 2 * NG + 1].bitcast(I32)
        in_lane = XF[:, 0:NG * P // 2].bitcast(BF16).rearrange("p (g n) -> p g n", g=NG)
        in_blk = XF[:, F:F + NG * VALUES * NBLK // 2].bitcast(BF16).rearrange("p (g v n) -> p g v n", g=NG, v=VALUES)
        row_e = sb("row_e", [P, P])
        f_sel = simm[:].bitcast(BF16).rearrange("p (b n) -> p b n", b=2)
        f_h = XF[:, 0:F]
        f_hT = XF[:, F:2 * F]
        f_in, f_inT, f_out, f_x2 = (XF[:, 2 * F + 2 * i * D:2 * F + 2 * (i + 1) * D].rearrange("p (b n) -> p b n", b=2)
                                    for i in range(4))

        pT = [ps("pT0"), ps("pT1")]
        pK = [ps("pK0"), ps("pK1")]
        b4, b5, b6, b7 = ps("b4"), ps("b5"), ps("b6"), ps("b7")
        p_score = b4[:, 0:C]
        p_pT = b4[:, 0:CF]
        p_attT = b4[:, 0:P]
        p_oT = b4[:, 0:D]
        p_xnT = b5[:, 0:D]
        p_sim = b5[:, 0:P]
        p_scoreB = b5[:, 0:P]
        p_msg = b5[:, 0:D]
        p_hT = b6[:, 0:D]
        p_qk = b6[0:2 * H, 0:P]
        p_q = b6[:, 0:D]
        p_a = b6[:, 0:D]
        p_o = b7[:, 0:D]
        p_xn3T = b7[:, 0:D]
        p_route = b7[:, 0:E]
        p_in = (b6[:, 0:D], b7[:, 0:D])
        p_out = (b4[:, 0:D], b5[:, 0:D])

        names = """consts wk_ld wqk_ld w_ld x_ld xrest_ld last_ld bias_ld logs_ld w1_ld w2_ld
            wkT_tr wkT_cp wkr_mm wkr_cp wqkT_tr wqkT_cp bkr_mm bkr_sum bkr_cp lastT_tr lastT_cp lastK_mm
            last_turn last_whole last_fr khat_last_r scal_act scal_dve gains bias_split
            ctxT_tr ctxT0_cp ctxT1_cp kproj turns_r whole_r frac_r khat_r klast_r
            st1_r mv1_r ve1_r rs1_r xn_r xb_r xnT_tr xnT_cp qproj q_r
            scoresA nmaxA_r probsA rsumA_r last_r pT_tr pT_cp pv o_r oT_tr oT_cp aproj x1_r
            st2_r mv2_r ve2_r rs2_r h_r hg_m hg_r hT_tr hT_cp sim_mm qk_mm qk_cp
            simm_r top_r marked_r pick_r base_r scoreB_mm selected nmaxB_r
            probsB rsumB_r att_r attT_tr attT_cp msg_mm ymsg_r y_r gelu_r x2_r
            st3_r mv3_r ve3_r rs3_r xn3_r xn3T_tr xn3T_cp route_mm logits_r
            route route_exp rank_mm in_blk_r in_lane_r in_values_r slot_mm token_r expert_r in_at_r x2_at_r out_at_r
            f_sel_r f_inT_tr f_inT_cp f_h_mm f_gelu f_hT_tr f_hT0_cp f_hT1_cp f_y_mm f_y_cp""".split()
        S = {n: sem(n) for n in names}
        ctx_ld = [sem("ctx_ld0"), sem("ctx_ld1")]
        last_row_ld = [sem("last_row_ld0"), sem("last_row_ld1")]
        f_in_ld = [sem("f_in_ld0"), sem("f_in_ld1")]
        f_y_st = [sem("f_y_st0"), sem("f_y_st1")]
        f_x2_ld = [sem("f_x2_ld0"), sem("f_x2_ld1")]
        kept = [sem("kept0"), sem("kept1")]

        block = ctx.enter_context(nc.Block())
        CTX_LOADS = CC
        W_LOADS = 7
        made_at = {}

        x_v = a["x"].rearrange("(g j) t d -> (j t) g d", j=BG)
        out_v = out.rearrange("b t d -> (b t) d")
        c_in = a["ctx_1024"]

        def col(v):
            return v.rearrange("(c p) -> p c", p=P)

        def rows(w):
            return w.rearrange("(c p) n -> p c n", p=P)

        def group_of(t, g):
            return t[:, bass.ds(g, 1), :].rearrange("p o d -> p (o d)")

        @block.gpsimd
        def _(pool):
            n = [0]

            def made(ins):
                n[0] += 1
                ins.then_inc(S["consts"], 1)
                pool.wait_ge(S["consts"], n[0])

            def keep(t, pattern, base, mult, cmp, fill):
                made(pool.affine_select(t, t, pattern, cmp, fill, base=base, channel_multiplier=mult))

            def rstd(g, mv, ve, rs, mv_r, ve_r, rs_r):
                count = in_register(pool, g + 1)
                settle(pool, S["consts"])
                pool.wait_ge(S[mv_r], count)
                pool.tensor_scalar(ve[:], mv[:, 1:2], EPS, None, ALU.add).then_inc(S[ve_r], 1)
                pool.wait_ge(S[ve_r], g + 1)
                pool.tensor_tensor(rs[:], ve[:], minus_half[:], ALU.pow).then_inc(S[rs_r], 1)

            def add_bv(g):
                pool.wait_ge(S["xn_r"], g + 1)
                pool.tensor_tensor(group_of(X, g), group_of(X, g), bv[:], ALU.add).then_inc(S["xb_r"], 1)

            made(pool.memset(ident[:], 0.0))
            keep(ident[:], [[-1, P]], 0, 1, ALU.not_equal, 1.0)
            made_at["ident"] = n[0]
            made(pool.memset(minus_half[:], -0.5))
            made(pool.memset(bias_rows, 0.0))
            made_at["bias_rows"] = n[0]
            rstd(0, mv1, ve1, rs1, "mv1_r", "ve1_r", "rs1_r")
            made(pool.memset(ones[:], 1.0))
            made(pool.memset(tri[:], 1.0))
            keep(tri[:], [[1, P]], 0, -1, ALU.is_gt, 0.0)
            made(pool.iota(order_i[:], [[-1, E]], base=E, channel_multiplier=0))
            made(pool.tensor_copy(order_w[:], order_i[:]))
            made(pool.iota(blk_i[:], [[1, NBLK]], base=0, channel_multiplier=0))
            made(pool.tensor_copy(blk[:], blk_i[:]))
            made(pool.memset(one8[:], 1.0))
            for q in range(0, P, 32):
                made(pool.iota(row_i[q:q + 32, :], [[0, P]], base=0, channel_multiplier=1))
            made(pool.tensor_copy(row_e[:], row_i))
            made(pool.iota(lane_i, [[1, P]], base=0, channel_multiplier=0))
            made(pool.tensor_copy(lane, lane_i))
            made(pool.iota(few_i[:, 0:NG], [[1, NG]], base=0, channel_multiplier=0))
            made(pool.tensor_copy(values[:, :, 0], few_i[:, 0:NG]))
            made(pool.iota(few_i[:, NG:2 * NG], [[0, NG]], base=0, channel_multiplier=1))
            made(pool.tensor_copy(values[:, :, 1], few_i[:, NG:2 * NG]))
            made(pool.memset(values[:, :, 2], 1.0))
            made(pool.iota(few_i[:, 2 * NG:], [[0, 1]], base=2 * TOK, channel_multiplier=1))
            made(pool.tensor_copy(pad_row[:], few_i[:, 2 * NG:]))
            made_at["routing"] = n[0]
            pool.wait_ge(S["w_ld"], 16 * W_LOADS)
            add_bv(0)

            def late_constants():
                pool.wait_ge(S["scal_dve"], 3)
                pool.tensor_scalar(gain_msg[:], gain, sc[:, 3:4], None, ALU.mult).then_inc(S["gains"], 1)
                pool.tensor_scalar(gain_self[:], gain, sc[:, 2:3], None, ALU.mult).then_inc(S["gains"], 1)
                for t, start, fill in ((causal, 0.0, LOWEST), (pickable, PICKED, 1.0), (unpicked, UNPICKED, OUTSIDE)):
                    v = t[:].rearrange("p (j n) -> p j n", j=BG)
                    made(pool.memset(t[:], start))
                    keep(v, [[-T, BG], [0, T]], 0, 1, ALU.is_ge, fill)
                    keep(v, [[T, BG], [0, T]], T - 1, -1, ALU.is_ge, fill)
                    if t is not unpicked:
                        keep(v, [[-T, BG], [-1, T]], 0, 1, ALU.is_gt, fill)
                made_at["masks"] = n[0]
                pool.wait_ge(S["gains"], 2)

            def step(k, parity):
                now, one, two, three, four, coming = (groups(k, parity, n) for n in (0, 1, 2, 3, 4, -1))
                if now:
                    g, b, _ = now
                    if isinstance(g, int) and g == 0:
                        pool.wait_ge(S["khat_last_r"], 1)
                    settle(pool, S["consts"])
                    at_least(pool, S["scoresA"], g - 1)
                    pool.tensor_copy(khat[b][:, :, :, CF], khat_last[:, :, bass.ds(g * BG, BG)]
                                     ).then_inc(S["klast_r"], 1)
                if two:
                    rstd(two[0], mv2, ve2, rs2, "mv2_r", "ve2_r", "rs2_r")
                if two:
                    g, b, _ = two
                    count = in_register(pool, g - 1)
                    settle(pool, S["consts"])
                    at_least(pool, S["probsB"], count)
                    pool.tensor_copy(scoreB[:, b, :], unpicked[:]).then_inc(S["base_r"], 1)
                if coming:
                    rstd(coming[0], mv1, ve1, rs1, "mv1_r", "ve1_r", "rs1_r")
                if one:
                    g, b, q = one
                    counts = [in_register(pool, n) for n in (g + 1, 16 * BG * (q + 1))]
                    settle(pool, S["consts"])
                    at_least(pool, S["oT_tr"], g)
                    pool.wait_ge(last_row_ld[b], counts[1])
                    pool.wait_ge(S["rsumA_r"], counts[0])
                    pool.tensor_scalar(o_norm[:], ctx_last[:, b, :], probs[:, CF:C], rsumA[:, 0:1], ALU.mult, ALU.mult
                                       ).then_inc(S["last_r"], 1)
                if four:
                    rstd(four[0], mv3, ve3, rs3, "mv3_r", "ve3_r", "rs3_r")
                if coming:
                    add_bv(coming[0])
                if two:
                    g, b, _ = two
                    pool.wait_ge(S["h_r"], g + 1)
                    at_least(pool, S["y_r"], g - 1)
                    pool.tensor_tensor(hg[:, b, :], h[:, b, :], gain_self[:], ALU.mult).then_inc(S["hg_m"], 1)
                    pool.wait_ge(S["hg_m"], g + 1)
                    pool.tensor_tensor(hg[:, b, :], hg[:, b, :], gbias[:], ALU.add).then_inc(S["hg_r"], 1)
                if isinstance(k, int) and 2 * k + parity == 0:
                    late_constants()

            run_steps(pool, step)

            for half in range(2):
                gs = slice(half * NG // 2, (half + 1) * NG // 2)
                pool.wait_ge(S["in_blk_r"], half + 1)
                for i in (0, 1, 3, 4, 5):
                    pool.tensor_tensor(in_blk[:, gs, i, :], in_blk[:, gs, 2, :],
                                       values[:, gs, i:i + 1].to_broadcast([P, NG // 2, NBLK]), ALU.mult
                                       ).then_inc(S["in_values_r"], 1)

            def next_in(j, b):
                count = in_register(pool, j - 1)
                settle(pool, S["consts"])
                at_least(pool, S["f_inT_tr"], count)
                pool.tensor_copy(in_at[:, b:b + 1], token_i[:, 0, bass.ds(j, 1)]).then_inc(S["in_at_r"], 1)
                count = in_register(pool, j + 1)
                settle(pool, S["consts"])
                pool.wait_ge(S["in_at_r"], count)
                pool.indirect_dma_start(f_in[:, b, :], None, xn3_dram,
                                        bass.IndirectOffsetOnAxis(ap=in_at[:, b:b + 1], axis=0)
                                        ).then_inc(f_in_ld[b], 16)

            def next_x2(j, b):
                count = in_register(pool, j - 1)
                settle(pool, S["consts"])
                at_least(pool, S["f_y_cp"], count)
                pool.tensor_copy(x2_at[:, b:b + 1], token_i[:, 0, bass.ds(j, 1)]).then_inc(S["x2_at_r"], 1)
                count = in_register(pool, j + 1)
                settle(pool, S["consts"])
                pool.wait_ge(S["x2_at_r"], count)
                pool.indirect_dma_start(f_x2[:, b, :], None, x2_dram,
                                        bass.IndirectOffsetOnAxis(ap=x2_at[:, b:b + 1], axis=0)
                                        ).then_inc(f_x2_ld[b], 16)

            def store(j, b):
                count = in_register(pool, j + 1)
                settle(pool, S["consts"])
                pool.wait_ge(S["f_y_cp"], count)
                pool.tensor_copy(out_at[:, b:b + 1], token_i[:, 1, bass.ds(j, 1)]).then_inc(S["out_at_r"], 1)
                count = in_register(pool, j + 1)
                settle(pool, S["consts"])
                pool.wait_ge(S["out_at_r"], count)
                pool.indirect_dma_start(out_v, bass.IndirectOffsetOnAxis(ap=out_at[:, b:b + 1], axis=0),
                                        f_out[:, b, :], None, bounds_check=TOK - 1, oob_is_err=False
                                        ).then_inc(f_y_st[b], 16)

            def block_io(j, b, k):
                more = not isinstance(j, int)
                if more or j + 2 < NBLK:
                    next_in(j + 2, b)
                if more or j > 0:
                    store(j - 1, 1 - b)
                    if more or j + 1 < NBLK:
                        next_x2(j + 1, 1 - b)

            pool.wait_ge(S["token_r"], 1)
            for b in range(2):
                pool.wait_ge(kept[b], 32 * NG // 2)
            for b in range(2):
                next_in(b, b)
            pool.wait_ge(S["token_r"], 2)
            for b in range(2):
                next_x2(b, b)
            run_blocks(pool, block_io)
            store(NBLK - 1, (NBLK - 1) % 2)
            pool.wait_ge(f_y_st[0], 16 * ((NBLK + 1) // 2))
            pool.wait_ge(f_y_st[1], 16 * (NBLK // 2))

        @block.sync
        def _(sp):
            def load_ctx(g, b):
                for i in range(CC):
                    sp.dma_start(ctx_rows[b][:, :, i, :],
                                 c_in[bass.ds(g * BG, BG), i * P:(i + 1) * P, :].rearrange("j p d -> p j d")
                                 ).then_inc(ctx_ld[b], 16)

            def load_last(g, b):
                for j in range(BG):
                    sp.dma_start(ctx_last[j * T:(j + 1) * T, b, :],
                                 c_in[bass.ds(g * BG + j, 1), CF, :].to_broadcast([T, D])).then_inc(last_row_ld[b], 16)

            sp.dma_start(Wk, rows(a["L0_xattn_Wk"])).then_inc(S["wk_ld"], 16)
            sp.dma_start(Wr, rows(a["L0_xattn_Wr"])).then_inc(S["wk_ld"], 16)
            load_ctx(0, 0)
            sp.dma_start(last_rows, c_in[:, CF, :]).then_inc(S["last_ld"], 16)
            load_ctx(1, 1)
            sp.wait_ge(S["w_ld"], 16 * W_LOADS)
            for g in range(2):
                load_last(g, g)
            sp.dma_start(X[:, 2:NG, :], x_v[:, 2:NG, :]).then_inc(S["xrest_ld"], 16)
            sp.wait_ge(S["consts"], made_at["bias_rows"])
            for i in range(3):
                at = slice(32 * i, 32 * i + E)
                sp.dma_start(bias_rows[at, 0:F], a["L0_ffn_b1"]).then_inc(S["bias_ld"], 16)
                sp.dma_start(bias_rows[at, F:F + D], a["L0_ffn_b2"]).then_inc(S["bias_ld"], 16)

            def load_w1(e):
                sp.dma_start(W1[:, bass.ds(e, 1)].rearrange("p e c f -> p (e c) f"),
                             a["L0_ffn_W1"][bass.ds(e, 1)].rearrange("e (c p) f -> p (e c) f", p=P)
                             ).then_inc(S["w1_ld"], 16)

            def keep(g, b):
                sp.wait_ge(S["xn3_r"], g + 1)
                sp.dma_start(xn3_dram[bass.ds(g * P, P), :], xn3[:, b, :]).then_inc(kept[b], 16)
                sp.dma_start(x2_dram[bass.ds(g * P, P), :], group_of(X, g)).then_inc(kept[b], 16)

            def next_group(g, b):
                sp.wait_ge(S["pv"], g - 1)
                load_ctx(g, b)
                sp.wait_ge(S["last_r"], g - 1)
                load_last(g, b)
                if not isinstance(g, int) or g >= 5:
                    keep(g - 5, 1 - b)

            for g in range(2, PEELED):
                next_group(g, g % 2)
                if g % 2:
                    load_w1(g // 2 - 1)
            with sp.Fori(PEELED // 2, NG // 2) as k:
                for b in range(2):
                    next_group(2 * k + b, b)
                load_w1(k - 1)
            load_w1(E - 1)
            for g in range(NG - 5, NG - 3):
                keep(g, g % 2)
            sp.wait_ge(S["pv"], NG)
            sp.wait_ge(S["bias_split"], 6)
            for e in range(E):
                sp.dma_start(w2[:, e], rows(a["L0_ffn_W2"][e])).then_inc(S["w2_ld"], 16)
                if e in (2, 4, 6):
                    g = NG - 4 + e // 2
                    keep(g, g % 2)

        @block.vector
        def _(v):
            def stats(g, st, st_r):
                v.bn_stats(st[:], group_of(X, g)).then_inc(S[st_r], 1)

            def moments(g, st, mv, st_r, mv_r):
                count = in_register(v, g + 1)
                settle(v, S["consts"])
                v.wait_ge(S[st_r], count)
                v.bn_aggr(mv[:], st[:]).then_inc(S[mv_r], 1)

            def normal(g, dst, mv, rs, rs_r, done):
                v.wait_ge(S[rs_r], g + 1)
                v.tensor_scalar(dst, group_of(X, g), mv[:, 0:1], rs[:, 0:1], ALU.subtract, ALU.mult
                                ).then_inc(S[done], 1)

            def stats_x(g):
                if isinstance(g, int) and g in (0, 2):
                    v.wait_ge(S["x_ld" if g == 0 else "xrest_ld"], 16)
                settle(v, S["consts"])
                at_least(v, S["rs1_r"], g)
                stats(g, st1, "st1_r")

            def normal_x(g, b):
                at_least(v, S["xnT_tr"], g - 1)
                normal(g, xn[:, b, :], mv1, rs1, "rs1_r", "xn_r")

            v.wait_ge(S["wkT_tr"], 1)
            v.tensor_copy(WkT.rearrange("p c n -> p (c n)"), pT[0][:]).then_inc(S["wkT_cp"], 1)
            stats_x(0)
            moments(0, st1, mv1, "st1_r", "mv1_r")
            v.wait_ge(S["wkr_mm"], 1)
            v.tensor_scalar(Wkr[:].rearrange("p c n -> p (c n)"), pK[0][:], INV_2PI, None, ALU.mult
                            ).then_inc(S["wkr_cp"], 1)
            v.wait_ge(S["bkr_mm"], 1)
            v.tensor_tensor(bkr[:], b4[:, 0:DC], br[:], ALU.add).then_inc(S["bkr_sum"], 1)
            v.wait_ge(S["bkr_sum"], 1)
            v.tensor_scalar(bkr[:], bkr[:], INV_2PI, 0.25, ALU.mult, ALU.add).then_inc(S["bkr_cp"], 1)
            v.wait_ge(S["wqkT_tr"], 1)
            v.tensor_copy(WqkT[:].rearrange("p c n -> p (c n)"), b5[:, 0:DC * 2 * H]).then_inc(S["wqkT_cp"], 1)
            v.wait_ge(S["lastT_tr"], 1)
            v.tensor_copy(last_T.rearrange("p c n -> p (c n)"), b7[:, 0:DC * B]).then_inc(S["lastT_cp"], 1)
            normal_x(0, 0)
            v.wait_ge(S["lastK_mm"], 1)
            v.wait_ge(S["bkr_cp"], 1)
            for r in range(DC):
                v.tensor_scalar(last_turns[:, r, :], b6[:, r * B:(r + 1) * B], bkr[:, r:r + 1], None, ALU.add
                                ).then_inc(S["last_turn"], 1)
            v.wait_ge(S["last_turn"], 2)
            v.tensor_scalar(last_frac, last_turns, ROUND, ROUND, ALU.add, ALU.subtract
                            ).then_inc(S["last_whole"], 1)
            v.wait_ge(S["last_whole"], 1)
            v.tensor_tensor(last_frac, last_turns, last_frac, ALU.subtract).then_inc(S["last_fr"], 1)
            v.wait_ge(S["scal_act"], 1)
            v.tensor_scalar(sc[:, 1:2], sc[:, 0:1], 1.0, None, ALU.add).then_inc(S["scal_dve"], 1)
            v.wait_ge(S["scal_dve"], 1)
            v.reciprocal(sc[:, 2:3], sc[:, 1:2]).then_inc(S["scal_dve"], 1)
            v.wait_ge(S["scal_dve"], 2)
            v.tensor_scalar(sc[:, 3:4], sc[:, 2:3], -1.0, 1.0, ALU.mult, ALU.add).then_inc(S["scal_dve"], 1)
            v.tensor_scalar(sc[:, 8:9], logs[:, 1:2], 0.0, 0.01, ALU.max, ALU.add).then_inc(S["scal_dve"], 1)
            v.wait_ge(S["scal_act"], 4)
            v.wait_ge(S["scal_dve"], 4)
            v.tensor_tensor(sc[:, 9:10], sc[:, 7:8], sc[:, 8:9], ALU.add).then_inc(S["scal_dve"], 1)
            v.wait_ge(S["scal_dve"], 5)

            def whole(g, u):
                b = u % 2
                v.wait_ge(S["turns_r"], 4 * g + u + 1)
                at_least(v, S["khat_r"], 4 * g + u - 1)
                v.tensor_scalar(frac[b], turns[b], ROUND, ROUND, ALU.add, ALU.subtract).then_inc(S["whole_r"], 1)

            def fraction(g, u):
                b = u % 2
                v.wait_ge(S["whole_r"], 4 * g + u + 1)
                v.tensor_tensor(frac[b], turns[b], frac[b], ALU.subtract).then_inc(S["frac_r"], 1)

            def ctx_T_copy(g, half):
                v.wait_ge(S["ctxT_tr"], 4 * g + 2 * half + 1)
                at_least(v, S["kproj"], 4 * g + 2 * half - 2)
                v.tensor_copy(ctx_T[:, 0, half * 512:(half + 1) * 512], pT[0][:]).then_inc(S["ctxT0_cp"], 1)

            def split_biases(third):
                def part(rows, n):
                    v.tensor_copy(b_parts[rows, :], bias_rows[rows, :]).then_inc(S["bias_split"], 1)
                    v.wait_ge(S["bias_split"], n)

                def rest(rows, n):
                    v.tensor_tensor(bias_rows[rows, :], bias_rows[rows, :], b_parts[rows, :], ALU.subtract
                                    ).then_inc(S["bias_split"], 1)
                    v.wait_ge(S["bias_split"], n)

                if third == 0:
                    v.wait_ge(S["bias_ld"], 6 * 16)
                    part(slice(0, P), 1)
                    rest(slice(0, P), 2)
                elif third == 1:
                    part(slice(32, 64), 3)
                    part(slice(64, P), 4)
                else:
                    rest(slice(64, P), 5)
                    part(slice(64, P), 6)

            def step(k, parity):
                now, one, two, three, four, coming = (groups(k, parity, n) for n in (0, 1, 2, 3, 4, -1))
                if now:
                    ctx_T_copy(now[0], 0)
                if two:
                    g, b, _ = two
                    settle(v, S["consts"])
                    v.wait_ge(S["x1_r"], g + 1)
                    at_least(v, S["rs2_r"], g)
                    stats(g, st2, "st2_r")
                if now:
                    g, b, _ = now
                    v.wait_ge(S["xnT_tr"], g + 1)
                    at_least(v, S["qproj"], g)
                    v.tensor_copy(xnT[:].rearrange("p c n -> p (c n)"), p_xnT).then_inc(S["xnT_cp"], 1)
                if two:
                    moments(two[0], st2, mv2, "st2_r", "mv2_r")
                if four:
                    g, b, _ = four
                    v.wait_ge(S["ymsg_r"], g + 1)
                    v.wait_ge(S["hg_r"], g + 1)
                    at_least(v, S["gelu_r"], g)
                    v.tensor_tensor(y[:], y_msg[:], hg[:, b, :], ALU.add).then_inc(S["y_r"], 1)
                if one:
                    g, b, _ = one
                    v.wait_ge(S["scoresA"], g + 1)
                    v.tensor_reduce(nmaxA[:], p_score, AX.X, ALU.max, negate=True).then_inc(S["nmaxA_r"], 1)
                if two:
                    g, b, _ = two
                    at_least(v, S["msg_mm"], g - 1)
                    at_least(v, S["hg_m"], g - 1)
                    normal(g, h[:, b, :], mv2, rs2, "rs2_r", "h_r")
                if three:
                    g, b, _ = three
                    v.wait_ge(S["probsB"], g + 1)
                    v.reciprocal(rsumB[:], sumB[:]).then_inc(S["rsumB_r"], 1)
                if coming:
                    stats_x(coming[0])
                if three:
                    g, b, _ = three
                    v.wait_ge(S["rsumB_r"], g + 1)
                    at_least(v, S["attT_tr"], g)
                    v.tensor_scalar(att[:], expB[:], rsumB[:, 0:1], 0.0, ALU.mult, ALU.max).then_inc(S["att_r"], 1)
                if coming:
                    moments(coming[0], st1, mv1, "st1_r", "mv1_r")
                if one:
                    g, b, _ = one
                    v.wait_ge(S["probsA"], g + 1)
                    v.reciprocal(rsumA[:], sumA[:]).then_inc(S["rsumA_r"], 1)
                if coming:
                    normal_x(coming[0], coming[1])
                if isinstance(k, int) and 1 <= 2 * k + parity <= 3:
                    split_biases(2 * k + parity - 1)
                if four:
                    g, b, _ = four
                    v.wait_ge(S["gelu_r"], g + 1)
                    v.scalar_tensor_tensor(group_of(X, g), gel[:], sc[:, 9:10], group_of(X, g), ALU.mult, ALU.add
                                           ).then_inc(S["x2_r"], 1)
                    settle(v, S["consts"])
                    v.wait_ge(S["x2_r"], g + 1)
                    at_least(v, S["rs3_r"], g)
                    stats(g, st3, "st3_r")
                if one:
                    g, b, _ = one
                    v.wait_ge(S["pT_tr"], g + 1)
                    at_least(v, S["pv"], g)
                    v.tensor_copy(probsT[:].rearrange("p c n -> p (c n)"), p_pT).then_inc(S["pT_cp"], 1)
                if four:
                    moments(four[0], st3, mv3, "st3_r", "mv3_r")
                if two:
                    g, b, _ = two
                    if isinstance(g, int) and g == 0:
                        v.wait_ge(S["consts"], made_at["masks"])
                    v.wait_ge(S["sim_mm"], g + 1)
                    v.tensor_tensor(simm[:], p_sim, causal[:], ALU.add).then_inc(S["simm_r"], 1)
                if now:
                    whole(now[0], 0)
                if two:
                    g, b, _ = two
                    settle(v, S["consts"])
                    v.wait_ge(S["simm_r"], g + 1)
                    v.max(top8[:], simm[:]).then_inc(S["top_r"], 1)
                if now:
                    fraction(now[0], 0)
                if two:
                    g, b, _ = two
                    settle(v, S["consts"])
                    v.wait_ge(S["top_r"], g + 1)
                    v.match_replace(marked[:], top8[:], simm[:], PICKED).then_inc(S["marked_r"], 1)
                if now:
                    whole(now[0], 1)
                    ctx_T_copy(now[0], 1)
                if two:
                    g, b, _ = two
                    v.wait_ge(S["marked_r"], g + 1)
                    v.tensor_tensor(pick[:], marked[:], pickable[:], ALU.is_equal).then_inc(S["pick_r"], 1)
                if now:
                    fraction(now[0], 1)
                if three:
                    g, b, _ = three
                    v.wait_ge(S["attT_tr"], g + 1)
                    at_least(v, S["msg_mm"], g)
                    v.tensor_copy(attT[:], p_attT).then_inc(S["attT_cp"], 1)
                if one:
                    g, b, _ = one
                    v.wait_ge(S["pv"], g + 1)
                    v.wait_ge(S["last_r"], g + 1)
                    v.scalar_tensor_tensor(o_norm[:], p_o, rsumA[:, 0:1], o_norm[:], ALU.mult, ALU.add
                                           ).then_inc(S["o_r"], 1)
                if two:
                    g, b, _ = two
                    settle(v, S["consts"])
                    v.wait_ge(S["scoreB_mm"], g + 1)
                    v.wait_ge(S["base_r"], g + 1)
                    v.wait_ge(S["pick_r"], g + 1)
                    v.copy_predicated(scoreB[:, b, :], pick[:], p_scoreB).then_inc(S["selected"], 1)
                if four:
                    g, b, _ = four
                    at_least(v, kept[b], 32 * four[2])
                    at_least(v, S["xn3T_tr"], g)
                    normal(g, xn3[:, b, :], mv3, rs3, "rs3_r", "xn3_r")
                if two:
                    g, b, _ = two
                    v.wait_ge(S["selected"], g + 1)
                    v.tensor_reduce(nmaxB[:, b:b + 1], scoreB[:, b, :], AX.X, ALU.max, negate=True
                                    ).then_inc(S["nmaxB_r"], 1)
                if one:
                    g, b, _ = one
                    v.wait_ge(S["oT_tr"], g + 1)
                    at_least(v, S["aproj"], g)
                    v.tensor_copy(o_T[:].rearrange("p c n -> p (c n)"), p_oT).then_inc(S["oT_cp"], 1)
                if now:
                    whole(now[0], 2)
                    fraction(now[0], 2)
                    whole(now[0], 3)
                    fraction(now[0], 3)
                if three:
                    g, b, _ = three
                    v.wait_ge(S["msg_mm"], g + 1)
                    v.tensor_tensor(y_msg[:], p_msg, gain_msg[:], ALU.mult).then_inc(S["ymsg_r"], 1)
                if one:
                    g, b, _ = one
                    v.wait_ge(S["aproj"], g + 1)
                    v.wait_ge(S["xb_r"], g + 1)
                    v.tensor_tensor(group_of(X, g), p_a, group_of(X, g), ALU.add).then_inc(S["x1_r"], 1)
                if four:
                    g, b, _ = four
                    v.wait_ge(S["route_mm"], g + 1)
                    v.tensor_copy(group_of(logits, g), p_route).then_inc(S["logits_r"], 1)

            run_steps(v, step)

            n = [0]

            def then(ins):
                n[0] += 1
                ins.then_inc(S["route"], 1)
                v.wait_ge(S["route"], n[0])

            def per_group(t):
                return t.rearrange("p (g o) -> p g o", o=1).to_broadcast([P, NG, E])

            def per_expert(t):
                return t.rearrange("p (o e) -> p o e", o=1).to_broadcast([P, NG, E])

            v.wait_ge(S["consts"], made_at["routing"])
            v.wait_ge(S["logits_r"], NG)
            then(v.tensor_reduce(per_token[:, 0, :], logits[:], AX.X, ALU.max))
            then(v.tensor_tensor(rt[0], logits[:], per_group(per_token[:, 0, :]), ALU.subtract))
            made_at["route_sub"] = n[0]
            v.wait_ge(S["route_exp"], 1)
            then(v.tensor_reduce(per_token[:, 2, :], rt[1], AX.X, ALU.max))
            then(v.tensor_tensor(rt[0], rt[1], per_group(per_token[:, 2, :]), ALU.is_equal))
            then(v.tensor_tensor(rt[2], rt[0], per_expert(order_w[:]), ALU.mult))
            then(v.tensor_reduce(per_token[:, 0, :], rt[2], AX.X, ALU.max))
            then(v.tensor_tensor(onehot[:], rt[2], per_group(per_token[:, 0, :]), ALU.is_equal))
            then(v.tensor_reduce(starts[:], onehot[:].rearrange("p g e -> p e g"), AX.X, ALU.add))
            then(v.tensor_copy(cnt[:], starts[:]))
            made_at["onehot"] = n[0]
            then(v.tensor_reduce(per_token[:, 1, :], rt[1], AX.X, ALU.add))
            then(v.reciprocal(per_token[:, 0, :], per_token[:, 1, :]))
            then(v.tensor_tensor(p_max[:], per_token[:, 0, :], per_token[:, 2, :], ALU.mult))
            then(v.tensor_copy(values[:, :, 3], p_max[:]))
            then(v.tensor_tensor(p_rest, p_max[:], values[:, :, 3], ALU.subtract))
            then(v.tensor_copy(values[:, :, 4], p_rest))
            then(v.tensor_tensor(p_rest, p_rest, values[:, :, 4], ALU.subtract))
            then(v.tensor_copy(values[:, :, 5], p_rest))
            v.wait_ge(S["rank_mm"], 1)
            then(v.tensor_scalar(blocks_i[:, 0, :], b7[:, 0:E], float(P - 1), None, ALU.add))
            then(v.tensor_scalar(blocks_i[:, 1, :], blocks_i[:, 0, :], 7, None, ALU.logical_shift_right))
            then(v.tensor_copy(blocks[:], blocks_i[:, 1, :]))
            then(v.tensor_tensor_scan(ends[:], one8[:], blocks[:], 0.0, ALU.mult, ALU.add))
            then(v.tensor_tensor(starts[:], ends[:], blocks[:], ALU.subtract))
            then(v.tensor_scalar(starts[:], starts[:], float(P), None, ALU.mult))
            then(v.tensor_tensor(rt[0], b6[:, 0:NG * E].rearrange("p (g e) -> p g e", g=NG),
                                 per_expert(starts[:]), ALU.add))
            then(v.tensor_tensor(rt[2], rt[0], onehot[:], ALU.mult))
            then(v.tensor_reduce(per_token[:, 1, :], rt[2], AX.X, ALU.add))
            then(v.tensor_copy(slot_i[:, 0, :], per_token[:, 1, :]))
            then(v.tensor_scalar(slot_i[:, 1, :], slot_i[:, 0, :], 7, None, ALU.logical_shift_right))
            then(v.tensor_copy(slot_blk, slot_i[:, 1, :]))
            then(v.scalar_tensor_tensor(slot_lane, slot_blk, float(-P), per_token[:, 1, :], ALU.mult, ALU.add))

            def each_blk(t, gs):
                return t[:, gs].rearrange("p (g o) -> p g o", o=1).to_broadcast([P, NG // 2, NBLK])

            halves = [slice(half * NG // 2, (half + 1) * NG // 2) for half in range(2)]
            for gs in halves:
                v.tensor_tensor(in_blk[:, gs, 2, :],
                                blk[:].rearrange("p (o n) -> p o n", o=1).to_broadcast([P, NG // 2, NBLK]),
                                each_blk(slot_blk, gs), ALU.is_equal).then_inc(S["in_blk_r"], 1)
            for gs in halves:
                v.tensor_tensor(in_lane[:, gs, :],
                                lane.rearrange("p (o n) -> p o n", o=1).to_broadcast([P, NG // 2, P]),
                                slot_lane[:, gs].rearrange("p (g o) -> p g o", o=1).to_broadcast([P, NG // 2, P]),
                                ALU.is_equal).then_inc(S["in_lane_r"], 1)
            then(v.tensor_tensor(past, blk[:].rearrange("p (n o) -> p n o", o=1).to_broadcast([P, NBLK, E]),
                                 ends[:].rearrange("p (o e) -> p o e", o=1).to_broadcast([P, NBLK, E]),
                                 ALU.is_ge))
            then(v.tensor_reduce(expert[:], past, AX.X, ALU.add))
            then(v.tensor_scalar(expert[:], expert[:], float(E - 1), None, ALU.min))
            v.tensor_copy(expert_i[:], expert[:]).then_inc(S["expert_r"], 1)
            v.wait_ge(S["slot_mm"], 1)
            then(v.tensor_copy(by_slot.rearrange("p v n -> p (v n)"), b6[:, 0:VALUES * NBLK]))
            then(v.scalar_tensor_tensor(token[:, 0, :], by_slot[:, 0, :], float(P), by_slot[:, 1, :],
                                        ALU.mult, ALU.add))
            v.tensor_copy(token_i[:, 0, :], token[:, 0, :]).then_inc(S["token_r"], 1)
            then(v.tensor_scalar(token[:, 1, :], by_slot[:, 2, :], -1.0, 1.0, ALU.mult, ALU.add))
            then(v.scalar_tensor_tensor(token[:, 1, :], token[:, 1, :], pad_row[:, 0:1], token[:, 0, :],
                                        ALU.mult, ALU.add))
            v.tensor_copy(token_i[:, 1, :], token[:, 1, :]).then_inc(S["token_r"], 1)
            then(v.tensor_tensor(p_slot[:], by_slot[:, 3, :], by_slot[:, 4, :], ALU.add))
            then(v.tensor_tensor(p_slot[:], p_slot[:], by_slot[:, 5, :], ALU.add))

            def select(j, b):
                v.tensor_scalar(f_sel[:, b, :], row_e[:], expert[:, bass.ds(j, 1)], None, ALU.is_equal
                                ).then_inc(S["f_sel_r"], 1)

            def in_T(j, b):
                v.wait_ge(S["f_inT_tr"], j + 1)
                at_least(v, S["f_h_mm"], 2 * (j - 1))
                v.tensor_copy(f_inT[:, b, :], p_in[b]
                              ).then_inc(S["f_inT_cp"], 1)

            def expert_block(j, b, k):
                v.wait_ge(S["f_hT_tr"], 2 * j + 1)
                at_least(v, S["f_y_mm"], j)
                v.tensor_copy(f_hT[:, 0:512], pT[0][:]).then_inc(S["f_hT0_cp"], 1)
                if not isinstance(j, int) or j + 2 < NBLK:
                    in_T(j + 2, b)
                v.wait_ge(S["f_y_mm"], j + 1)
                v.wait_ge(f_x2_ld[b], 16 * (k + 1))
                at_least(v, f_y_st[b], 16 * k)
                v.scalar_tensor_tensor(f_out[:, b, :], p_out[b], p_slot[:, bass.ds(j, 1)], f_x2[:, b, :],
                                       ALU.mult, ALU.add).then_inc(S["f_y_cp"], 1)
                if not isinstance(j, int) or j + 2 < NBLK:
                    select(j + 2, b)

            v.wait_ge(S["expert_r"], 1)
            select(0, 0)
            select(1, 1)
            in_T(0, 0)
            in_T(1, 1)
            run_blocks(v, expert_block)

        @block.scalar
        def _(act):
            act.dma_start(bk[:], col(a["L0_xattn_bk"]), allow_slow_non_contiguous=True).then_inc(S["wk_ld"], 16)
            act.dma_start(br[:], col(a["L0_xattn_br"]), allow_slow_non_contiguous=True).then_inc(S["wk_ld"], 16)
            act.dma_start(X[:, 0:2, :], x_v[:, 0:2, :]).then_inc(S["x_ld"], 16)
            act.dma_start(Wqk[0:H, :], a["L0_attn_W_q"]).then_inc(S["wqk_ld"], 16)
            act.dma_start(Wqk[H:2 * H, :], a["L0_attn_W_k"]).then_inc(S["wqk_ld"], 16)
            act.dma_start(logs[:, 0:1], a["L0_attn_log_mix"].partition_broadcast(P)).then_inc(S["logs_ld"], 16)
            act.dma_start(logs[:, 1:2], a["L0_attn_log_scale"].partition_broadcast(P)).then_inc(S["logs_ld"], 16)
            act.dma_start(bq[:], col(a["L0_xattn_bq"]), allow_slow_non_contiguous=True).then_inc(S["w_ld"], 16)
            act.dma_start(Wq[:], rows(a["L0_xattn_Wq"])).then_inc(S["w_ld"], 16)
            act.dma_start(bv[:], a["L0_xattn_bv"].partition_broadcast(P)).then_inc(S["w_ld"], 16)
            act.dma_start(gain, a["L0_attn_gain"].partition_broadcast(P)).then_inc(S["w_ld"], 16)
            act.dma_start(gbias[:], a["L0_attn_bias"].partition_broadcast(P)).then_inc(S["w_ld"], 16)
            act.dma_start(Wv[:], rows(a["L0_xattn_Wv"])).then_inc(S["w_ld"], 16)
            act.dma_start(Wroute[:], rows(a["L0_ffn_Wr"])).then_inc(S["w_ld"], 16)

            act.wait_ge(S["logs_ld"], 2 * 16)
            act.activation(sc[:, 0:1], logs[:, 0:1], ACT.Exp, scale=-1.0).then_inc(S["scal_act"], 1)
            act.activation(sc[:, 5:6], logs[:, 1:2], ACT.Abs).then_inc(S["scal_act"], 1)
            act.wait_ge(S["scal_act"], 2)
            act.activation(sc[:, 6:7], sc[:, 5:6], ACT.Exp, scale=-1.0).then_inc(S["scal_act"], 1)
            act.wait_ge(S["scal_act"], 3)
            act.activation(sc[:, 7:8], sc[:, 6:7], ACT.Ln, bias=1.0).then_inc(S["scal_act"], 1)
            act.wait_ge(S["last_fr"], 1)
            act.activation(khat_last[:], last_frac, ACT.Sin, scale=TWO_PI).then_inc(S["khat_last_r"], 1)

            def ctx_T_copy(g, half):
                act.wait_ge(S["ctxT_tr"], 4 * g + 2 * half + 2)
                at_least(act, S["kproj"], 4 * g + 2 * half - 2)
                act.copy(ctx_T[:, 1, half * 512:(half + 1) * 512], pT[1][:]).then_inc(S["ctxT1_cp"], 1)

            def turn(g, u):
                r = u % 2
                act.wait_ge(S["kproj"], 4 * g + u + 1)
                at_least(act, S["frac_r"], 4 * g + u - 1)
                act.activation(turns[r], pK[r][:], ACT.Identity, bias=bkr[:, r:r + 1]).then_inc(S["turns_r"], 1)

            def sine(g, b, u):
                half, r = u // 2, u % 2
                act.wait_ge(S["frac_r"], 4 * g + u + 1)
                at_least(act, S["scoresA"], g - 1)
                act.activation(khat[b][:, r, 2 * half:2 * half + 2, 0:CF], frac[r].rearrange("p (j n) -> p j n", j=2),
                               ACT.Sin, scale=TWO_PI).then_inc(S["khat_r"], 1)

            act.wait_ge(S["bkr_cp"], 1)

            def step(k, parity):
                now, one, two, three, four = (groups(k, parity, n) for n in (0, 1, 2, 3, 4))
                if now:
                    ctx_T_copy(now[0], 0)
                if three:
                    g, b, _ = three
                    act.wait_ge(S["nmaxB_r"], g + 1)
                    at_least(act, S["att_r"], g)
                    act.activation(expB[:], scoreB[:, b, :], ACT.Exp, bias=nmaxB[:, b:b + 1], accum_out=sumB[:]
                                   ).then_inc(S["probsB"], 1)
                if one:
                    g, b, _ = one
                    act.wait_ge(S["nmaxA_r"], g + 1)
                    at_least(act, S["pT_tr"], g)
                    at_least(act, S["last_r"], g)
                    at_least(act, S["rsumA_r"], g)
                    act.activation(probs[:], p_score, ACT.Exp, bias=nmaxA[:, 0:1], accum_out=sumA[:]
                                   ).then_inc(S["probsA"], 1)
                def gelu_y():
                    g, b, _ = four
                    act.wait_ge(S["y_r"], g + 1)
                    at_least(act, S["x2_r"], g)
                    act.activation(gel[:], y[:], ACT.Gelu).then_inc(S["gelu_r"], 1)

                if four and now:
                    gelu_y()
                if two:
                    g, b, _ = two
                    act.wait_ge(S["hT_tr"], g + 1)
                    at_least(act, S["qk_mm"], g)
                    act.copy(hT[:].rearrange("p c n -> p (c n)"), p_hT).then_inc(S["hT_cp"], 1)
                if four and not now:
                    gelu_y()
                if now:
                    turn(now[0], 0)
                    turn(now[0], 1)
                if two:
                    g, b, _ = two
                    act.wait_ge(S["qk_mm"], g + 1)
                    at_least(act, S["scoreB_mm"], g)
                    act.mul(qB[:], p_qk[0:H, :], float(H ** -0.5)).then_inc(S["qk_cp"], 1)
                    act.copy(kB[:], p_qk[H:2 * H, :]).then_inc(S["qk_cp"], 1)
                if now:
                    g, b, _ = now
                    sine(g, b, 0)
                    ctx_T_copy(g, 1)
                    sine(g, b, 1)
                    if isinstance(g, int) and g == 0:
                        act.wait_ge(S["w_ld"], 16 * W_LOADS)
                    act.wait_ge(S["qproj"], g + 1)
                    at_least(act, S["scoresA"], g)
                    for c in range(DC):
                        act.activation(qT[:, c, :], p_q[:, c * P:(c + 1) * P], ACT.Identity, bias=bq[:, c:c + 1]
                                       ).then_inc(S["q_r"], 1)
                    turn(g, 2)
                    turn(g, 3)
                if four:
                    g, b, _ = four
                    act.wait_ge(S["xn3T_tr"], g + 1)
                    at_least(act, S["route_mm"], g)
                    act.copy(xn3T[:].rearrange("p c n -> p (c n)"), p_xn3T).then_inc(S["xn3T_cp"], 1)
                if now:
                    g, b, _ = now
                    sine(g, b, 2)
                    sine(g, b, 3)

            run_steps(act, step)

            act.wait_ge(S["route"], made_at["route_sub"])
            act.activation(rt[1], rt[0], ACT.Exp).then_inc(S["route_exp"], 1)

            def gelus(j):
                at_least(act, S["f_hT_tr"], 2 * j)
                for i in range(2):
                    act.wait_ge(S["f_h_mm"], 2 * j + i + 1)
                    act.activation(f_h[:, i * 512:(i + 1) * 512], pK[i][:], ACT.Gelu).then_inc(S["f_gelu"], 1)

            def expert_block(j, b, k):
                act.wait_ge(S["f_hT_tr"], 2 * j + 2)
                at_least(act, S["f_y_mm"], j)
                act.copy(f_hT[:, 512:1024], pT[1][:]).then_inc(S["f_hT1_cp"], 1)
                if not isinstance(j, int) or j + 1 < NBLK:
                    gelus(j + 1)

            gelus(0)
            run_blocks(act, expert_block)

        @block.tensor
        def _(pe):
            def transposed(dst, src, done=None):
                k = src.shape[0]
                ins = pe.transpose(dst, src, ident[0:k, 0:k])
                if done:
                    ins.then_inc(S[done], 1)

            pe.wait_ge(S["consts"], made_at["ident"])
            pe.wait_ge(S["wk_ld"], 64)
            for ec in range(DC):
                for dc in range(DC):
                    transposed(pT[0][:, (ec * DC + dc) * P:(ec * DC + dc + 1) * P], Wk[:, dc, ec * P:(ec + 1) * P],
                               "wkT_tr" if (ec, dc) == (DC - 1, DC - 1) else None)
            pe.wait_ge(S["wkT_cp"], 1)
            for dc in range(DC):
                for ec in range(DC):
                    mm = pe.matmul(pK[0][:, dc * D:(dc + 1) * D], WkT[:, ec, dc * P:(dc + 1) * P], Wr[:, ec, :],
                                   start=ec == 0, stop=ec == DC - 1)
            mm.then_inc(S["wkr_mm"], 1)
            for r in range(DC):
                for ec in range(DC):
                    mm = pe.matmul(b4[:, r:r + 1], Wr[:, ec, r * P:(r + 1) * P], bk[:, ec:ec + 1],
                                   start=ec == 0, stop=ec == DC - 1)
            mm.then_inc(S["bkr_mm"], 1)
            pe.wait_ge(S["wqk_ld"], 32)
            for c in range(DC):
                transposed(b5[:, c * 2 * H:(c + 1) * 2 * H], Wqk[:, c * P:(c + 1) * P],
                           "wqkT_tr" if c == DC - 1 else None)
            pe.wait_ge(S["last_ld"], 16)
            for c in range(DC):
                transposed(b7[:, c * B:(c + 1) * B], last_rows[:, c * P:(c + 1) * P],
                           "lastT_tr" if c == DC - 1 else None)
            pe.wait_ge(S["wkr_cp"], 1)
            pe.wait_ge(S["lastT_cp"], 1)
            for r in range(DC):
                for c in range(DC):
                    mm = pe.matmul(b6[:, r * B:(r + 1) * B], Wkr[:, c, r * P:(r + 1) * P], last_T[:, c, :],
                                   start=c == 0, stop=c == DC - 1)
            mm.then_inc(S["lastK_mm"], 1)
            pe.wait_ge(S["bkr_cp"], 1)
            pe.wait_ge(S["wqkT_cp"], 1)
            pe.wait_ge(S["last_turn"], 2)

            def ctx_transposes(g, b, q, half):
                pe.wait_ge(ctx_ld[b], 16 * CTX_LOADS * (q + 1))
                for c in range(DC):
                    at_least(pe, S["ctxT0_cp" if c == 0 else "ctxT1_cp"], 2 * g + half)
                    for i in range(4):
                        src = ctx_rows[b][:, 2 * half + i // 2, i % 2, c * P:(c + 1) * P]
                        transposed(pT[c][:, i * P:(i + 1) * P], src, "ctxT_tr" if i == 3 else None)

            def ctx_project(g, half, r):
                pe.wait_ge(S["ctxT0_cp"], 2 * g + half + 1)
                pe.wait_ge(S["ctxT1_cp"], 2 * g + half + 1)
                at_least(pe, S["turns_r"], 4 * g + 2 * half + r - 1)
                for c in range(DC):
                    mm = pe.matmul(pK[r][:], Wkr[:, c, r * P:(r + 1) * P],
                                   ctx_T[:, c, half * 512:(half + 1) * 512], start=c == 0, stop=c == DC - 1)
                mm.then_inc(S["kproj"], 1)

            def step(k, parity):
                now, one, two, three, four = (groups(k, parity, n) for n in (0, 1, 2, 3, 4))
                if now:
                    g, b, q = now
                    ctx_transposes(g, b, q, 0)
                    pe.wait_ge(S["xn_r"], g + 1)
                    at_least(pe, S["selected"], g - 2)
                    at_least(pe, S["ymsg_r"], g - 3)
                    for c in range(DC):
                        transposed(p_xnT[:, c * P:(c + 1) * P], xn[:, b, c * P:(c + 1) * P],
                                   "xnT_tr" if c == DC - 1 else None)
                if one:
                    g, b, _ = one
                    pe.wait_ge(S["khat_r"], 4 * g + 4)
                    pe.wait_ge(S["klast_r"], g + 1)
                    pe.wait_ge(S["q_r"], 2 * g + 2)
                    at_least(pe, S["oT_cp"], g)
                    at_least(pe, S["attT_cp"], g - 2)
                    for r in range(DC):
                        for j in range(BG):
                            mm = pe.matmul(p_score[j * T:(j + 1) * T, :], qT[:, r, j * T:(j + 1) * T],
                                           khat[b][:, r, j, :], start=r == 0, stop=r == DC - 1,
                                           skip_group_check=True)
                    mm.then_inc(S["scoresA"], 1)
                if now:
                    ctx_project(now[0], 0, 0)
                if two:
                    g, b, _ = two
                    pe.wait_ge(S["h_r"], g + 1)
                    pe.wait_ge(S["x1_r"], g + 1)
                    for c in range(DC):
                        transposed(p_hT[:, c * P:(c + 1) * P], h[:, b, c * P:(c + 1) * P],
                                   "hT_tr" if c == DC - 1 else None)
                if now:
                    ctx_project(now[0], 0, 1)
                if one:
                    g, b, _ = one
                    pe.wait_ge(S["probsA"], g + 1)
                    for c in range(CC):
                        transposed(p_pT[:, c * P:(c + 1) * P], probs[:, c * P:(c + 1) * P],
                                   "pT_tr" if c == CC - 1 else None)
                if two:
                    g, b, _ = two
                    pe.wait_ge(S["hT_cp"], g + 1)
                    at_least(pe, S["xnT_cp"], upto(g + 3, NG))
                    at_least(pe, S["ymsg_r"], g - 1)
                    for c in range(DC):
                        mm = pe.matmul(p_sim, hT[:, c, :], hT[:, c, :], start=c == 0, stop=c == DC - 1)
                    mm.then_inc(S["sim_mm"], 1)
                    for c in range(DC):
                        mm = pe.matmul(p_qk, WqkT[:, c, :], hT[:, c, :], start=c == 0, stop=c == DC - 1)
                    mm.then_inc(S["qk_mm"], 1)
                if now:
                    g, b, q = now
                    ctx_transposes(g, b, q, 1)
                if one:
                    g, b, _ = one
                    pe.wait_ge(S["pT_cp"], g + 1)
                    at_least(pe, S["o_r"], g)
                    at_least(pe, S["logits_r"], g - 3)
                    for c in range(CC):
                        for j in range(BG):
                            mm = pe.matmul(p_o[j * T:(j + 1) * T, :], probsT[:, c, j * T:(j + 1) * T],
                                           ctx_rows[b][:, j, c, :], start=c == 0, stop=c == CC - 1,
                                           skip_group_check=True)
                    mm.then_inc(S["pv"], 1)
                if three:
                    g, b, _ = three
                    pe.wait_ge(S["att_r"], g + 1)
                    at_least(pe, S["pT_cp"], upto(g + 3, NG))
                    at_least(pe, S["oT_cp"], upto(g + 2, NG))
                    transposed(p_attT, att[:], "attT_tr")
                if two:
                    g, b, _ = two
                    pe.wait_ge(S["qk_cp"], 2 * g + 2)
                    pe.wait_ge(S["simm_r"], g + 1)
                    pe.matmul(p_scoreB, qB[:], kB[:], start=True, stop=True).then_inc(S["scoreB_mm"], 1)
                if now:
                    g, b, _ = now
                    if isinstance(g, int) and g == 0:
                        pe.wait_ge(S["w_ld"], 16 * W_LOADS)
                    pe.wait_ge(S["xnT_cp"], g + 1)
                    at_least(pe, S["qk_cp"], 2 * g - 2)
                    at_least(pe, S["x1_r"], g - 1)
                    for r in range(DC):
                        for c in range(DC):
                            mm = pe.matmul(p_q[:, r * P:(r + 1) * P], Wq[:, c, r * P:(r + 1) * P], xnT[:, c, :],
                                           start=c == 0, stop=c == DC - 1)
                    mm.then_inc(S["qproj"], 1)
                    ctx_project(g, 1, 0)
                if one:
                    g, b, _ = one
                    pe.wait_ge(S["o_r"], g + 1)
                    at_least(pe, S["attT_cp"], g - 1)
                    for c in range(DC):
                        transposed(p_oT[:, c * P:(c + 1) * P], o_norm[:, c * P:(c + 1) * P],
                                   "oT_tr" if c == DC - 1 else None)
                if now:
                    ctx_project(now[0], 1, 1)
                if four:
                    g, b, _ = four
                    pe.wait_ge(S["xn3_r"], g + 1)
                    at_least(pe, S["o_r"], upto(g + 4, NG))
                    at_least(pe, S["logits_r"], g)
                    for c in range(DC):
                        transposed(p_xn3T[:, c * P:(c + 1) * P], xn3[:, b, c * P:(c + 1) * P],
                                   "xn3T_tr" if c == DC - 1 else None)
                if three:
                    g, b, _ = three
                    pe.wait_ge(S["attT_cp"], g + 1)
                    at_least(pe, S["selected"], upto(g + 2, NG))
                    pe.matmul(p_msg, attT[:], h[:, b, :], start=True, stop=True).then_inc(S["msg_mm"], 1)
                if one:
                    g, b, _ = one
                    pe.wait_ge(S["oT_cp"], g + 1)
                    at_least(pe, S["q_r"], upto(2 * g + 4, 2 * NG))
                    at_least(pe, S["qk_cp"], 2 * g)
                    for c in range(DC):
                        mm = pe.matmul(p_a, o_T[:, c, :], Wv[:, c, :], start=c == 0, stop=c == DC - 1)
                    mm.then_inc(S["aproj"], 1)
                if four:
                    g, b, _ = four
                    pe.wait_ge(S["xn3T_cp"], g + 1)
                    for c in range(DC):
                        mm = pe.matmul(p_route, xn3T[:, c, :], Wroute[:, c, :], start=c == 0, stop=c == DC - 1)
                    mm.then_inc(S["route_mm"], 1)

            run_steps(pe, step)

            pe.wait_ge(S["route"], made_at["onehot"])
            pe.matmul(b6[:, 0:NG * E], tri[:], onehot[:].rearrange("p g e -> p (g e)"), start=True, stop=False,
                      skip_group_check=True)
            for g in range(NG - 1):
                later = NG - 1 - g
                pe.matmul(b6[:, (g + 1) * E:NG * E], ones[:],
                          onehot[:, g:g + 1, :].to_broadcast([P, later, E]), start=False, stop=g == NG - 2,
                          skip_group_check=True)
            pe.matmul(b7[:, 0:E], ones[:], cnt[:], start=True, stop=True).then_inc(S["rank_mm"], 1)

            for g in range(NG):
                if g % (NG // 2) == 0:
                    pe.wait_ge(S["in_lane_r"], 1 + g // (NG // 2))
                    pe.wait_ge(S["in_values_r"], (VALUES - 1) * (1 + g // (NG // 2)))
                mm = pe.matmul(b6[:, 0:VALUES * NBLK], in_lane[:, g, :],
                               in_blk[:, g].rearrange("p v n -> p (v n)"), start=g == 0, stop=g == NG - 1)
            mm.then_inc(S["slot_mm"], 1)

            def in_T(j, b, k):
                pe.wait_ge(f_in_ld[b], 16 * (k + 1))
                if isinstance(j, int) and j == 0:
                    pe.wait_ge(S["expert_r"], 1)
                at_least(pe, S["f_inT_cp"], j - 1)
                for c in range(DC):
                    transposed(p_in[b][:, c * P:(c + 1) * P], f_in[:, b, c * P:(c + 1) * P],
                               "f_inT_tr" if c == DC - 1 else None)

            def expert_of(j):
                return pe.value_load(expert_i[0:1, bass.ds(j, 1)], min_val=0, max_val=E - 1)

            def up(j, b, e):
                pe.wait_ge(S["f_inT_cp"], j + 1)
                pe.wait_ge(S["f_sel_r"], j + 1)
                for i in range(2):
                    at_least(pe, S["f_gelu"], 2 * (j - 1) + i + 1)
                    pe.matmul(pK[i][:], f_sel[:, b, :], b_parts[:, i * 512:(i + 1) * 512], start=True, stop=False)
                    for c in range(DC):
                        mm = pe.matmul(pK[i][:], f_inT[:, b, c * P:(c + 1) * P],
                                       W1[:, bass.ds(e, 1), c, i * 512:(i + 1) * 512].rearrange("p o n -> p (o n)"),
                                       start=False, stop=c == DC - 1)
                    mm.then_inc(S["f_h_mm"], 1)

            def expert_block(j, b, k):
                more = not isinstance(j, int)
                e = expert_of(j)
                if more or j + 1 < NBLK:
                    e_next = expert_of(j + 1)
                for i in range(2):
                    pe.wait_ge(S["f_gelu"], 2 * j + i + 1)
                    at_least(pe, S[f"f_hT{i}_cp"], j)
                    for c in range(4):
                        n = 4 * i + c
                        transposed(pT[i][:, c * P:(c + 1) * P], f_h[:, n * P:(n + 1) * P],
                                   "f_hT_tr" if c == 3 else None)
                if more or j + 2 < NBLK:
                    in_T(j + 2, b, k + 1)
                if more or j + 1 < NBLK:
                    up(j + 1, 1 - b, e_next)
                pe.wait_ge(S["f_hT0_cp"], j + 1)
                pe.wait_ge(S["f_hT1_cp"], j + 1)
                if not more and j == 0:
                    pe.wait_ge(S["w2_ld"], 16 * E)
                at_least(pe, S["f_y_cp"], j)
                acc = p_out[b]
                pe.matmul(acc, f_sel[:, b, :], b_parts[:, F:F + D], start=True, stop=False)
                for c in range(FC):
                    mm = pe.matmul(acc, f_hT[:, c * P:(c + 1) * P],
                                   w2[:, bass.ds(e, 1), c, :].rearrange("p o n -> p (o n)"),
                                   start=False, stop=c == FC - 1)
                mm.then_inc(S["f_y_mm"], 1)

            in_T(0, 0, 0)
            in_T(1, 1, 0)
            pe.wait_ge(S["w1_ld"], 16 * E)
            pe.wait_ge(S["bias_split"], 6)
            up(0, 0, expert_of(0))
            run_blocks(pe, expert_block)


_INS = ["x", "ctx_1024", "L0_xattn_Wq", "L0_xattn_bq", "L0_xattn_Wk", "L0_xattn_bk", "L0_xattn_Wv", "L0_xattn_bv",
        "L0_xattn_Wr", "L0_xattn_br", "L0_attn_W_q", "L0_attn_W_k", "L0_attn_gain", "L0_attn_bias",
        "L0_attn_log_mix", "L0_attn_log_scale", "L0_ffn_Wr", "L0_ffn_W1", "L0_ffn_b1", "L0_ffn_W2", "L0_ffn_b2"]


def kernel(**inputs):
    import numpy as _np
    import concourse.bacc as _bacc
    from concourse import mybir as _mybir
    from concourse.bass_utils import run_bass_kernel_spmd as _run

    nc = _bacc.Bacc("TRN2", target_bir_lowering=False, num_devices=1)
    arrays, args = {}, {}
    for name in _INS:
        v = _np.ascontiguousarray(inputs[name])
        if not v.shape:
            v = v.reshape(1)
        arrays[f"in_{name}_dram"] = v
        args[name] = nc.dram_tensor(f"in_{name}_dram", v.shape, _mybir.dt.from_np(v.dtype), kind="ExternalInput").ap()
    o = nc.dram_tensor("out_0_dram", (B, T, D), F32, kind="ExternalOutput").ap()
    perceiver_layer(nc, args, o)
    r = _run(nc, [arrays], core_ids=[0])
    return r.results[0]["out_0_dram"]
```
